# Optimizing a Trainium2 kernel written in Bass

```python
import numpy as np
import jax
import jax.numpy as jnp

def _softmax(x, axis=-1):
    return jax.nn.softmax(x, axis=axis)

def _gelu(x):
    return jax.nn.gelu(x, approximate=True)

def _silu(x):
    return jax.nn.silu(x)

def _sigmoid(x):
    return jax.nn.sigmoid(x)

def _layernorm(x, axis=-1, eps=1e-05):
    m = jnp.mean(x, axis=axis, keepdims=True)
    v = jnp.var(x, axis=axis, keepdims=True)
    return (x - m) / jnp.sqrt(v + eps)

def _scatter_add(tgt, idx, src, axis=0):
    return tgt.at[idx].add(src)

def _segment_sum(src, seg, n):
    return jax.ops.segment_sum(src, seg, n)
kernel_name = 'mk_gps_d1_gnn_r8_7d5517'

def setup_inputs(seed: int=0):
    np.random.seed(seed)
    _w = jnp.asarray

    def _rec_inputs():
        import jax
        import jax.numpy as jnp
        _gk = jax.random.key(seed)
        x = -8.776e-05 + 1 * jax.random.normal(jax.random.fold_in(_gk, 1), (1250, 512), jnp.float32)
        src = jax.random.randint(jax.random.fold_in(_gk, 2), (20000,), 0, 1250, jnp.int32)
        dst = jax.random.randint(jax.random.fold_in(_gk, 3), (20000,), 0, 1250, jnp.int32)
        _o = jnp.argsort(dst, stable=True)
        src = src[_o]
        dst = dst[_o]
        return (x, src, dst)
    x, src, dst = _rec_inputs()

    def _L0_gnn_setup():
        import jax, jax.numpy as jnp
        import numpy as np
        N_NODES = 1250
        N_EDGES = 20000
        D = 512
        key = jax.random.key(seed)
        k_h, k_e, k_w1, k_w2 = jax.random.split(key, 4)
        h = jax.random.normal(k_h, (N_NODES, D), dtype=jnp.float32)
        edge_index = jax.random.randint(k_e, (2, N_EDGES), 0, N_NODES, dtype=jnp.int64)
        scale = 1.0 / np.sqrt(D)
        W1 = jax.random.normal(k_w1, (D, D), dtype=jnp.float32) * scale
        b1 = jnp.zeros((D,), dtype=jnp.float32)
        W2 = jax.random.normal(k_w2, (D, D), dtype=jnp.float32) * scale
        b2 = jnp.zeros((D,), dtype=jnp.float32)
        return {'h': h, 'edge_index': edge_index, 'W1': W1, 'b1': b1, 'W2': W2, 'b2': b2}
    _L0_gnn_all = _L0_gnn_setup()
    _L0_gnn_in = {k: v for k, v in _L0_gnn_all.items() if k in ('W1', 'b1', 'W2', 'b2')}
    del _L0_gnn_all

    def _L0_mix_setup():
        import jax, jax.numpy as jnp
        import numpy as np
        NUM_HEADS = 8

        def _reference_tuple_inner(x, Wq, bq, Wk, bk, Wv, bv):
            R, C, E = x.shape
            H = NUM_HEADS
            D = E // H
            q = (x @ Wq.T + bq).reshape(R, C, H, D).transpose(0, 2, 1, 3)
            k = (x @ Wk.T + bk).reshape(R, C, H, D).transpose(0, 2, 1, 3)
            v = (x @ Wv.T + bv).reshape(R, C, H, D).transpose(0, 2, 1, 3)
            q = q.mean(axis=0)
            k = k.mean(axis=0)
            q = jax.nn.softmax(q, axis=-1) * D ** (-0.5)
            k = jax.nn.softmax(k, axis=-2)
            attn_weights = jnp.einsum('hnd,hmd->hnm', q, k)
            context = jnp.einsum('hnd,bhne->bhde', k, v)
            out = jnp.einsum('hnd,bhde->bhne', q, context)
            out = out.transpose(0, 2, 1, 3).reshape(R, C, E)
            return (out, attn_weights)
        key = jax.random.key(seed)
        ks = jax.random.split(key, 7)
        R, C, E = (64, 256, 512)
        x = jax.random.normal(ks[0], (R, C, E), dtype=jnp.float32)
        s = 0.02
        Wq = jax.random.normal(ks[1], (E, E), dtype=jnp.float32) * s
        bq = jax.random.normal(ks[2], (E,), dtype=jnp.float32) * s
        Wk = jax.random.normal(ks[3], (E, E), dtype=jnp.float32) * s
        bk = jax.random.normal(ks[4], (E,), dtype=jnp.float32) * s
        Wv = jax.random.normal(ks[5], (E, E), dtype=jnp.float32) * s
        bv = jax.random.normal(ks[6], (E,), dtype=jnp.float32) * s
        return {'x': x, 'Wq': Wq, 'bq': bq, 'Wk': Wk, 'bk': bk, 'Wv': Wv, 'bv': bv}
    _L0_mix_all = _L0_mix_setup()
    _L0_mix_in = {k: v for k, v in _L0_mix_all.items() if k in ('Wq', 'bq', 'Wk', 'bk', 'Wv', 'bv')}
    del _L0_mix_all

    def _L0_ffn_setup():
        import jax, jax.numpy as jnp
        import numpy as np
        B, S, D, H, E = (4, 1024, 512, 256, 8)
        key = jax.random.key(seed)
        ks = jax.random.split(key, 7)
        scale = 1.0 / np.sqrt(D)
        return {'x': jax.random.normal(ks[0], (B, S, D), dtype=jnp.float32), 'Wg': jax.random.normal(ks[1], (D, E), dtype=jnp.float32) * scale, 'bg': jnp.zeros((E,), dtype=jnp.float32), 'W1': jax.random.normal(ks[2], (E, D, H), dtype=jnp.float32) * scale, 'b1': jnp.zeros((E, H), dtype=jnp.float32), 'W2': jax.random.normal(ks[3], (E, H, D), dtype=jnp.float32) * (1.0 / np.sqrt(H)), 'b2': jnp.zeros((E, D), dtype=jnp.float32)}
    _L0_ffn_all = _L0_ffn_setup()
    _L0_ffn_in = {k: v for k, v in _L0_ffn_all.items() if k in ('Wg', 'bg', 'W1', 'b1', 'W2', 'b2')}
    del _L0_ffn_all
    return {'x': x, 'src': src, 'dst': dst, 'L0_gnn_W1': _L0_gnn_in['W1'], 'L0_gnn_b1': _L0_gnn_in['b1'], 'L0_gnn_W2': _L0_gnn_in['W2'], 'L0_gnn_b2': _L0_gnn_in['b2'], 'L0_mix_Wq': _L0_mix_in['Wq'], 'L0_mix_bq': _L0_mix_in['bq'], 'L0_mix_Wk': _L0_mix_in['Wk'], 'L0_mix_bk': _L0_mix_in['bk'], 'L0_mix_Wv': _L0_mix_in['Wv'], 'L0_mix_bv': _L0_mix_in['bv'], 'L0_ffn_Wg': _L0_ffn_in['Wg'], 'L0_ffn_bg': _L0_ffn_in['bg'], 'L0_ffn_W1': _L0_ffn_in['W1'], 'L0_ffn_b1': _L0_ffn_in['b1'], 'L0_ffn_W2': _L0_ffn_in['W2'], 'L0_ffn_b2': _L0_ffn_in['b2']}

def reference(x, src, dst, L0_gnn_W1, L0_gnn_b1, L0_gnn_W2, L0_gnn_b2, L0_mix_Wq, L0_mix_bq, L0_mix_Wk, L0_mix_bk, L0_mix_Wv, L0_mix_bv, L0_ffn_Wg, L0_ffn_bg, L0_ffn_W1, L0_ffn_b1, L0_ffn_W2, L0_ffn_b2):
    import jax
    import jax.numpy as jnp

    def _L0_gnn_ref(h, edge_index, W1, b1, W2, b2):
        import jax, jax.numpy as jnp
        import numpy as np
        N_NODES = 1250
        N_EDGES = 20000
        D = 512
        send, rec = (edge_index[0], edge_index[1])
        agg = jax.ops.segment_sum(h[send], rec, num_segments=h.shape[0])
        x = h + agg
        x = jax.nn.relu(x @ W1 + b1)
        x = x @ W2 + b2
        return x

    def _L0_mix_ref(x, Wq, bq, Wk, bk, Wv, bv):
        import jax, jax.numpy as jnp
        import numpy as np
        NUM_HEADS = 8

        def _reference_tuple_inner(x, Wq, bq, Wk, bk, Wv, bv):
            R, C, E = x.shape
            H = NUM_HEADS
            D = E // H
            q = (x @ Wq.T + bq).reshape(R, C, H, D).transpose(0, 2, 1, 3)
            k = (x @ Wk.T + bk).reshape(R, C, H, D).transpose(0, 2, 1, 3)
            v = (x @ Wv.T + bv).reshape(R, C, H, D).transpose(0, 2, 1, 3)
            q = q.mean(axis=0)
            k = k.mean(axis=0)
            q = jax.nn.softmax(q, axis=-1) * D ** (-0.5)
            k = jax.nn.softmax(k, axis=-2)
            attn_weights = jnp.einsum('hnd,hmd->hnm', q, k)
            context = jnp.einsum('hnd,bhne->bhde', k, v)
            out = jnp.einsum('hnd,bhde->bhne', q, context)
            out = out.transpose(0, 2, 1, 3).reshape(R, C, E)
            return (out, attn_weights)
        return _reference_tuple_inner(x, Wq, bq, Wk, bk, Wv, bv)[0]

    def _L0_ffn_ref(x, Wg, bg, W1, b1, W2, b2):
        import jax, jax.numpy as jnp
        import numpy as np
        B, S, D, H, E = (4, 1024, 512, 256, 8)
        b, s, d = x.shape
        xf = x.reshape(-1, d)
        logits = xf @ Wg + bg
        scores = jax.nn.softmax(logits, axis=-1)
        top_s, top_i = jax.lax.top_k(scores, 1)
        idx = top_i[:, 0]
        sc = top_s[:, 0]
        n_experts = Wg.shape[1]
        out = jnp.zeros_like(xf)
        for e in range(n_experts):
            h = jax.nn.relu(xf @ W1[e] + b1[e]) @ W2[e] + b2[e]
            out = jnp.where((idx == e)[:, None], h, out)
        out = out * sc[:, None]
        return out.reshape(b, s, d)
    edge_index = jnp.stack([src, dst])
    xn = _layernorm(x, axis=-1)
    x = x + _L0_gnn_ref(xn, edge_index, L0_gnn_W1, L0_gnn_b1, L0_gnn_W2, L0_gnn_b2) + _L0_mix_ref(xn[None], L0_mix_Wq, L0_mix_bq, L0_mix_Wk, L0_mix_bk, L0_mix_Wv, L0_mix_bv)[0]
    x = x + _L0_ffn_ref(_layernorm(x, axis=-1)[None], L0_ffn_Wg, L0_ffn_bg, L0_ffn_W1, L0_ffn_b1, L0_ffn_W2, L0_ffn_b2)[0]
    return x

_drawn_inputs = setup_inputs


def setup_inputs(seed=0):
    import zlib

    import numpy as np

    out = dict(_drawn_inputs(seed))
    spreads = {'L0_gnn_b1': (0.0, 0.306),
     'L0_gnn_b2': (0.0, 0.1),
     'L0_ffn_bg': (0.0, 0.36),
     'L0_ffn_b1': (0.0, 0.8),
     'L0_ffn_b2': (0.0, 0.624)}
    factors = {'L0_mix_Wq': 8.0,
     'L0_mix_bq': 64.0,
     'L0_mix_Wk': 8.0,
     'L0_mix_bk': 64.0,
     'L0_mix_Wv': 8.0,
     'L0_mix_bv': 50.636}
    for name, (base, spread) in spreads.items():
        noise = np.random.default_rng([zlib.crc32(name.encode()), seed]).standard_normal(out[name].shape)
        drawn = base * np.exp(spread * noise) if base else spread * noise
        out[name] = jnp.asarray(drawn.astype(out[name].dtype))
    for name, factor in factors.items():
        out[name] = (out[name] * factor).astype(out[name].dtype)
    return out
```

```python
from contextlib import ExitStack

import numpy as np

import concourse.bass as bass
from concourse import mybir

ALU = mybir.AluOpType
ACT = mybir.ActivationFunctionType
AX = mybir.AxisListType
F32 = mybir.dt.float32
F16 = mybir.dt.float16
I32 = mybir.dt.int32

P = 128
N, D = 1250, 512
T = -(-N // P)
NPAD = T * P
LAST = N - (T - 1) * P
K4 = D // P
HEADS, DH = 8, 64
CH = ((0, 420), (420, 420), (840, 410))
NCH = len(CH)

EDGES = 20000
EC = -(-EDGES // P)
ECP = 256
ECF = 160
WN = 24
KEYS = WN * T
WINDOWS = 54
WCH = 5
PAIRS = WINDOWS * WCH
GATHERS = 3
PG = PAIRS // GATHERS
ATW = WINDOWS * WN
PAD_DST = ATW
WPAIRS = WINDOWS // 2
AK, AQ = 4, 2

NE, HID = 8, 256
ET = (N + NE * (P - 1)) // P
SLOTS = ET * P
ROW = D + 4
NO_TOKEN = 1 << 20

WS = 64.0
HS = 0.125
KS = 4096.0
EPS = 1e-5

C_ID, C_THR = 0, P
C_K = C_THR + PAIRS
C_WK = C_K + GATHERS
C_C = C_WK + GATHERS
C_J = C_C + 2
C_TRI = C_J + NE
C_TILE = C_TRI + NE * NE
C_TOK = C_TILE + ET * NE
C_ALL = C_TOK + T
H_IOTA, H_TRI, H_ONE = 0, KEYS, KEYS + P
H_ALL = KEYS + 2 * P
R_BQ, R_BV, R_B2, R_BG = 0, D, 2 * D, 3 * D
R_ALL = 3 * D + NE
B_K, B_G1, B_F1 = 0, K4, 2 * K4
B_ALL = 2 * K4 + 2 * NE


def constants():
    f = np.zeros((P, C_ALL), np.float32)
    p = np.arange(P)
    f[:, C_ID:C_ID + P] = np.eye(P)
    pair = np.arange(PAIRS)
    f[:, C_THR:C_THR + PAIRS] = (pair // WCH) * WN
    for g in range(GATHERS):
        q = g * PG + np.minimum(p, PG - 1)
        f[:, C_K + g] = q % WCH
        f[:, C_WK + g] = (q // WCH) * KEYS
    for g in range(2):
        f[:, C_C + g] = g * P + p
    f[:, C_J:C_J + NE] = NE - np.arange(NE)
    f[:, C_TRI:C_TRI + NE * NE] = (np.arange(NE)[None, :] < np.arange(NE)[:, None]).reshape(-1)
    f[:, C_TILE:C_TILE + ET * NE] = np.repeat(np.arange(ET), NE)
    f[:, C_TOK:C_TOK + T] = np.arange(T)[None, :] * P + p[:, None]
    h = np.zeros((P, H_ALL), np.float16)
    h[:, H_IOTA:H_IOTA + KEYS] = np.arange(KEYS)
    h[:, H_TRI:H_TRI + P] = p[:, None] < p[None, :]
    h[:, H_ONE:H_ONE + P] = 1
    return f, h


def build(nc, x, edges, edge_cols, wk, wq, wv, g1, g2, w1, w2, wg, rows, b2f, cols, cf, ch, out):
    ctx = ExitStack()
    with ctx:
        def sb(name, shape, dt=F32):
            return ctx.enter_context(nc.sbuf_tensor(name, shape, dt))

        def sem(name):
            return ctx.enter_context(nc.semaphore(name))

        slot_rows = nc.dram_tensor("slot_rows", (SLOTS, ROW), F32, kind="Internal").ap()

        AT_W, E_W, KF_W, XT_W = ATW * T // 2, T * D, 2 * NPAD, K4 * NPAD
        one = sb("one", [P, AT_W + E_W + KF_W + XT_W])
        two = sb("two", [P, 2 * XT_W])

        def halves(region, start, words, pattern, **dims):
            w = words // 2
            return [region[:, start + i * w:start + (i + 1) * w].bitcast(F16).rearrange(pattern, **dims)
                    for i in range(2)]

        at = one[:, 0:AT_W].bitcast(F16).rearrange("p (a d) -> p a d", a=T)
        e_nat = halves(one, AT_W, E_W, "p (t n) -> p t n", t=T)
        kf = one[:, AT_W + E_W:AT_W + E_W + KF_W].rearrange("p (r n) -> p r n", r=2)
        gt = halves(one, AT_W + E_W, K4 * D, "p (k n) -> p k n", k=K4)
        xt = halves(one, AT_W + E_W + KF_W, XT_W, "p (k n) -> p k n", k=K4)
        ctxf = one[:, 0:D].rearrange("p (k n) -> p k n", k=K4)
        ffw = one[:, 0:NE * 2048].bitcast(F16).rearrange("p (e s n) -> p e s n", e=NE, s=4)
        ffh = one[:, 0:NE * 2048].bitcast(F16).rearrange("p (e s n) -> p e s n", e=2 * NE, s=2)
        tail = one[:, NE * 2048:NE * 2048 + 2560]
        xft = [halves(tail, s * 512, 512, "p (k n) -> p k n", k=K4) for s in range(2)]
        hidf = tail[:, 1024:1536].rearrange("p (s n) -> p s n", s=2)
        hid = [halves(tail, 1536 + s * 256, 256, "p (m n) -> p m n", m=2) for s in range(2)]
        xn = halves(two, 0, XT_W, "p (t n) -> p t n", t=T)
        rt = halves(two, 0, XT_W, "p (k n) -> p k n", k=K4)
        xnf = two[:, XT_W:2 * XT_W].rearrange("p (t n) -> p t n", t=T)
        qt = halves(two, XT_W, XT_W, "p (k n) -> p k n", k=K4)
        rb = two[:, 0:ET * ROW].rearrange("p (t n) -> p t n", t=ET)
        xff = two[:, ET * ROW:ET * ROW + 2 * D].rearrange("p (s n) -> p s n", s=2)

        X = sb("X", [P, T, ROW])
        wt = sb("wt", [P, 4, 2, K4, D], F16)
        b2b = wt[:, 1:3].rearrange("p w s k n -> p (w s k n)").bitcast(F32)
        stage = sb("stage", [P, 2, 1024])
        ohb = sb("ohb", [P, 2 * WCH, P], F16)
        ohk = sb("ohk", [P, 2 * WCH, KEYS], F16)
        keys = sb("keys", [P, 2, PAIRS])
        bc = sb("bc", [P, R_ALL])
        bias = sb("bias", [P, B_ALL])
        b1s = sb("b1s", [P, K4])
        qf = sb("qf", [P, 2, D])
        yf = qf
        ctxt = [sb(f"ctxt{i}", [P, K4, P], F16) for i in range(2)]
        cst = sb("cst", [P, C_ALL])
        csh = sb("csh", [P, H_ALL], F16)
        ident = cst[:, C_ID:C_ID + P]
        onesh = csh[:, H_ONE:H_ONE + P]
        small = sb("small", [P, 1016])
        used = [0]

        def sm(n, dt=F32):
            a = small[:, used[0]:used[0] + n]
            used[0] += n
            assert used[0] <= 1016, used
            return a if dt == F32 else a.bitcast(dt)

        def sm2(a, b, dt=F32):
            return sm(a * b, dt).rearrange("p (a b) -> p a b", a=a)

        ps = ctx.enter_context(nc.psum_tensor("ps", [P, 8, 512], F32))
        TB, AB, PB = 0, 2, 4

        stats, mv = sm2(T, 6), sm2(T, 2)
        vpe, sd, rstd, nwt = (sm(T) for _ in range(4))
        scr = one
        etab = scr[:, 0:256].bitcast(I32).rearrange("p (g n) -> p g n", g=2)
        got = [scr[0:PG, 256 * (g + 1):256 * (g + 2)].bitcast(I32) for g in range(GATHERS)]
        g_a = [scr[0:PG, 1024 + P * g:1024 + P * (g + 1)].bitcast(I32) for g in range(GATHERS)]
        g_b = [scr[0:PG, 1408 + P * g:1408 + P * (g + 1)].bitcast(I32) for g in range(GATHERS)]
        g_key = [scr[0:PG, 1792 + P * g:1792 + P * (g + 1)] for g in range(GATHERS)]
        g_bf = [scr[0:PG, 2176 + P * g:2176 + P * (g + 1)] for g in range(GATHERS)]
        before = scr[:, 2560:2560 + PAIRS].bitcast(F16).rearrange("p (g n) -> p g n", g=2)
        vio = [scr[:, 2900 + WINDOWS * i:2900 + WINDOWS * (i + 1)] for i in range(7)]
        emax, emin = sm(2), sm(2)
        pidx = sm(GATHERS, I32)
        viosum, vioh = sm(2), sm(1).bitcast(F16)
        flag = sm(1, I32)
        ge_i = kf[:, 0, 0:2 * ECF].bitcast(I32).rearrange("p (s n) -> p s n", s=2)
        ge_t = kf[:, 0, 2 * ECF:4 * ECF].bitcast(I32).rearrange("p (s n) -> p s n", s=2)
        ge_k = kf[:, 0, 4 * ECF:5 * ECF]
        ge_b = kf[:, 0, 5 * ECF:6 * ECF]
        ge_w = kf[:, 0, 6 * ECF:7 * ECF]
        kmax, ksum, krec = sm(K4), sm(K4), sm(K4)
        qmax, qsum, qrec = sm2(2, HEADS), sm2(2, HEADS), sm2(2, HEADS)
        wgf = sm2(K4, NE)
        wgs = sm(K4 * NE).bitcast(F16).rearrange("p (k s e) -> p k s e", k=K4, s=2)
        lgle = sm(2 * T * NE)
        lg, le = (lgle[:, i * T * NE:(i + 1) * T * NE].rearrange("p (t e) -> p t e", t=T) for i in range(2))
        oh, rk = sm2(T, NE), sm2(T, NE)
        ohp = sm((2 * T - 1) * NE // 2).bitcast(F16)
        ohh = ohp[:, (T - 1) * NE:].rearrange("p (t e) -> p t e", t=T)
        valid, lmax, lsum, lpick = sm(T), sm(T), sm(T), sm(T)
        slot_i = sm(T, I32)
        ne_i, tiles, base, ends = sm(NE, I32), sm(NE), sm(NE), sm(NE)
        tri_p = rk.rearrange("p a b -> p (a b)")[:, 0:NE * NE].rearrange("p (a b) -> p a b", a=NE)
        tile_p = lgle[:, 0:ET * NE].rearrange("p (j e) -> p j e", j=ET)
        texp_f, texp = sm(ET), sm(ET, I32)
        tokc = sm(2, I32)
        fill = qf[:, :, :].rearrange("p s n -> p (s n)")[:, 0:ROW]

        def sems(names):
            return [sem(n) for n in names.split()]

        consts_in, etab_in, rows_in, wg_in, b2f_in, pad_zero = sems("consts_in etab_in rows_in wg_in b2f_in pad_zero")
        x_in, w_in, row_in, out_done = sems("x_in0 x_in1"), sems("w_in0 w_in1"), sems("row_in0 row_in1"), sems("out_done0 out_done1")
        w_hi, w_lo, wg_hi, wg_lo = sems("w_hi w_lo wg_hi wg_lo")
        ln_step, ln_var, ln_sd, xnf_ok, xnh_ok, xnl_ok = sems("ln_step ln_var ln_sd xnf_ok xnh_ok xnl_ok")
        tr_done, tr_hi, tr_free = sems("tr_done tr_hi tr_free")
        ed_range, ed_before, ed_count, ed_idx, ed_int, ed_key, ed_turned, ed_vio, ed_viotot = sems(
            "ed_range ed_before ed_count ed_idx ed_int ed_key ed_turned ed_vio ed_viotot")
        ed_got = sems("ed_got0 ed_got1 ed_got2")
        keys_ok, flag_ok, oh_zero = sems("keys_ok flag_ok oh_zero")
        oh_ok, cnt_win, cnt_free, at_ok = sems("oh_ok cnt_win cnt_free at_ok")
        gen_in, gen_step, gen_oh, gen_mm, gen_ev = sems("gen_in gen_step gen_oh gen_mm gen_ev")
        pj_done, pj_hi, pj_free = sems("pj_done pj_hi pj_free")
        kf_zero, k_max, k_exp, k_rec, k_norm = sems("kf_zero k_max k_exp k_rec k_norm")
        q_lin, q_max, q_sub, q_exp, q_sum, q_rec, q_norm = sems("q_lin q_max q_sub q_exp q_sum q_rec q_norm")
        xb_ok, ct_zero, ct_f, ct_hi, ct_lo, b1s_ok, r_lin, r_lo, pads_ok = sems(
            "xb_ok ct_zero ct_f ct_hi ct_lo b1s_ok r_lin r_lo pads_ok")
        l2_step, l2_var, l2_sd, xf_ok, xg_ok, gate_done, g_step, g_exp, rank_done = sems(
            "l2_step l2_var l2_sd xf_ok xg_ok gate_done g_step g_exp rank_done")
        fill_ok, fill_out, tok_ok, slot_ok, sent, texp_ok = sems("fill_ok fill_out tok_ok slot_ok sent texp_ok")
        f_x, f_tr, f_hi, f_xt, f_h, f_hr, f_hf, f_hl, f_y, f_yb, f_tok, f_out = sems(
            "f_x f_tr f_hi f_xt f_h f_hr f_hf f_hl f_y f_yb f_tok f_out")

        J_K, J_Q = 0, NCH * K4
        J_A = J_Q + T
        J_G = J_A + NCH * K4
        J_C = J_G + K4
        J_1 = J_C + 1
        J_2 = J_1 + NCH * K4
        J_END = J_2 + T
        FREE0 = 3
        T_X, T_E = 0, T
        T_Q = T_E + NCH * K4
        T_F = T_Q + T
        ETB = ((0, 4), (4, 4), (8, 2))
        WHALVES = 10
        w_dram = [w.rearrange("(k p) n -> p k n", p=P) for w in (wk, wq, wv, g1, g2)]
        w_slot = (0, 1, 2, 3, 0)
        WK, WQ, WV, WG1, WG2 = w_slot
        LN_STEPS = 15

        block = ctx.enter_context(nc.Block())

        @block.sync
        def _(sp):
            sp.dma_start(X[:, 0:5, 0:D], x[0:5 * P, :].rearrange("(t p) n -> p t n", p=P)).then_inc(x_in[0], 16)
            sp.dma_start(X[:, 5:9, 0:D], x[5 * P:9 * P, :].rearrange("(t p) n -> p t n", p=P)).then_inc(x_in[1], 16)
            sp.wait_ge(pad_zero, 1)
            sp.dma_start(X[0:LAST, T - 1, 0:D], x[(T - 1) * P:N, :]).then_inc(x_in[1], 16)
            for i in range(WHALVES):
                if i >= 2:
                    sp.wait_ge(w_lo, i - 1)
                sp.dma_start(stage[:, i % 2, :].rearrange("p (k n) -> p k n", k=2),
                             w_dram[i // 2][:, 2 * (i % 2):2 * (i % 2) + 2, :]).then_inc(w_in[i % 2], 16)
            with sp.Fori(0, NE) as e:
                sp.wait_ge(w_lo, WHALVES - 1 + 2 * e)
                sp.dma_start(stage[:, 0, :].rearrange("p (k n) -> p k n", k=K4),
                             w1[bass.ds(e * D, D), :].rearrange("(k p) n -> p k n", p=P)).then_inc(w_in[0], 16)
                sp.wait_ge(w_lo, WHALVES + 2 * e)
                sp.dma_start(stage[:, 1, :].rearrange("p (k n) -> p k n", k=2),
                             w2[bass.ds(e * HID, HID), :].rearrange("(k p) n -> p k n", p=P)).then_inc(w_in[1], 16)
            sp.wait_ge(pj_done, J_1)
            sp.dma_start(b2b, b2f.partition_broadcast(P)).then_inc(b2f_in, 16)
            sp.wait_ge(sent, 16 * T)
            sp.wait_ge(fill_out, 16)
            sp.wait_ge(pj_free, FREE0 + J_END)

            def slot_row(j, s):
                sp.dma_start(rb[:, bass.ds(j, 1), :].rearrange("p o n -> p (o n)"),
                             slot_rows[bass.ds(j * P, P), :]).then_inc(row_in[s], 16)

            slot_row(0, 0)
            slot_row(1, 1)
            with sp.Fori(1, ET // 2) as i:
                for s in range(2):
                    sp.wait_ge(row_in[s], 16 * i)
                    slot_row(2 * i + s, s)
            sp.wait_ge(row_in[0], 16 * (ET // 2))
            slot_row(ET - 1, 0)

        @block.gpsimd
        def _(pool):
            pool.memset(X[:, T - 1, :], 0.0).then_inc(pad_zero, 1)
            pool.memset(fill[:, 0:ROW - 1], 0.0).then_inc(fill_ok, 1)
            pool.memset(fill[:, ROW - 1:ROW].bitcast(I32), NO_TOKEN).then_inc(fill_ok, 1)
            pool.wait_ge(ed_idx, 1)
            for g in range(GATHERS):
                pool.indirect_dma_start(out=got[g], out_offset=None, in_=edges,
                                        in_offset=bass.IndirectOffsetOnAxis(ap=pidx[0:PG, g:g + 1], axis=0),
                                        bounds_check=ECP - 1, oob_is_err=False).then_inc(ed_got[g], 16)
            pool.wait_ge(fill_ok, 2)
            pool.dma_start(slot_rows.rearrange("(t p) n -> p t n", p=P),
                           fill.unsqueeze(1).to_broadcast([P, ET, ROW])).then_inc(fill_out, 16)
            for i in range(2):
                pool.memset(ctxt[i][:, :, :], 0.0).then_inc(ct_zero, 1)
            pool.wait_ge(rows_in, 32)
            pool.wait_ge(xnf_ok, T)
            for t in range(T):
                pool.tensor_tensor(X[:, t, 0:D], X[:, t, 0:D], bc[:, R_B2:R_B2 + D], ALU.add).then_inc(xb_ok, 1)

            def by_head(s):
                return qf[:, s, :].rearrange("p (h n) -> p h n", h=HEADS)

            with pool.Fori(0, T // 2) as i:
                for s in range(2):
                    pool.wait_ge(q_max, 2 * i + s + 1)
                    pool.tensor_tensor(by_head(s), by_head(s), qmax[:, s, :].unsqueeze(2).to_broadcast([P, HEADS, DH]),
                                       ALU.add).then_inc(q_sub, 1)
                    pool.wait_ge(q_rec, 2 * i + s + 1)
                    pool.tensor_tensor(by_head(s), by_head(s), qrec[:, s, :].unsqueeze(2).to_broadcast([P, HEADS, DH]),
                                       ALU.mult).then_inc(q_norm, 1)
            pool.wait_ge(slot_ok, 1)
            pool.wait_ge(tok_ok, 1)
            pool.wait_ge(fill_out, 16)
            for t in range(T):
                r = P if t < T - 1 else LAST
                pool.indirect_dma_start(out=slot_rows, out_offset=bass.IndirectOffsetOnAxis(ap=slot_i[0:r, t:t + 1], axis=0),
                                        in_=X[0:r, t, :], in_offset=None, bounds_check=SLOTS - 1, oob_is_err=False).then_inc(sent, 16)

            for j in range(ET):
                s = j % 2
                pool.wait_ge(f_out, j + 1)
                pool.indirect_dma_start(out=out, out_offset=bass.IndirectOffsetOnAxis(ap=tokc[:, s:s + 1], axis=0),
                                        in_=yf[:, s, :], in_offset=None, bounds_check=N - 1, oob_is_err=False).then_inc(out_done[s], 16)

            pool.wait_ge(out_done[0], 16 * (ET // 2 + 1))
            pool.wait_ge(out_done[1], 16 * (ET // 2))

        @block.tensor
        def _(pe):
            def three(o, lhs, rhs, start, stop):
                pe.matmul(o, lhs[0], rhs[0], start=start, stop=False)
                pe.matmul(o, lhs[0], rhs[1], start=False, stop=False)
                return pe.matmul(o, lhs[1], rhs[0], start=False, stop=stop)

            pe.wait_ge(consts_in, 32)
            pe.wait_ge(ed_before, 2)
            for g in range(GATHERS):
                for h in range(2):
                    pe.matmul(ps[0:PG, 5, g:g + 1], before[:, h, g * PG:(g + 1) * PG], onesh[:, 0:1], start=(h == 0), stop=(h == 1))
            for h in range(2):
                mm = pe.matmul(ps[:, 5, 64:64 + WINDOWS], onesh, before[:, h, 0:PAIRS:WCH], start=(h == 0), stop=(h == 1))
            mm.then_inc(ed_count, 1)

            def turn_x(t):
                pe.wait_ge(xnf_ok, t + 1)
                if t >= 2:
                    pe.wait_ge(tr_free, t - 1)
                for k in range(K4):
                    mm = pe.transpose(ps[:, TB + t % 2, k * P:(k + 1) * P], xnf[:, t, k * P:(k + 1) * P], ident)
                mm.then_inc(tr_done, 1)

            for t in range(5):
                turn_x(t)
            pe.wait_ge(ed_key, GATHERS)
            for g in range(GATHERS):
                pe.transpose(ps[:, 7, g * PG:(g + 1) * PG], g_key[g], ident[0:PG, 0:PG])
            for g in range(GATHERS):
                mm = pe.transpose(ps[:, 6, g * PG:(g + 1) * PG], g_bf[g], ident[0:PG, 0:PG])
            mm.then_inc(ed_turned, 1)
            for t in range(5, T):
                turn_x(t)

            def count_pair(q, b):
                pe.wait_ge(cnt_free, q + 1)
                for h in range(2):
                    pe.wait_ge(oh_ok, 2 * q + h + 1)
                    for k in range(WCH):
                        mm = pe.matmul(ps[:, AB + b, h * KEYS:(h + 1) * KEYS], ohb[:, h * WCH + k, :], ohk[:, h * WCH + k, :],
                                       start=(k == 0), stop=(k == WCH - 1))
                    mm.then_inc(cnt_win, 1)

            pe.wait_ge(keys_ok, 2)
            pe.wait_ge(pj_free, FREE0)
            pe.wait_ge(w_lo, 2)
            pe.wait_ge(tr_free, T)
            pe.matmul(ps[0:1, PB, 0:1], vioh[:, 0:1], onesh[:, 0:1], start=True, stop=True).then_inc(ed_viotot, 1)
            with pe.Fori(0, K4 // 2) as i:
                for r in range(2):
                    m = 2 * i + r
                    for c, (n0, n) in enumerate(CH):
                        pe.wait_ge(pj_free, FREE0 + NCH * m + c - 2)
                        o = ps[:, PB + 1 + c, 0:n]
                        for k in range(K4):
                            lhs = [wt[:, WK, s, k, bass.ds(m * P, P)] for s in range(2)]
                            mm = three(o, lhs, [xt[s][:, k, n0:n0 + n] for s in range(2)], k == 0, k == K4 - 1)
                        mm.then_inc(pj_done, 1)
                        count_pair(2 * AK * i + AK * r + c, (AK * r + c) % 2)
                    count_pair(2 * AK * i + AK * r + NCH, (AK * r + NCH) % 2)
                    pe.wait_ge(k_norm, m + 1)
                    for b, (t0, nt) in enumerate(ETB):
                        pe.wait_ge(tr_free, T_E + NCH * m + b - 1)
                        for t in range(nt):
                            mm = pe.transpose(ps[:, TB + (NCH * r + b) % 2, t * P:(t + 1) * P],
                                              kf[:, r, (t0 + t) * P:(t0 + t + 1) * P], ident)
                        mm.then_inc(tr_done, 1)

            def q_rows(t, s):
                pe.wait_ge(pj_free, FREE0 + J_Q + t - 1)
                for k in range(K4):
                    lhs = [xt[h][:, k, bass.ds(t * P, P)] for h in range(2)]
                    mm = three(ps[:, PB + 1 + s, :], lhs, [wt[:, WQ, h, k, :] for h in range(2)], k == 0, k == K4 - 1)
                mm.then_inc(pj_done, 1)

            def turn_q(t, s):
                pe.wait_ge(q_norm, t + 1)
                pe.wait_ge(tr_free, T_Q + t - 1)
                for k in range(K4):
                    mm = pe.transpose(ps[:, TB + s, k * P:(k + 1) * P], qf[:, s, k * P:(k + 1) * P], ident)
                mm.then_inc(tr_done, 1)

            CQ = K4 * AK
            pe.wait_ge(w_lo, 4)
            for s in range(2):
                q_rows(s, s)
                count_pair(CQ + s, s)
            with pe.Fori(1, T // 2) as i:
                for s in range(2):
                    turn_q(2 * i + s - 2, s)
                    q_rows(2 * i + s, s)
                    count_pair(CQ + 2 * i + s, s)
            turn_q(T - 2, 0)
            turn_q(T - 1, 1)
            count_pair(WPAIRS - 1, (WPAIRS - 1) % 2)

            pe.wait_ge(flag_ok, 1)
            general = pe.value_load(flag[0:1, 0:1], min_val=0, max_val=1)
            with pe.If(general > 0):
                with pe.Fori(0, WINDOWS) as w:
                    pe.wait_ge(gen_ev, w + 1)

                    def count(c, start, stop):
                        pe.wait_ge(gen_oh, w * EC + c + 1)
                        pe.matmul(ps[:, AB, 0:KEYS], ohb[:, 0, :], ohk[:, 0, :], start=start, stop=stop).then_inc(gen_mm, 1)

                    count(0, True, False)
                    with pe.Fori(1, EC - 1) as c:
                        count(c, False, False)
                    count(EC - 1, False, True)

            pe.wait_ge(at_ok, T)
            pe.wait_ge(xnl_ok, T)
            with pe.Fori(0, K4) as m:
                for c, (n0, n) in enumerate(CH):
                    pe.wait_ge(pj_free, FREE0 + J_A + NCH * m + c - 1)
                    o = ps[:, PB + 1 + c, 0:n]
                    for a in range(T):
                        for s in range(2):
                            mm = pe.matmul(o, xn[s][:, a, bass.ds(m * P, P)], at[:, a, n0:n0 + n],
                                           start=(a == 0 and s == 0), stop=(a == T - 1 and s == 1))
                    mm.then_inc(pj_done, 1)

            pe.wait_ge(tr_free, T_Q)
            with pe.Fori(0, K4) as m:
                pe.wait_ge(pj_free, FREE0 + J_G + m - 1)
                for t in range(T):
                    mm = three(ps[:, bass.ds(PB + m, 1), :].rearrange("p o n -> p (o n)"), [xn[s][:, t, bass.ds(m * P, P)] for s in range(2)],
                               [e_nat[s][:, t, :] for s in range(2)], t == 0, t == T - 1)
                mm.then_inc(pj_done, 1)

            pe.wait_ge(w_lo, 6)
            pe.wait_ge(pj_free, FREE0 + J_C)
            for p in range(K4):
                for k in range(K4):
                    mm = three(ps[:, PB, p * P:(p + 1) * P], [gt[s][:, k, p * P:(p + 1) * P] for s in range(2)],
                               [wt[:, WV, s, k, p * P:(p + 1) * P] for s in range(2)], k == 0, k == K4 - 1)
            mm.then_inc(pj_done, 1)

            pe.wait_ge(w_lo, 8)
            with pe.Fori(0, K4) as m:
                for c, (n0, n) in enumerate(CH):
                    pe.wait_ge(pj_free, FREE0 + J_1 + NCH * m + c - 1)
                    for k in range(K4):
                        mm = three(ps[:, PB + 1 + c, 0:n], [wt[:, WG1, s, k, bass.ds(m * P, P)] for s in range(2)],
                                   [xt[s][:, k, n0:n0 + n] for s in range(2)], k == 0, k == K4 - 1)
                    mm.then_inc(pj_done, 1)

            pe.wait_ge(w_lo, WHALVES)
            pe.wait_ge(r_lo, NCH * K4 + 1)
            pe.wait_ge(pads_ok, 2)
            pe.wait_ge(ct_lo, 1)
            pe.wait_ge(tr_free, T_F)
            with pe.Fori(0, T // 2) as i:
                for s in range(2):
                    t = 2 * i + s
                    pe.wait_ge(pj_free, FREE0 + J_2 + t - 1)
                    def layer(ks):
                        for k in ks:
                            mm = three(ps[:, PB + 1 + s, :], [rt[h][:, k, bass.ds(t * P, P)] for h in range(2)],
                                       [wt[:, WG2, h, k, :] for h in range(2)], k == 0, k == K4 - 1)
                        return mm

                    layer(range(K4 - 1))
                    for p in range(K4):
                        o = ps[:, PB + 1 + s, p * P:(p + 1) * P]
                        lhs = [qt[h][:, p, bass.ds(t * P, P)] for h in range(2)]
                        pe.matmul(o, lhs[0], ctxt[0][:, p, :], start=False, stop=False, skip_group_check=True)
                        pe.matmul(o, lhs[0], ctxt[1][:, p, :], start=False, stop=False, skip_group_check=True)
                        pe.matmul(o, lhs[1], ctxt[0][:, p, :], start=False, stop=False, skip_group_check=True)
                    layer([K4 - 1]).then_inc(pj_done, 1)

            pe.wait_ge(wg_lo, 1)

            def gate(t):
                pe.wait_ge(xg_ok, t + 1)
                for k in range(K4):
                    for s in range(2):
                        mm = pe.matmul(ps[:, AB + 1, t * 2 * NE:(t + 1) * 2 * NE], xft[t % 2][s][:, k, :],
                                       wgs[:, k, :, :].rearrange("p s e -> p (s e)"), start=(k == 0 and s == 0), stop=(k == K4 - 1 and s == 1))
                mm.then_inc(gate_done, 1)

            for t in range(T):
                pe.wait_ge(xf_ok, t + 1)
                pe.wait_ge(tr_free, T_F + t - 1)
                for k in range(K4):
                    mm = pe.transpose(ps[:, TB + t % 2, k * P:(k + 1) * P], qf[:, t % 2, k * P:(k + 1) * P], ident)
                mm.then_inc(tr_done, 1)
                if t >= 1:
                    gate(t - 1)
            gate(T - 1)
            pe.wait_ge(g_step, 10)
            rk_o = ps[:, AB, 0:T * NE]
            pe.matmul(rk_o, csh[:, H_TRI:H_TRI + P], ohh.rearrange("p t e -> p (t e)"), start=True, stop=False)
            for back in range(1, T):
                pe.matmul(rk_o, onesh, ohp[:, (T - 1 - back) * NE:(2 * T - 1 - back) * NE], start=False, stop=(back == T - 1))
            for t in range(T):
                mm = pe.matmul(ps[:, PB + 3, 0:NE], onesh, ohh[:, t, :], start=(t == 0), stop=(t == T - 1))
            mm.then_inc(rank_done, 1)

            def expert_of(j):
                return pe.value_load(texp[0:1, bass.ds(j, 1)], min_val=0, max_val=NE - 1)

            def turn_f(j, s):
                pe.wait_ge(f_x, j + 1)
                for k in range(K4):
                    mm = pe.transpose(ps[:, TB + s, k * P:(k + 1) * P], xff[:, s, k * P:(k + 1) * P], ident)
                mm.then_inc(f_tr, 1)

            def layer1(j, s):
                e = expert_of(j)
                pe.wait_ge(f_xt, j + 1)
                for m in range(2):
                    for k in range(K4):
                        lhs = [ffw[:, bass.ds(e, 1), h, k * HID + m * P:k * HID + (m + 1) * P].rearrange("p o n -> p (o n)") for h in range(2)]
                        mm = three(ps[:, AB + s, m * P:(m + 1) * P], lhs, [xft[s][h][:, k, :] for h in range(2)], k == 0, k == K4 - 1)
                mm.then_inc(f_h, 1)

            def layer2(j, s):
                e = expert_of(j)
                pe.wait_ge(f_hl, j + 1)
                for k in range(2):
                    rhs = [ffw[:, bass.ds(e, 1), 2 + h, k * D:(k + 1) * D].rearrange("p o n -> p (o n)") for h in range(2)]
                    mm = three(ps[:, PB + s, :], [hid[s][h][:, k, :] for h in range(2)], rhs, k == 0, k == 1)
                mm.then_inc(f_y, 1)

            pe.wait_ge(texp_ok, 1)
            turn_f(0, 0)
            turn_f(1, 1)
            pe.wait_ge(w_lo, WHALVES + 2 * NE)
            layer1(0, 0)
            with pe.Fori(0, (ET - 3) // 2) as i:
                for s in range(2):
                    turn_f(2 * i + s + 2, s)
                    layer1(2 * i + s + 1, 1 - s)
                    layer2(2 * i + s, s)
            turn_f(ET - 1, 0)
            layer1(ET - 2, 1)
            layer2(ET - 3, 0)
            layer1(ET - 1, 0)
            layer2(ET - 2, 1)
            layer2(ET - 1, 0)

        @block.scalar
        def _(act):
            act.dma_start(etab, edges.rearrange("(g p) n -> p g n", p=P)[:, :, P:2 * P]).then_inc(etab_in, 16)
            act.dma_start(cst[:, :], cf).then_inc(consts_in, 16)
            act.dma_start(csh[:, :], ch).then_inc(consts_in, 16)
            act.dma_start(bias[:, :], cols).then_inc(rows_in, 16)
            act.dma_start(bc[:, :], rows.partition_broadcast(P)).then_inc(rows_in, 16)
            act.dma_start(wgf, wg.rearrange("(k p) e -> p k e", p=P)).then_inc(wg_in, 16)

            def xn_tiles(ts):
                for t in ts:
                    act.wait_ge(xnf_ok, t + 1)
                    act.activation(xn[0][:, t, :], xnf[:, t, :], ACT.Copy).then_inc(xnh_ok, 1)
                    act.wait_ge(tr_done, t + 1)
                    act.activation(xt[0][:, :, t * P:(t + 1) * P], ps[:, TB + t % 2, :].rearrange("p (k n) -> p k n", k=K4),
                                   ACT.Copy).then_inc(tr_hi, 1)

            def w_part(i):
                act.wait_ge(w_in[i % 2], 16 * (i // 2 + 1))
                if i // 2 == 4:
                    act.wait_ge(pj_done, J_Q)
                act.activation(wt[:, w_slot[i // 2], 0, 2 * (i % 2):2 * (i % 2) + 2, :],
                               stage[:, i % 2, :].rearrange("p (k n) -> p k n", k=2), ACT.Copy, scale=WS).then_inc(w_hi, 1)

            for g in range(2):
                act.wait_ge(ln_var, g + 1)
                act.activation(sd[:, 5 * g:5 * g + 5], vpe[:, 5 * g:5 * g + 5], ACT.Sqrt).then_inc(ln_sd, 1)
                xn_tiles(range(5 * g, 5 * g + 5))
                w_part(2 * g)
                w_part(2 * g + 1)
            act.wait_ge(wg_in, 16)
            act.activation(wgs[:, :, 0, :], wgf, ACT.Copy, scale=WS).then_inc(wg_hi, 1)
            act.wait_ge(rows_in, 32)
            act.activation(b1s[:, :], bias[:, B_G1:B_G1 + K4], ACT.Copy, scale=HS).then_inc(b1s_ok, 1)
            act.preload_act_table(ACT.Exp)

            def counted(q, b):
                act.wait_ge(cnt_win, 2 + 2 * q + 2)
                act.activation(at[:, :, bass.ds(2 * WN * q, 2 * WN)],
                               ps[:, AB + b, 0:2 * KEYS].rearrange("p (d a) -> p a d", a=T), ACT.Copy).then_inc(cnt_free, 1)

            with act.Fori(0, K4 // 2) as i:
                for r in range(2):
                    m = 2 * i + r
                    for c in range(NCH):
                        counted(2 * AK * i + AK * r + c, (AK * r + c) % 2)
                    act.wait_ge(k_max, m + 1)
                    act.activation(kf[:, r, 0:N], kf[:, r, 0:N], ACT.Exp, bias=kmax[:, bass.ds(m, 1)],
                                   accum_out=ksum[:, bass.ds(m, 1)]).then_inc(k_exp, 1)
                    act.wait_ge(k_rec, m + 1)
                    act.activation(kf[:, r, 0:N], kf[:, r, 0:N], ACT.Copy, scale=krec[:, bass.ds(m, 1)]).then_inc(k_norm, 1)
                    counted(2 * AK * i + AK * r + NCH, (AK * r + NCH) % 2)
                    for b, (t0, nt) in enumerate(ETB):
                        act.wait_ge(tr_done, T_E + NCH * m + b + 1)
                        act.activation(e_nat[0][:, t0:t0 + nt, bass.ds(m * P, P)],
                                       ps[:, TB + (NCH * r + b) % 2, 0:nt * P].rearrange("p (t n) -> p t n", t=nt),
                                       ACT.Copy, scale=KS).then_inc(tr_hi, 1)

            CQ = K4 * AK

            def q_exps(t, s):
                act.wait_ge(q_sub, t + 1)
                act.activation(qf[:, s, :], qf[:, s, :], ACT.Exp).then_inc(q_exp, 1)

            def q_turned(t, s):
                act.wait_ge(tr_done, T_Q + t + 1)
                act.activation(qt[0][:, :, bass.ds(t * P, P)], ps[:, TB + s, :].rearrange("p (k n) -> p k n", k=K4),
                               ACT.Copy).then_inc(tr_hi, 1)

            for s in range(2):
                q_exps(s, s)
                counted(CQ + s, s)
            with act.Fori(1, T // 2) as i:
                for s in range(2):
                    q_turned(2 * i + s - 2, s)
                    q_exps(2 * i + s, s)
                    counted(CQ + 2 * i + s, s)
            q_turned(T - 2, 0)
            q_turned(T - 1, 1)
            counted(WPAIRS - 1, (WPAIRS - 1) % 2)

            act.wait_ge(flag_ok, 1)
            general = act.value_load(flag[0:1, 0:1], min_val=0, max_val=1)
            with act.If(general > 0):
                act.dma_start(ge_i, edge_cols).then_inc(gen_in, 16)
                with act.Fori(0, WINDOWS) as w:
                    act.wait_ge(gen_mm, w * EC + EC + 1)
                    act.activation(at[:, :, bass.ds(WN * w, WN)], ps[:, AB, 0:KEYS].rearrange("p (d a) -> p a d", a=T),
                                   ACT.Copy).then_inc(gen_ev, 1)

            for i in range(4, WHALVES):
                w_part(i)
            with act.Fori(0, K4) as m:
                for c, (n0, n) in enumerate(CH):
                    act.wait_ge(pj_done, J_A + NCH * m + c + 1)
                    act.activation(xt[0][:, bass.ds(m, 1), n0:n0 + n].rearrange("p o n -> p (o n)"), ps[:, PB + 1 + c, 0:n],
                                   ACT.Copy, scale=HS).then_inc(pj_hi, 1)
            for m in range(K4):
                act.wait_ge(pj_done, J_G + m + 1)
                act.activation(gt[0][:, m, :], ps[:, PB + m, :], ACT.Copy, scale=1 / KS).then_inc(pj_hi, 1)
            act.wait_ge(ct_f, 2)
            act.wait_ge(ct_zero, 2)
            for h in range(2):
                r = slice(h * DH, (h + 1) * DH)
                act.activation(ctxt[0][r, :, r], ctxf[r, :, r], ACT.Copy).then_inc(ct_hi, 1)
            def expert_part(h, s, landed):
                act.wait_ge(w_in[s], 16 * (WHALVES // 2) + 16 * landed)
                act.activation(ffh[:, bass.ds(h, 1), 0, :].rearrange("p o n -> p (o n)"), stage[:, s, :], ACT.Copy, scale=WS).then_inc(w_hi, 1)

            act.wait_ge(ct_lo, 1)
            with act.Fori(0, K4 // 2) as i:
                for r in range(2):
                    m = 2 * i + r
                    for c, (n0, n) in enumerate(CH):
                        act.wait_ge(pj_done, J_1 + NCH * m + c + 1)
                        act.activation(rt[0][:, bass.ds(m, 1), n0:n0 + n].rearrange("p o n -> p (o n)"), ps[:, PB + 1 + c, 0:n],
                                       ACT.Relu, scale=1 / WS, bias=b1s[:, bass.ds(m, 1)]).then_inc(pj_hi, 1)
                        u = NCH * r + c
                        expert_part(2 * NCH * i + u, u % 2, NCH * i + u // 2 + 1)
            act.wait_ge(pj_done, J_2)
            for h in range(NCH * K4, 2 * NE):
                expert_part(h, h % 2, h // 2 + 1)
            for g in range(2):
                act.wait_ge(l2_var, g + 1)
                act.activation(sd[:, 5 * g:5 * g + 5], vpe[:, 5 * g:5 * g + 5], ACT.Sqrt).then_inc(l2_sd, 1)
                for t in range(5 * g, 5 * g + 5):
                    act.wait_ge(tr_done, T_F + t + 1)
                    if t >= 2:
                        act.wait_ge(gate_done, t - 1)
                    act.activation(xft[t % 2][0], ps[:, TB + t % 2, :].rearrange("p (k n) -> p k n", k=K4), ACT.Copy).then_inc(tr_hi, 1)
            act.wait_ge(g_step, 5)
            act.activation(le, le, ACT.Exp).then_inc(g_exp, 1)

            def turned_f(j, s):
                act.wait_ge(f_tr, j + 1)
                act.activation(xft[s][0], ps[:, TB + s, :].rearrange("p (k n) -> p k n", k=K4), ACT.Copy).then_inc(f_hi, 1)

            def relu_f(j, s):
                e = act.value_load(texp[0:1, bass.ds(j, 1)], min_val=0, max_val=NE - 1)
                act.wait_ge(f_h, j + 1)
                for m in range(2):
                    act.activation(hid[s][0][:, m, :], ps[:, AB + s, m * P:(m + 1) * P], ACT.Relu, scale=1 / WS,
                                   bias=bias[:, bass.ds(B_F1 + 2 * e + m, 1)]).then_inc(f_hr, 1)

            act.wait_ge(texp_ok, 1)
            turned_f(0, 0)
            turned_f(1, 1)
            relu_f(0, 0)
            with act.Fori(0, (ET - 3) // 2) as i:
                for s in range(2):
                    turned_f(2 * i + s + 2, s)
                    relu_f(2 * i + s + 1, 1 - s)
            turned_f(ET - 1, 0)
            relu_f(ET - 2, 1)
            relu_f(ET - 1, 0)

        @block.vector
        def _(dve):
            dve.wait_ge(etab_in, 16)
            dve.tensor_reduce(emax, etab, AX.X, ALU.max).then_inc(ed_range, 1)
            dve.tensor_reduce(emin, etab, AX.X, ALU.min).then_inc(ed_range, 1)
            dve.wait_ge(consts_in, 32)
            dve.wait_ge(ed_range, 2)
            for g in range(2):
                dve.tensor_scalar(before[:, g, :], cst[:, C_THR:C_THR + PAIRS], emax[:, g:g + 1], None, ALU.is_gt).then_inc(ed_before, 1)

            def statistics(g, landed, step, var, base):
                ts = range(5 * g, 5 * g + 5)
                c = slice(5 * g, 5 * g + 5)
                for t in ts:
                    landed(t)
                    dve.bn_stats(stats[:, t, :], X[:, t, 0:D]).then_inc(step, 1)
                dve.wait_ge(step, base + 5)
                for t in ts:
                    dve.bn_aggr(mv[:, t, :], stats[:, t, :]).then_inc(step, 1)
                dve.wait_ge(step, base + 10)
                dve.tensor_scalar(vpe[:, c], mv[:, c, 1], EPS, None, ALU.add).then_inc(var, 1)

            def inverse(g, step, var, sdone, base):
                c = slice(5 * g, 5 * g + 5)
                dve.wait_ge(sdone, g + 1)
                dve.wait_ge(var, g + 1)
                dve.reciprocal(sd[:, c], sd[:, c]).then_inc(step, 1)
                dve.wait_ge(step, base + 11)
                dve.tensor_tensor(nwt[:, c], sd[:, c], sd[:, c], ALU.mult).then_inc(step, 1)
                dve.wait_ge(step, base + 12)
                dve.tensor_tensor(nwt[:, c], nwt[:, c], vpe[:, c], ALU.mult).then_inc(step, 1)
                dve.wait_ge(step, base + 13)
                dve.tensor_scalar(nwt[:, c], nwt[:, c], -0.5, 1.5, ALU.mult, ALU.add).then_inc(step, 1)
                dve.wait_ge(step, base + 14)
                dve.tensor_tensor(rstd[:, c], sd[:, c], nwt[:, c], ALU.mult).then_inc(step, 1)
                dve.wait_ge(step, base + 15)

            def xn_tiles(ts):
                for t in ts:
                    dve.tensor_scalar(xnf[:, t, :], X[:, t, 0:D], mv[:, t, 0:1], rstd[:, t:t + 1],
                                      ALU.subtract, ALU.mult).then_inc(xnf_ok, 1)
                for t in ts:
                    dve.wait_ge(xnh_ok, t + 1)
                    dve.wait_ge(xnf_ok, t + 1)
                    dve.tensor_tensor(xn[1][:, t, :], xnf[:, t, :], xn[0][:, t, :], ALU.subtract).then_inc(xnl_ok, 1)
                    dve.wait_ge(tr_hi, t + 1)
                    dve.tensor_tensor(xt[1][:, :, t * P:(t + 1) * P], ps[:, TB + t % 2, :].rearrange("p (k n) -> p k n", k=K4),
                                      xt[0][:, :, t * P:(t + 1) * P], ALU.subtract).then_inc(tr_free, 1)

            def w_part(i):
                dve.wait_ge(w_hi, i + 1)
                dve.scalar_tensor_tensor(wt[:, w_slot[i // 2], 1, 2 * (i % 2):2 * (i % 2) + 2, :].rearrange("p k n -> p (k n)"),
                                         stage[:, i % 2, :], WS,
                                         wt[:, w_slot[i // 2], 0, 2 * (i % 2):2 * (i % 2) + 2, :].rearrange("p k n -> p (k n)"),
                                         ALU.mult, ALU.subtract).then_inc(w_lo, 1)

            statistics(0, lambda t: dve.wait_ge(x_in[0], 16), ln_step, ln_var, 0)
            dve.wait_ge(ed_count, 1)
            dve.tensor_tensor(pidx[0:PG, :], ps[0:PG, 5, 0:GATHERS], cst[0:PG, C_K:C_K + GATHERS], ALU.add).then_inc(ed_idx, 1)
            dve.tensor_copy(vio[0], ps[:, 5, 64:64 + WINDOWS]).then_inc(pj_free, 1)
            inverse(0, ln_step, ln_var, ln_sd, 0)
            xn_tiles(range(0, 5))
            for g in range(GATHERS):
                dve.wait_ge(ed_got[g], 16)
                dve.tensor_scalar(g_a[g], got[g][:, 0:P], 7, None, ALU.logical_shift_right).then_inc(ed_int, 1)
                dve.tensor_scalar(g_b[g], got[g][:, 0:P], P - 1, None, ALU.bitwise_and).then_inc(ed_int, 1)
                dve.wait_ge(ed_int, 4 * g + 2)
                dve.scalar_tensor_tensor(g_key[g], got[g][:, P:2 * P], float(T), g_a[g], ALU.mult, ALU.add).then_inc(ed_int, 1)
                dve.tensor_copy(g_bf[g], g_b[g]).then_inc(ed_int, 1)
                dve.wait_ge(ed_int, 4 * g + 4)
                dve.tensor_scalar(g_key[g], g_key[g], cst[0:PG, C_WK + g:C_WK + g + 1], None, ALU.subtract).then_inc(ed_key, 1)
            VS = 0
            dve.wait_ge(pj_free, 1)
            for g in range(2):
                thr = cst[:, C_THR:C_THR + PAIRS:WCH]
                last, first, dist, sq = vio[1], vio[2], vio[3], vio[4]
                dve.tensor_scalar(last, thr, emax[:, g:g + 1], None, ALU.is_le).then_inc(ed_vio, 1)
                dve.tensor_scalar(first, thr, float(WN - 1), emin[:, g:g + 1], ALU.add, ALU.is_ge).then_inc(ed_vio, 1)
                dve.tensor_scalar(dist, vio[0], -1.0, cst[:, C_C + g:C_C + g + 1], ALU.mult, ALU.add).then_inc(ed_vio, 1)
                dve.wait_ge(ed_vio, VS + 3)
                dve.tensor_scalar(dist, dist, -(WCH - 1) / 2, None, ALU.add).then_inc(ed_vio, 1)
                dve.tensor_tensor(last, last, first, ALU.mult).then_inc(ed_vio, 1)
                dve.wait_ge(ed_vio, VS + 5)
                dve.tensor_tensor(sq, dist, dist, ALU.mult).then_inc(ed_vio, 1)
                dve.wait_ge(ed_vio, VS + 6)
                dve.tensor_scalar(sq, sq, (WCH / 2) ** 2, None, ALU.is_gt).then_inc(ed_vio, 1)
                dve.wait_ge(ed_vio, VS + 7)
                dve.tensor_tensor(sq, sq, last, ALU.mult).then_inc(ed_vio, 1)
                dve.wait_ge(ed_vio, VS + 8)
                dve.tensor_reduce(viosum[:, g:g + 1], sq, AX.X, ALU.max).then_inc(ed_vio, 1)
                VS += 9
                dve.wait_ge(ed_vio, VS)
            statistics(1, lambda t: dve.wait_ge(x_in[1], 32), ln_step, ln_var, LN_STEPS)
            for i in range(2):
                w_part(i)
            inverse(1, ln_step, ln_var, ln_sd, LN_STEPS)
            xn_tiles(range(5, T))
            dve.wait_ge(ed_turned, 1)
            for s in range(2):
                dve.tensor_copy(keys[:, s, :], ps[:, 7 - s, 0:PAIRS]).then_inc(pj_free, 1)
            dve.wait_ge(pj_free, FREE0)
            for s in range(2):
                dve.memset(kf[:, s, N:NPAD], 0.0).then_inc(kf_zero, 1)
                dve.memset(ps[:, AB + s, :], 0.0).then_inc(cnt_free, 1)
                dve.memset(ohb[:, s * WCH, :], 0.0).then_inc(cnt_win, 1)
            dve.memset(vioh, 0.0).then_inc(keys_ok, 1)
            dve.memset(ohp, 0.0).then_inc(oh_zero, 1)
            for i in range(2, 4):
                w_part(i)
            dve.wait_ge(keys_ok, 1)
            dve.tensor_tensor(vioh[:, 0:1], viosum[:, 0:1], viosum[:, 1:2], ALU.max).then_inc(keys_ok, 1)
            dve.wait_ge(wg_hi, 1)
            dve.scalar_tensor_tensor(wgs[:, :, 1, :], wgf, WS, wgs[:, :, 0, :], ALU.mult, ALU.subtract).then_inc(wg_lo, 1)

            def one_hots(q):
                for h in range(2):
                    dve.wait_ge(cnt_win, 2 * q + h + 1)
                    for k in range(WCH):
                        col = (2 * q + h) * WCH + k
                        dve.tensor_scalar(ohb[:, h * WCH + k, :], csh[:, H_IOTA:H_IOTA + P],
                                          keys[:, 1, bass.ds(col, 1)], None, ALU.is_equal)
                        d = dve.tensor_scalar(ohk[:, h * WCH + k, :], csh[:, H_IOTA:H_IOTA + KEYS],
                                              keys[:, 0, bass.ds(col, 1)], None, ALU.is_equal)
                    d.then_inc(oh_ok, 1)

            with dve.Fori(0, K4 // 2) as i:
                for r in range(2):
                    m = 2 * i + r
                    q = 2 * AK * i + AK * r
                    one_hots(q)
                    for c, (n0, n) in enumerate(CH):
                        dve.wait_ge(pj_done, NCH * m + c + 1)
                        dve.tensor_scalar(kf[:, r, n0:n0 + n], ps[:, PB + 1 + c, 0:n], 1 / WS, bias[:, bass.ds(B_K + m, 1)],
                                          ALU.mult, ALU.add).then_inc(pj_free, 1)
                        if c < NCH - 1:
                            one_hots(q + c + 1)
                    dve.wait_ge(pj_free, FREE0 + NCH * m + NCH)
                    dve.tensor_reduce(kmax[:, bass.ds(m, 1)], kf[:, r, 0:N], AX.X, ALU.max, negate=True).then_inc(k_max, 1)
                    one_hots(q + NCH)
                    dve.wait_ge(k_exp, m + 1)
                    dve.reciprocal(krec[:, bass.ds(m, 1)], ksum[:, bass.ds(m, 1)]).then_inc(k_rec, 1)
                    for b, (t0, nt) in enumerate(ETB):
                        dve.wait_ge(tr_hi, T_E + NCH * m + b + 1)
                        dve.scalar_tensor_tensor(e_nat[1][:, t0:t0 + nt, bass.ds(m * P, P)],
                                                 ps[:, TB + (NCH * r + b) % 2, 0:nt * P].rearrange("p (t n) -> p t n", t=nt), KS,
                                                 e_nat[0][:, t0:t0 + nt, bass.ds(m * P, P)], ALU.mult, ALU.subtract).then_inc(tr_free, 1)

            CQ = K4 * AK

            def q_first(t, s):
                dve.wait_ge(pj_done, J_Q + t + 1)
                dve.scalar_tensor_tensor(qf[:, s, :], ps[:, PB + 1 + s, :], 1 / WS, bc[:, R_BQ:R_BQ + D],
                                         ALU.mult, ALU.add).then_inc(pj_free, 1)
                dve.wait_ge(pj_free, FREE0 + J_Q + t + 1)
                dve.tensor_reduce(qmax[:, s, :], qf[:, s, :].rearrange("p (h n) -> p h n", h=HEADS), AX.X, ALU.max,
                                  negate=True).then_inc(q_max, 1)

            def q_second(t, s):
                dve.wait_ge(q_exp, t + 1)
                dve.tensor_reduce(qsum[:, s, :], qf[:, s, :].rearrange("p (h n) -> p h n", h=HEADS), AX.X, ALU.add).then_inc(q_sum, 1)
                dve.wait_ge(q_sum, t + 1)
                dve.reciprocal(qrec[:, s, :], qsum[:, s, :]).then_inc(q_rec, 1)

            def q_turned(t, s):
                dve.wait_ge(tr_hi, T_Q + t + 1)
                dve.tensor_tensor(qt[1][:, :, bass.ds(t * P, P)], ps[:, TB + s, :].rearrange("p (k n) -> p k n", k=K4),
                                  qt[0][:, :, bass.ds(t * P, P)], ALU.subtract).then_inc(tr_free, 1)

            dve.wait_ge(fill_out, 16)
            for s in range(2):
                one_hots(CQ + s)
                q_first(s, s)
                q_second(s, s)
            with dve.Fori(1, T // 2) as i:
                for s in range(2):
                    one_hots(CQ + 2 * i + s)
                    q_turned(2 * i + s - 2, s)
                    q_first(2 * i + s, s)
                    q_second(2 * i + s, s)
            one_hots(WPAIRS - 1)
            q_turned(T - 2, 0)
            q_turned(T - 1, 1)

            dve.wait_ge(ed_viotot, 1)
            dve.tensor_scalar(flag[0:1, :], ps[0:1, PB, 0:1], 1.0, None, ALU.min).then_inc(flag_ok, 1)
            dve.wait_ge(flag_ok, 1)
            general = dve.value_load(flag[0:1, 0:1], min_val=0, max_val=1)
            with dve.If(general > 0):
                dve.memset(ohb[:, 0, :], 0.0).then_inc(gen_mm, 1)
                dve.memset(ps[:, AB, :], 0.0).then_inc(gen_ev, 1)
                dve.wait_ge(gen_mm, 1)
                dve.wait_ge(gen_in, 16)
                dve.tensor_scalar(ge_t[:, 0, :], ge_i[:, 0, :], 7, None, ALU.logical_shift_right).then_inc(gen_step, 1)
                dve.tensor_scalar(ge_t[:, 1, :], ge_i[:, 0, :], P - 1, None, ALU.bitwise_and).then_inc(gen_step, 1)
                dve.wait_ge(gen_step, 2)
                dve.scalar_tensor_tensor(ge_k, ge_i[:, 1, :], float(T), ge_t[:, 0, :], ALU.mult, ALU.add).then_inc(gen_step, 1)
                dve.tensor_copy(ge_b, ge_t[:, 1, :]).then_inc(gen_step, 1)
                dve.wait_ge(gen_step, 4)
                dve.tensor_copy(ge_w, ge_k).then_inc(gen_step, 1)
                with dve.Fori(0, WINDOWS) as w:
                    with dve.Fori(0, EC) as c:
                        dve.wait_ge(gen_step, w + 5)
                        dve.wait_ge(gen_mm, w * EC + c + 1)
                        dve.tensor_scalar(ohb[:, 0, :], csh[:, H_IOTA:H_IOTA + P], ge_b[:, bass.ds(c, 1)], None, ALU.is_equal)
                        dve.tensor_scalar(ohk[:, 0, :], csh[:, H_IOTA:H_IOTA + KEYS], ge_w[:, bass.ds(c, 1)], None,
                                          ALU.is_equal).then_inc(gen_oh, 1)
                    dve.wait_ge(gen_oh, w * EC + EC)
                    dve.tensor_scalar(ge_w, ge_w, float(KEYS), None, ALU.subtract).then_inc(gen_step, 1)
                dve.wait_ge(gen_ev, WINDOWS + 1)

            dve.wait_ge(cnt_free, 2 + WPAIRS)
            for a in range(T):
                dve.tensor_tensor(at[:, a, a * P:(a + 1) * P], at[:, a, a * P:(a + 1) * P], ident, ALU.add).then_inc(at_ok, 1)
            for i in range(4, 8):
                w_part(i)
            with dve.Fori(0, K4) as m:
                for c, (n0, n) in enumerate(CH):
                    dve.wait_ge(pj_hi, NCH * m + c + 1)
                    dve.scalar_tensor_tensor(xt[1][:, bass.ds(m, 1), n0:n0 + n].rearrange("p o n -> p (o n)"), ps[:, PB + 1 + c, 0:n], HS,
                                             xt[0][:, bass.ds(m, 1), n0:n0 + n].rearrange("p o n -> p (o n)"),
                                             ALU.mult, ALU.subtract).then_inc(pj_free, 1)
            for i in range(8, WHALVES):
                w_part(i)
            for m in range(K4):
                dve.wait_ge(pj_hi, NCH * K4 + m + 1)
                dve.scalar_tensor_tensor(gt[1][:, m, :], ps[:, PB + m, :], 1 / KS, gt[0][:, m, :], ALU.mult, ALU.subtract).then_inc(pj_free, 1)
            dve.wait_ge(pj_done, J_C)
            for i in range(2):
                dve.memset(rt[i][:, :, N:NPAD], 0.0).then_inc(pads_ok, 1)
            dve.wait_ge(pj_done, J_C + 1)
            for h in range(2):
                r = slice(h * DH, (h + 1) * DH)
                d = dve.scalar_tensor_tensor(ctxf[r, :, r], ps[r, PB, :].rearrange("p (k n) -> p k n", k=K4)[:, :, r], 1 / WS,
                                             bc[r, R_BV:R_BV + D].rearrange("p (k n) -> p k n", k=K4)[:, :, r], ALU.mult, ALU.add)
                d.then_inc(ct_f, 1)
            dve.wait_ge(ct_f, 2)
            dve.memset(nwt[:, 0:1], 0.0).then_inc(pj_free, 1)
            dve.wait_ge(ct_hi, 2)
            for h in range(2):
                r = slice(h * DH, (h + 1) * DH)
                d = dve.tensor_tensor(ctxt[1][r, :, r], ctxf[r, :, r], ctxt[0][r, :, r], ALU.subtract)
            d.then_inc(ct_lo, 1)
            J1H = NCH * K4 + K4
            lin = qf.rearrange("p s n -> p (s n)")
            dve.wait_ge(tr_free, T_F)
            dve.memset(lin[:, 0:1], 0.0).then_inc(r_lo, 1)

            def expert_part(h, s):
                dve.wait_ge(w_hi, WHALVES + h + 1)
                dve.scalar_tensor_tensor(ffh[:, bass.ds(h, 1), 1, :].rearrange("p o n -> p (o n)"), stage[:, s, :], WS,
                                         ffh[:, bass.ds(h, 1), 0, :].rearrange("p o n -> p (o n)"), ALU.mult, ALU.subtract).then_inc(w_lo, 1)

            with dve.Fori(0, K4 // 2) as i:
                for r in range(2):
                    m = 2 * i + r
                    for c, (n0, n) in enumerate(CH):
                        hi = rt[0][:, bass.ds(m, 1), n0:n0 + n].rearrange("p o n -> p (o n)")
                        lo = rt[1][:, bass.ds(m, 1), n0:n0 + n].rearrange("p o n -> p (o n)")
                        dve.wait_ge(pj_hi, J1H + NCH * m + c + 1)
                        dve.wait_ge(r_lo, NCH * m + c + 1)
                        dve.tensor_scalar(lin[:, 0:n], ps[:, PB + 1 + c, 0:n], 1 / WS, b1s[:, bass.ds(m, 1)],
                                          ALU.mult, ALU.add).then_inc(pj_free, 1)
                        dve.wait_ge(pj_free, FREE0 + J_1 + NCH * m + c + 1)
                        dve.scalar_tensor_tensor(lo, lin[:, 0:n], 0.0, hi, ALU.max, ALU.subtract).then_inc(r_lo, 1)
                        expert_part(2 * NCH * i + NCH * r + c, (NCH * r + c) % 2)
            dve.tensor_copy(X[:, :, D + 3].bitcast(I32), cst[:, C_TOK:C_TOK + T]).then_inc(tok_ok, 1)
            dve.tensor_scalar(valid, cst[:, C_TOK:C_TOK + T], float(N), None, ALU.is_lt).then_inc(tok_ok, 1)
            for t in range(T):
                if t == 0:
                    dve.wait_ge(xb_ok, T)
                dve.wait_ge(pj_done, J_2 + t + 1)
                dve.scalar_tensor_tensor(X[:, t, 0:D], ps[:, PB + 1 + t % 2, :], HS, X[:, t, 0:D], ALU.mult, ALU.add).then_inc(pj_free, 1)
                if NCH * K4 + t < 2 * NE:
                    expert_part(NCH * K4 + t, (NCH * K4 + t) % 2)
            for g in range(2):
                statistics(g, lambda t: dve.wait_ge(pj_free, FREE0 + J_2 + t + 1), l2_step, l2_var, g * LN_STEPS)
                inverse(g, l2_step, l2_var, l2_sd, g * LN_STEPS)
                for t in range(5 * g, 5 * g + 5):
                    if t >= 2:
                        dve.wait_ge(tr_done, T_F + t - 1)
                    dve.tensor_scalar(qf[:, t % 2, :], X[:, t, 0:D], mv[:, t, 0:1], rstd[:, t:t + 1], ALU.subtract, ALU.mult).then_inc(xf_ok, 1)
                    dve.wait_ge(tr_hi, T_F + t + 1)
                    dve.tensor_tensor(xft[t % 2][1], ps[:, TB + t % 2, :].rearrange("p (k n) -> p k n", k=K4), xft[t % 2][0],
                                      ALU.subtract).then_inc(tr_free, 1)
                    dve.wait_ge(tr_free, T_F + t + 1)
                    dve.tensor_copy(X[:, t, D + 1:D + 2], rstd[:, t:t + 1]).then_inc(xg_ok, 1)
            dve.tensor_copy(X[:, :, D], mv[:, :, 0]).then_inc(tok_ok, 1)

            def step(n):
                dve.wait_ge(g_step, n)

            dve.wait_ge(gate_done, T)
            gp = ps[:, AB + 1, 0:2 * T * NE].rearrange("p (t s e) -> p t s e", t=T, s=2)
            bge = [P, T, NE]
            dve.tensor_scalar(rk, gp[:, :, 0, :], 1 / WS, None, ALU.mult).then_inc(g_step, 1)
            step(1)
            dve.scalar_tensor_tensor(lg, gp[:, :, 1, :], 1 / WS, rk, ALU.mult, ALU.add).then_inc(g_step, 1)
            step(2)
            dve.tensor_tensor(lg, lg, bc[:, R_BG:R_BG + NE].unsqueeze(1).to_broadcast(bge), ALU.add).then_inc(g_step, 1)
            step(3)
            dve.tensor_reduce(lmax, lg, AX.X, ALU.max).then_inc(g_step, 1)
            step(4)
            dve.tensor_tensor(le, lg, lmax.unsqueeze(2).to_broadcast(bge), ALU.subtract).then_inc(g_step, 1)
            dve.tensor_tensor(oh, lg, lmax.unsqueeze(2).to_broadcast(bge), ALU.is_equal).then_inc(g_step, 1)
            step(6)
            dve.tensor_tensor(oh, oh, cst[:, C_J:C_J + NE].unsqueeze(1).to_broadcast(bge), ALU.mult).then_inc(g_step, 1)
            step(7)
            dve.tensor_reduce(lpick, oh, AX.X, ALU.max).then_inc(g_step, 1)
            step(8)
            dve.tensor_tensor(oh, oh, lpick.unsqueeze(2).to_broadcast(bge), ALU.is_equal).then_inc(g_step, 1)
            step(9)
            dve.wait_ge(oh_zero, 1)
            dve.tensor_tensor(ohh, oh, valid.unsqueeze(2).to_broadcast(bge), ALU.mult).then_inc(g_step, 1)
            dve.wait_ge(g_exp, 1)
            dve.tensor_reduce(lsum, le, AX.X, ALU.add).then_inc(g_step, 1)
            step(11)
            dve.reciprocal(X[:, :, D + 2], lsum).then_inc(g_step, 1)
            dve.wait_ge(rank_done, 1)
            dve.tensor_scalar(ne_i, ps[:, PB + 3, 0:NE], float(P - 1), None, ALU.add).then_inc(g_step, 1)
            step(13)
            dve.tensor_scalar(ne_i, ne_i, 7, None, ALU.logical_shift_right).then_inc(g_step, 1)
            step(14)
            dve.tensor_copy(tiles, ne_i).then_inc(g_step, 1)
            step(15)
            dve.tensor_tensor(tri_p, cst[:, C_TRI:C_TRI + NE * NE].rearrange("p (a b) -> p a b", a=NE),
                              tiles.unsqueeze(1).to_broadcast([P, NE, NE]), ALU.mult).then_inc(g_step, 1)
            step(16)
            dve.tensor_reduce(base, tri_p, AX.X, ALU.add).then_inc(g_step, 1)
            step(17)
            dve.scalar_tensor_tensor(rk, base.unsqueeze(1).to_broadcast(bge), float(P),
                                     ps[:, AB, 0:T * NE].rearrange("p (t e) -> p t e", t=T), ALU.mult, ALU.add).then_inc(g_step, 1)
            step(18)
            dve.tensor_tensor(rk, rk, oh, ALU.mult).then_inc(g_step, 1)
            step(19)
            dve.tensor_reduce(lpick, rk, AX.X, ALU.add).then_inc(g_step, 1)
            step(20)
            dve.tensor_copy(slot_i, lpick).then_inc(slot_ok, 1)
            dve.tensor_tensor(ends, base, tiles, ALU.add).then_inc(g_step, 1)
            step(21)
            dve.tensor_tensor(tile_p, cst[:, C_TILE:C_TILE + ET * NE].rearrange("p (j e) -> p j e", j=ET),
                              ends.unsqueeze(1).to_broadcast([P, ET, NE]), ALU.is_ge).then_inc(g_step, 1)
            step(22)
            dve.tensor_reduce(texp_f, tile_p, AX.X, ALU.add).then_inc(g_step, 1)
            step(23)
            dve.tensor_scalar(texp, texp_f, float(NE - 1), None, ALU.min).then_inc(texp_ok, 1)

            def rows_f(j, i, s):
                dve.wait_ge(row_in[s], 16 * i + 16)
                dve.tensor_scalar(xff[:, s, :], rb[:, bass.ds(j, 1), 0:D].rearrange("p o n -> p (o n)"),
                                  rb[:, bass.ds(j, 1), D], rb[:, bass.ds(j, 1), D + 1], ALU.subtract, ALU.mult).then_inc(f_x, 1)

            def turned_f(j, s):
                dve.wait_ge(f_hi, j + 1)
                dve.tensor_tensor(xft[s][1], ps[:, TB + s, :].rearrange("p (k n) -> p k n", k=K4), xft[s][0], ALU.subtract).then_inc(f_xt, 1)

            def relu_f(j, s):
                e = dve.value_load(texp[0:1, bass.ds(j, 1)], min_val=0, max_val=NE - 1)
                dve.wait_ge(f_hr, 2 * j + 2)
                for m in range(2):
                    dve.tensor_scalar(hidf[:, s, m * P:(m + 1) * P], ps[:, AB + s, m * P:(m + 1) * P], 1 / WS,
                                      bias[:, bass.ds(B_F1 + 2 * e + m, 1)], ALU.mult, ALU.add).then_inc(f_hf, 1)
                dve.wait_ge(f_hf, 2 * j + 2)
                dve.scalar_tensor_tensor(hid[s][1].rearrange("p m n -> p (m n)"), hidf[:, s, :], 0.0,
                                         hid[s][0].rearrange("p m n -> p (m n)"), ALU.max, ALU.subtract).then_inc(f_hl, 1)

            def rows_out(j, i, s, first=False):
                e = dve.value_load(texp[0:1, bass.ds(j, 1)], min_val=0, max_val=NE - 1)
                if not first:
                    dve.wait_ge(out_done[s], 16 * i)
                dve.tensor_copy(tokc[:, s:s + 1], rb[:, bass.ds(j, 1), D + 3].bitcast(I32)).then_inc(f_tok, 1)
                dve.wait_ge(f_y, j + 1)
                dve.scalar_tensor_tensor(yf[:, s, :], ps[:, PB + s, :], 1 / WS, b2b[:, bass.ds(e * D, D)], ALU.mult, ALU.add).then_inc(f_yb, 1)
                dve.wait_ge(f_yb, j + 1)
                dve.wait_ge(f_tok, j + 1)
                dve.scalar_tensor_tensor(yf[:, s, :], yf[:, s, :], rb[:, bass.ds(j, 1), D + 2],
                                         rb[:, bass.ds(j, 1), 0:D].rearrange("p o n -> p (o n)"), ALU.mult, ALU.add).then_inc(f_out, 1)

            dve.wait_ge(texp_ok, 1)
            dve.wait_ge(b2f_in, 16)
            rows_f(0, 0, 0)
            rows_f(1, 0, 1)
            turned_f(0, 0)
            turned_f(1, 1)
            relu_f(0, 0)

            def two_tiles(i, first):
                for s in range(2):
                    rows_f(2 * i + s + 2, i + 1, s)
                    turned_f(2 * i + s + 2, s)
                    relu_f(2 * i + s + 1, 1 - s)
                    rows_out(2 * i + s, i, s, first)

            two_tiles(0, True)
            with dve.Fori(1, (ET - 3) // 2) as i:
                two_tiles(i, False)
            H = ET // 2
            rows_f(ET - 1, H, 0)
            turned_f(ET - 1, 0)
            relu_f(ET - 2, 1)
            rows_out(ET - 3, H - 1, 0)
            relu_f(ET - 1, 0)
            rows_out(ET - 2, H - 1, 1)
            rows_out(ET - 1, H, 0)


def kernel(x, src, dst, L0_gnn_W1, L0_gnn_b1, L0_gnn_W2, L0_gnn_b2, L0_mix_Wq, L0_mix_bq, L0_mix_Wk, L0_mix_bk,
           L0_mix_Wv, L0_mix_bv, L0_ffn_Wg, L0_ffn_bg, L0_ffn_W1, L0_ffn_b1, L0_ffn_W2, L0_ffn_b2):
    from concourse import bacc
    from concourse.bass_utils import run_bass_kernel_spmd

    src, dst = np.asarray(src), np.asarray(dst)
    table = np.zeros((ECP, 2, P), np.int32)
    table[:, 1, :] = PAD_DST
    flat = np.zeros((2, ECP * P), np.int32)
    flat[1] = PAD_DST
    flat[0, :EDGES], flat[1, :EDGES] = src, dst
    table = np.ascontiguousarray(flat.reshape(2, ECP, P).transpose(1, 0, 2)).reshape(ECP, 2 * P)
    columns = np.ascontiguousarray(flat[:, :ECF * P].reshape(2, ECF, P).transpose(2, 0, 1))
    cf, ch = constants()
    arrays = {
        "x": x, "edges": table, "edge_cols": columns,
        "wk": np.ascontiguousarray(np.asarray(L0_mix_Wk).T), "wq": np.ascontiguousarray(np.asarray(L0_mix_Wq).T),
        "wv": np.ascontiguousarray(np.asarray(L0_mix_Wv).T), "g1": L0_gnn_W1, "g2": L0_gnn_W2,
        "w1": np.asarray(L0_ffn_W1).reshape(NE * D, HID), "w2": np.asarray(L0_ffn_W2).reshape(NE * HID, D), "wg": L0_ffn_Wg,
        "rows": np.concatenate([np.asarray(v) for v in (L0_mix_bq, L0_mix_bv, L0_gnn_b2, L0_ffn_bg)]),
        "b2f": np.asarray(L0_ffn_b2).reshape(-1),
        "cols": np.ascontiguousarray(np.concatenate([np.asarray(L0_mix_bk), np.asarray(L0_gnn_b1),
                                                     np.asarray(L0_ffn_b1).reshape(-1)]).reshape(-1, P).T),
        "cf": cf, "ch": ch,
    }
    nc = bacc.Bacc("TRN2", target_bir_lowering=False, num_devices=1)
    aps = {}
    for name, a in arrays.items():
        arrays[name] = a = np.ascontiguousarray(a)
        aps[name] = nc.dram_tensor(name, a.shape, mybir.dt.from_np(a.dtype), kind="ExternalInput").ap()
    out = nc.dram_tensor("out", (N, D), F32, kind="ExternalOutput").ap()
    build(nc, out=out, **aps)
    r = run_bass_kernel_spmd(nc, [arrays], core_ids=[0])
    return r.results[0]["out"]
```

```python
from contextlib import ExitStack

import numpy as np

import concourse.bass as bass
from concourse import mybir

ALU = mybir.AluOpType
ACT = mybir.ActivationFunctionType
AX = mybir.AxisListType
F32 = mybir.dt.float32
F16 = mybir.dt.float16
I32 = mybir.dt.int32

P = 128
N, D = 1250, 512
T = -(-N // P)
NPAD = T * P
LAST = N - (T - 1) * P
K4 = D // P
HEADS, DH = 8, 64
CH = ((0, 420), (420, 420), (840, 410))
NCH = len(CH)

EDGES = 20000
EC = -(-EDGES // P)
ECP = 256
ECF = 160
WN = 24
KEYS = WN * T
WINDOWS = 54
WCH = 5
PAIRS = WINDOWS * WCH
GATHERS = 3
PG = PAIRS // GATHERS
ATW = WINDOWS * WN
PAD_DST = ATW
WPAIRS = WINDOWS // 2

NE, HID = 8, 256
ET = (N + NE * (P - 1)) // P
SLOTS = ET * P
ROW = D + 4
NO_TOKEN = 1 << 20

WS = 64.0
HS = 0.125
KS = 4096.0
EPS = 1e-5

C_ID, C_THR = 0, P
C_K = C_THR + PAIRS
C_WK = C_K + GATHERS
C_C = C_WK + GATHERS
C_J = C_C + 2
C_TRI = C_J + NE
C_TILE = C_TRI + NE * NE
C_TOK = C_TILE + ET * NE
C_ALL = C_TOK + T
H_IOTA, H_TRI, H_ONE = 0, KEYS, KEYS + P
H_ALL = KEYS + 2 * P
R_BQ, R_BV, R_B2, R_BG = 0, D, 2 * D, 3 * D
R_ALL = 3 * D + NE
B_K, B_G1, B_F1 = 0, K4, 2 * K4
B_ALL = 2 * K4 + 2 * NE


def constants():
    f = np.zeros((P, C_ALL), np.float32)
    p = np.arange(P)
    f[:, C_ID:C_ID + P] = np.eye(P)
    pair = np.arange(PAIRS)
    f[:, C_THR:C_THR + PAIRS] = (pair // WCH) * WN
    for g in range(GATHERS):
        q = g * PG + np.minimum(p, PG - 1)
        f[:, C_K + g] = q % WCH
        f[:, C_WK + g] = (q // WCH) * KEYS
    for g in range(2):
        f[:, C_C + g] = g * P + p
    f[:, C_J:C_J + NE] = NE - np.arange(NE)
    f[:, C_TRI:C_TRI + NE * NE] = (np.arange(NE)[None, :] < np.arange(NE)[:, None]).reshape(-1)
    f[:, C_TILE:C_TILE + ET * NE] = np.repeat(np.arange(ET), NE)
    f[:, C_TOK:C_TOK + T] = np.arange(T)[None, :] * P + p[:, None]
    h = np.zeros((P, H_ALL), np.float16)
    h[:, H_IOTA:H_IOTA + KEYS] = np.arange(KEYS)
    h[:, H_TRI:H_TRI + P] = p[:, None] < p[None, :]
    h[:, H_ONE:H_ONE + P] = 1
    return f, h


def build(nc, x, edges, edge_cols, wk, wq, wv, g1, g2, w1, w2, wg, rows, b2f, cols, cf, ch, out):
    ctx = ExitStack()
    with ctx:
        def sb(name, shape, dt=F32):
            return ctx.enter_context(nc.sbuf_tensor(name, shape, dt))

        def sem(name):
            return ctx.enter_context(nc.semaphore(name))

        slot_rows = nc.dram_tensor("slot_rows", (SLOTS, ROW), F32, kind="Internal").ap()

        AT_W, E_W, KF_W, XT_W = ATW * T // 2, T * D, 2 * NPAD, K4 * NPAD
        one = sb("one", [P, AT_W + E_W + KF_W + XT_W])
        two = sb("two", [P, 2 * XT_W])

        def halves(region, start, words, pattern, **dims):
            w = words // 2
            return [region[:, start + i * w:start + (i + 1) * w].bitcast(F16).rearrange(pattern, **dims)
                    for i in range(2)]

        at = one[:, 0:AT_W].bitcast(F16).rearrange("p (a d) -> p a d", a=T)
        e_nat = halves(one, AT_W, E_W, "p (t n) -> p t n", t=T)
        kf = one[:, AT_W + E_W:AT_W + E_W + KF_W].rearrange("p (r n) -> p r n", r=2)
        gt = halves(one, AT_W + E_W, K4 * D, "p (k n) -> p k n", k=K4)
        xt = halves(one, AT_W + E_W + KF_W, XT_W, "p (k n) -> p k n", k=K4)
        ctxf = one[:, AT_W + E_W + K4 * D:AT_W + E_W + K4 * D + D].rearrange("p (k n) -> p k n", k=K4)
        ffw = one[:, 0:NE * 2048].bitcast(F16).rearrange("p (e s n) -> p e s n", e=NE, s=4)
        ffh = one[:, 0:NE * 2048].bitcast(F16).rearrange("p (e s n) -> p e s n", e=2 * NE, s=2)
        tail = one[:, NE * 2048:NE * 2048 + 2560]
        xft = [halves(tail, s * 512, 512, "p (k n) -> p k n", k=K4) for s in range(2)]
        hidf = tail[:, 1024:1536].rearrange("p (s n) -> p s n", s=2)
        hid = [halves(tail, 1536 + s * 256, 256, "p (m n) -> p m n", m=2) for s in range(2)]
        xn = halves(two, 0, XT_W, "p (t n) -> p t n", t=T)
        rt = halves(two, 0, XT_W, "p (k n) -> p k n", k=K4)
        xnf = two[:, XT_W:2 * XT_W].rearrange("p (t n) -> p t n", t=T)
        qt = halves(two, XT_W, XT_W, "p (k n) -> p k n", k=K4)
        rb = two[:, 0:ET * ROW].rearrange("p (t n) -> p t n", t=ET)
        xff = two[:, ET * ROW:ET * ROW + 2 * D].rearrange("p (s n) -> p s n", s=2)

        X = sb("X", [P, T, ROW])
        wt = sb("wt", [P, 4, 2, K4, D], F16)
        b2b = wt[:, 1:3].rearrange("p w s k n -> p (w s k n)").bitcast(F32)
        stage = sb("stage", [P, 2, 1024])
        ohb = sb("ohb", [P, 2 * WCH, P], F16)
        ohk = sb("ohk", [P, 2 * WCH, KEYS], F16)
        keys = sb("keys", [P, 2, PAIRS, 2], F16)
        bc = sb("bc", [P, R_ALL])
        bias = sb("bias", [P, B_ALL])
        b1s = sb("b1s", [P, K4])
        qf = sb("qf", [P, 2, D])
        yf = qf
        ctxt = [sb(f"ctxt{i}", [P, K4, P], F16) for i in range(2)]
        cst = sb("cst", [P, C_ALL])
        csh = sb("csh", [P, H_ALL], F16)
        ident = cst[:, C_ID:C_ID + P]
        onesh = csh[:, H_ONE:H_ONE + P]
        small = sb("small", [P, 1016])
        used = [0]

        def sm(n, dt=F32):
            a = small[:, used[0]:used[0] + n]
            used[0] += n
            assert used[0] <= 1016, used
            return a if dt == F32 else a.bitcast(dt)

        def sm2(a, b, dt=F32):
            return sm(a * b, dt).rearrange("p (a b) -> p a b", a=a)

        ps = ctx.enter_context(nc.psum_tensor("ps", [P, 8, 512], F32))
        TB, AB, PB = 0, 2, 4

        stats, mv = sm2(T, 6), sm2(T, 2)
        vpe, sd, rstd, nwt = (sm(T) for _ in range(4))
        scr = one
        etab = scr[:, 0:256].bitcast(I32).rearrange("p (g n) -> p g n", g=2)
        got = [scr[0:PG, 256 * (g + 1):256 * (g + 2)].bitcast(I32) for g in range(GATHERS)]
        g_a = [scr[0:PG, 1024 + P * g:1024 + P * (g + 1)].bitcast(I32) for g in range(GATHERS)]
        g_b = [scr[0:PG, 1408 + P * g:1408 + P * (g + 1)].bitcast(I32) for g in range(GATHERS)]
        g_key = [scr[0:PG, 1792 + P * g:1792 + P * (g + 1)] for g in range(GATHERS)]
        g_bf = [scr[0:PG, 2176 + P * g:2176 + P * (g + 1)] for g in range(GATHERS)]
        before = scr[:, 2560:2560 + PAIRS].bitcast(F16).rearrange("p (g n) -> p g n", g=2)
        vio = [scr[:, 2900 + WINDOWS * i:2900 + WINDOWS * (i + 1)] for i in range(7)]
        emax, emin = sm(2), sm(2)
        pidx = sm(GATHERS, I32)
        viosum, vioh = sm(2), sm(1).bitcast(F16)
        flag = sm(1, I32)
        gen = qf.rearrange("p s n -> p (s n)")
        ge_i = gen[:, 0:2 * ECF].bitcast(I32).rearrange("p (s n) -> p s n", s=2)
        ge_t = gen[:, 2 * ECF:4 * ECF].bitcast(I32).rearrange("p (s n) -> p s n", s=2)
        ge_b = gen[:, 4 * ECF:5 * ECF]
        ge_w = gen[:, 5 * ECF:6 * ECF]
        kmax, ksum, krec = sm(K4), sm(K4), sm(K4)
        qmax, qsum, qrec = sm2(2, HEADS), sm2(2, HEADS), sm2(2, HEADS)
        wgf = sm2(K4, NE)
        wgs = sm(K4 * NE).bitcast(F16).rearrange("p (k s e) -> p k s e", k=K4, s=2)
        lgle = sm(2 * T * NE)
        lg, le = (lgle[:, i * T * NE:(i + 1) * T * NE].rearrange("p (t e) -> p t e", t=T) for i in range(2))
        oh, rk = sm2(T, NE), sm2(T, NE)
        ohp = sm((2 * T - 1) * NE // 2).bitcast(F16)
        ohh = ohp[:, (T - 1) * NE:].rearrange("p (t e) -> p t e", t=T)
        valid, lmax, lsum, lpick = sm(T), sm(T), sm(T), sm(T)
        slot_i = sm(T, I32)
        ne_i, tiles, base, ends = sm(NE, I32), sm(NE), sm(NE), sm(NE)
        tri_p = rk.rearrange("p a b -> p (a b)")[:, 0:NE * NE].rearrange("p (a b) -> p a b", a=NE)
        tile_p = lgle[:, 0:ET * NE].rearrange("p (j e) -> p j e", j=ET)
        texp_f, texp = sm(ET), sm(ET, I32)
        tokc = sm(2, I32)
        fill = qf[:, :, :].rearrange("p s n -> p (s n)")[:, 0:ROW]

        def sems(names):
            return [sem(n) for n in names.split()]

        consts_in, etab_in, rows_in, wg_in, b2f_in, pad_zero = sems("consts_in etab_in rows_in wg_in b2f_in pad_zero")
        x_in, w_in, row_in, out_done = sems("x_in0 x_in1"), sems("w_in0 w_in1"), sems("row_in0 row_in1"), sems("out_done0 out_done1")
        w_hi, w_lo, wg_hi, wg_lo = sems("w_hi w_lo wg_hi wg_lo")
        ln_step, ln_var, ln_sd, xnf_ok, xnh_ok, xnl_ok = sems("ln_step ln_var ln_sd xnf_ok xnh_ok xnl_ok")
        tr_done, tr_hi, tr_free = sems("tr_done tr_hi tr_free")
        ed_range, ed_before, ed_count, ed_idx, ed_int, ed_key, ed_turned, ed_vio, ed_viotot = sems(
            "ed_range ed_before ed_count ed_idx ed_int ed_key ed_turned ed_vio ed_viotot")
        ed_got = sems("ed_got0 ed_got1 ed_got2")
        keys_ok, flag_ok, oh_zero = sems("keys_ok flag_ok oh_zero")
        oh_ok, cnt_win, cnt_free, at_ok = sems("oh_ok cnt_win cnt_free at_ok")
        gen_in, gen_step, gen_oh, gen_mm, gen_ev = sems("gen_in gen_step gen_oh gen_mm gen_ev")
        pj_done, pj_hi, pj_free = sems("pj_done pj_hi pj_free")
        kf_zero, k_max, k_exp, k_rec, k_norm = sems("kf_zero k_max k_exp k_rec k_norm")
        q_lin, q_max, q_sub, q_exp, q_sum, q_rec, q_norm = sems("q_lin q_max q_sub q_exp q_sum q_rec q_norm")
        xb_ok, ct_zero, ct_f, ct_hi, ct_lo, b1s_ok, r_lin, r_lo, pads_ok = sems(
            "xb_ok ct_zero ct_f ct_hi ct_lo b1s_ok r_lin r_lo pads_ok")
        l2_step, l2_var, l2_sd, xf_ok, gate_done, g_step, g_exp, rank_done = sems(
            "l2_step l2_var l2_sd xf_ok gate_done g_step g_exp rank_done")
        fill_ok, fill_out, tok_ok, slot_ok, sent, texp_ok = sems("fill_ok fill_out tok_ok slot_ok sent texp_ok")
        f_x, f_tr, f_hi, f_xt, f_h, f_hr, f_hf, f_hl, f_y, f_yb, f_tok, f_out = sems(
            "f_x f_tr f_hi f_xt f_h f_hr f_hf f_hl f_y f_yb f_tok f_out")

        J_K, J_Q = 0, NCH * K4
        J_G = J_Q + T
        J_C = J_G + K4
        J_A = J_C + 1
        J_1 = J_A + NCH * K4
        J_2 = J_1 + NCH * K4
        J_END = J_2 + T
        FREE0 = 3
        T_X, T_E = 0, T
        T_Q = T_E + NCH * K4
        T_F = T_Q + T
        ETB = ((0, 4), (4, 4), (8, 2))
        CK, CQ, CG = 0, NCH * K4, NCH * K4 + T
        assert CG + 5 == WPAIRS
        WHALVES = 10
        w_dram = [w.rearrange("(k p) n -> p k n", p=P) for w in (wk, wq, wv, g1, g2)]
        w_slot = (0, 1, 2, 3, 0)
        WK, WQ, WV, WG1, WG2 = w_slot
        LN_GROUPS = (range(0, 5), range(5, T))
        INV_STEPS = 5

        block = ctx.enter_context(nc.Block())

        @block.sync
        def _(sp):
            sp.dma_start(X[:, 0:5, 0:D], x[0:5 * P, :].rearrange("(t p) n -> p t n", p=P)).then_inc(x_in[0], 16)
            sp.dma_start(X[:, 5:9, 0:D], x[5 * P:9 * P, :].rearrange("(t p) n -> p t n", p=P)).then_inc(x_in[1], 16)
            sp.wait_ge(pad_zero, 1)
            sp.dma_start(X[0:LAST, T - 1, 0:D], x[(T - 1) * P:N, :]).then_inc(x_in[1], 16)
            for i in range(WHALVES):
                if i >= 2:
                    sp.wait_ge(w_lo, i - 1)
                sp.dma_start(stage[:, i % 2, :].rearrange("p (k n) -> p k n", k=2),
                             w_dram[i // 2][:, 2 * (i % 2):2 * (i % 2) + 2, :]).then_inc(w_in[i % 2], 16)
            with sp.Fori(0, NE) as e:
                sp.wait_ge(w_lo, WHALVES - 1 + 2 * e)
                sp.dma_start(stage[:, 0, :].rearrange("p (k n) -> p k n", k=K4),
                             w1[bass.ds(e * D, D), :].rearrange("(k p) n -> p k n", p=P)).then_inc(w_in[0], 16)
                sp.wait_ge(w_lo, WHALVES + 2 * e)
                sp.dma_start(stage[:, 1, :].rearrange("p (k n) -> p k n", k=2),
                             w2[bass.ds(e * HID, HID), :].rearrange("(k p) n -> p k n", p=P)).then_inc(w_in[1], 16)
            sp.wait_ge(pj_done, J_1)
            sp.dma_start(b2b, b2f.partition_broadcast(P)).then_inc(b2f_in, 16)
            sp.wait_ge(sent, 16 * T)
            sp.wait_ge(fill_out, 16)
            sp.wait_ge(pj_free, FREE0 + J_END)

            def slot_row(j, s):
                sp.dma_start(rb[:, bass.ds(j, 1), :].rearrange("p o n -> p (o n)"),
                             slot_rows[bass.ds(j * P, P), :]).then_inc(row_in[s], 16)

            slot_row(0, 0)
            slot_row(1, 1)
            with sp.Fori(1, ET // 2) as i:
                for s in range(2):
                    sp.wait_ge(row_in[s], 16 * i)
                    slot_row(2 * i + s, s)
            sp.wait_ge(row_in[0], 16 * (ET // 2))
            slot_row(ET - 1, 0)

        @block.gpsimd
        def _(pool):
            pool.memset(X[:, T - 1, :], 0.0).then_inc(pad_zero, 1)
            pool.memset(fill[:, 0:ROW - 1], 0.0).then_inc(fill_ok, 1)
            pool.memset(fill[:, ROW - 1:ROW].bitcast(I32), NO_TOKEN).then_inc(fill_ok, 1)
            pool.wait_ge(ed_idx, 1)
            for g in range(GATHERS):
                pool.indirect_dma_start(out=got[g], out_offset=None, in_=edges,
                                        in_offset=bass.IndirectOffsetOnAxis(ap=pidx[0:PG, g:g + 1], axis=0),
                                        bounds_check=ECP - 1, oob_is_err=False).then_inc(ed_got[g], 16)
            pool.wait_ge(fill_ok, 2)
            pool.dma_start(slot_rows.rearrange("(t p) n -> p t n", p=P),
                           fill.unsqueeze(1).to_broadcast([P, ET, ROW])).then_inc(fill_out, 16)
            for i in range(2):
                pool.memset(ctxt[i][:, :, :], 0.0).then_inc(ct_zero, 1)
            pool.wait_ge(rows_in, 32)
            pool.wait_ge(xnf_ok, T)
            for t in range(T):
                pool.tensor_tensor(X[:, t, 0:D], X[:, t, 0:D], bc[:, R_B2:R_B2 + D], ALU.add).then_inc(xb_ok, 1)

            def by_head(s):
                return qf[:, s, :].rearrange("p (h n) -> p h n", h=HEADS)

            with pool.Fori(0, T // 2) as i:
                for s in range(2):
                    pool.wait_ge(q_max, 2 * i + s + 1)
                    pool.tensor_tensor(by_head(s), by_head(s), qmax[:, s, :].unsqueeze(2).to_broadcast([P, HEADS, DH]),
                                       ALU.add).then_inc(q_sub, 1)
                    pool.wait_ge(q_rec, 2 * i + s + 1)
                    pool.tensor_tensor(by_head(s), by_head(s), qrec[:, s, :].unsqueeze(2).to_broadcast([P, HEADS, DH]),
                                       ALU.mult).then_inc(q_norm, 1)
            pool.wait_ge(slot_ok, 1)
            pool.wait_ge(tok_ok, 4)
            pool.wait_ge(fill_out, 16)
            for t in range(T):
                r = P if t < T - 1 else LAST
                pool.indirect_dma_start(out=slot_rows, out_offset=bass.IndirectOffsetOnAxis(ap=slot_i[0:r, t:t + 1], axis=0),
                                        in_=X[0:r, t, :], in_offset=None, bounds_check=SLOTS - 1, oob_is_err=False).then_inc(sent, 16)

            for j in range(ET):
                s = j % 2
                pool.wait_ge(f_out, j + 1)
                pool.indirect_dma_start(out=out, out_offset=bass.IndirectOffsetOnAxis(ap=tokc[:, s:s + 1], axis=0),
                                        in_=yf[:, s, :], in_offset=None, bounds_check=N - 1, oob_is_err=False).then_inc(out_done[s], 16)

            pool.wait_ge(out_done[0], 16 * (ET // 2 + 1))
            pool.wait_ge(out_done[1], 16 * (ET // 2))

        @block.tensor
        def _(pe):
            def three(o, lhs, rhs, start, stop):
                pe.matmul(o, lhs[0], rhs[0], start=start, stop=False)
                pe.matmul(o, lhs[0], rhs[1], start=False, stop=False)
                return pe.matmul(o, lhs[1], rhs[0], start=False, stop=stop)

            pe.wait_ge(consts_in, 32)
            pe.wait_ge(ed_before, 2)
            for g in range(GATHERS):
                for h in range(2):
                    pe.matmul(ps[0:PG, 5, g:g + 1], before[:, h, g * PG:(g + 1) * PG], onesh[:, 0:1], start=(h == 0), stop=(h == 1))
            for h in range(2):
                mm = pe.matmul(ps[:, 5, 64:64 + WINDOWS], onesh, before[:, h, 0:PAIRS:WCH], start=(h == 0), stop=(h == 1))
            mm.then_inc(ed_count, 1)

            def turn_x(t):
                pe.wait_ge(xnf_ok, t + 1)
                if t >= 2:
                    pe.wait_ge(tr_free, t - 1)
                for k in range(K4):
                    mm = pe.transpose(ps[:, TB + t % 2, k * P:(k + 1) * P], xnf[:, t, k * P:(k + 1) * P], ident)
                mm.then_inc(tr_done, 1)

            for t in range(5):
                turn_x(t)
            pe.wait_ge(ed_key, GATHERS)
            for g in range(GATHERS):
                pe.transpose(ps[:, 7, g * PG:(g + 1) * PG], g_key[g], ident[0:PG, 0:PG])
            for g in range(GATHERS):
                mm = pe.transpose(ps[:, 6, g * PG:(g + 1) * PG], g_bf[g], ident[0:PG, 0:PG])
            mm.then_inc(ed_turned, 1)
            for t in range(5, T):
                turn_x(t)

            def count_pair(q, b):
                pe.wait_ge(cnt_free, q + 1)
                for h in range(2):
                    pe.wait_ge(oh_ok, 2 * q + h + 1)
                    for k in range(WCH):
                        mm = pe.matmul(ps[:, AB + b, h * KEYS:(h + 1) * KEYS], ohb[:, h * WCH + k, :], ohk[:, h * WCH + k, :],
                                       start=(k == 0), stop=(k == WCH - 1))
                    mm.then_inc(cnt_win, 1)

            pe.wait_ge(keys_ok, 2)
            pe.wait_ge(pj_free, FREE0)
            pe.wait_ge(w_lo, 2)
            pe.wait_ge(tr_free, T)
            pe.matmul(ps[0:1, PB, 0:1], vioh[:, 0:1], onesh[:, 0:1], start=True, stop=True).then_inc(ed_viotot, 1)
            def turn_e(m, b):
                t0, nt = ETB[b]
                pe.wait_ge(k_norm, m + 1)
                pe.wait_ge(tr_free, T_E + NCH * m + b - 1)
                for t in range(nt):
                    mm = pe.transpose(ps[:, TB + (NCH * m + b) % 2, t * P:(t + 1) * P], kf[:, m % 2, (t0 + t) * P:(t0 + t + 1) * P], ident)
                mm.then_inc(tr_done, 1)

            for m in range(K4):
                for c, (n0, n) in enumerate(CH):
                    pe.wait_ge(pj_free, FREE0 + NCH * m + c - 2)
                    for k in range(K4):
                        mm = three(ps[:, PB + 1 + c, 0:n], [wt[:, WK, s, k, m * P:(m + 1) * P] for s in range(2)],
                                   [xt[s][:, k, n0:n0 + n] for s in range(2)], k == 0, k == K4 - 1)
                    mm.then_inc(pj_done, 1)
                    u = NCH * m + c
                    if u >= 1:
                        count_pair(u - 1, (u - 1) % 2)
                    if m >= 1 and c >= 1:
                        turn_e(m - 1, c - 1)
                        if c == 2:
                            turn_e(m - 1, 2)

            def q_rows(t, s):
                pe.wait_ge(pj_free, FREE0 + J_Q + t - 1)
                for k in range(K4):
                    lhs = [xt[h][:, k, bass.ds(t * P, P)] for h in range(2)]
                    mm = three(ps[:, PB + 1 + s, :], lhs, [wt[:, WQ, h, k, :] for h in range(2)], k == 0, k == K4 - 1)
                mm.then_inc(pj_done, 1)

            def turn_q(t, s):
                pe.wait_ge(q_norm, t + 1)
                pe.wait_ge(tr_free, T_Q + t - 1)
                for k in range(K4):
                    mm = pe.transpose(ps[:, TB + s, k * P:(k + 1) * P], qf[:, s, k * P:(k + 1) * P], ident)
                mm.then_inc(tr_done, 1)

            pe.wait_ge(w_lo, 4)
            q_rows(0, 0)
            count_pair(CQ - 1, (CQ - 1) % 2)
            turn_e(K4 - 1, 0)
            q_rows(1, 1)
            count_pair(CQ, CQ % 2)
            turn_e(K4 - 1, 1)
            turn_e(K4 - 1, 2)
            with pe.Fori(1, T // 2) as i:
                for s in range(2):
                    turn_q(2 * i + s - 2, s)
                    q_rows(2 * i + s, s)
                    count_pair(CQ + 2 * i + s - 1, (CQ + s - 1) % 2)

            def keys_xn(m, ts):
                for t in ts:
                    mm = three(ps[:, bass.ds(PB + m, 1), :].rearrange("p o n -> p (o n)"), [xn[s][:, t, bass.ds(m * P, P)] for s in range(2)],
                               [e_nat[s][:, t, :] for s in range(2)], t == 0, t == T - 1)
                return mm

            pe.wait_ge(xnl_ok, T)
            pe.wait_ge(tr_free, T_Q)
            pe.wait_ge(flag_ok, 1)
            pe.wait_ge(pj_free, FREE0 + J_Q + T - 1)
            keys_xn(0, range(T)).then_inc(pj_done, 1)
            turn_q(T - 2, 0)
            turn_q(T - 1, 1)
            pe.wait_ge(pj_free, FREE0 + J_G)
            with pe.Fori(1, K4) as m:
                keys_xn(m, range(T // 2))
                count_pair(CG - 3 + 2 * m, (CG - 1) % 2)
                keys_xn(m, range(T // 2, T)).then_inc(pj_done, 1)
                count_pair(CG - 2 + 2 * m, CG % 2)

            pe.wait_ge(w_lo, 6)
            pe.wait_ge(pj_free, FREE0 + J_C)
            for p in range(K4):
                for k in range(K4):
                    mm = three(ps[:, PB, p * P:(p + 1) * P], [gt[s][:, k, p * P:(p + 1) * P] for s in range(2)],
                               [wt[:, WV, s, k, p * P:(p + 1) * P] for s in range(2)], k == 0, k == K4 - 1)
            mm.then_inc(pj_done, 1)

            general = pe.value_load(flag[0:1, 0:1], min_val=0, max_val=1)
            with pe.If(general > 0):
                with pe.Fori(0, WINDOWS) as w:
                    pe.wait_ge(gen_ev, w + 1)

                    def count(c, start, stop):
                        pe.wait_ge(gen_oh, w * EC + c + 1)
                        pe.matmul(ps[:, AB, 0:KEYS], ohb[:, 0, :], ohk[:, 0, :], start=start, stop=stop).then_inc(gen_mm, 1)

                    count(0, True, False)
                    with pe.Fori(1, EC - 1) as c:
                        count(c, False, False)
                    count(EC - 1, False, True)

            pe.wait_ge(at_ok, T)
            with pe.Fori(0, K4) as m:
                for c, (n0, n) in enumerate(CH):
                    pe.wait_ge(pj_free, FREE0 + J_A + NCH * m + c - 1)
                    o = ps[:, PB + 1 + c, 0:n]
                    for a in range(T):
                        for s in range(2):
                            mm = pe.matmul(o, xn[s][:, a, bass.ds(m * P, P)], at[:, a, n0:n0 + n],
                                           start=(a == 0 and s == 0), stop=(a == T - 1 and s == 1))
                    mm.then_inc(pj_done, 1)

            pe.wait_ge(w_lo, 8)
            with pe.Fori(0, K4) as m:
                for c, (n0, n) in enumerate(CH):
                    pe.wait_ge(pj_free, FREE0 + J_1 + NCH * m + c - 1)
                    for k in range(K4):
                        mm = three(ps[:, PB + 1 + c, 0:n], [wt[:, WG1, s, k, bass.ds(m * P, P)] for s in range(2)],
                                   [xt[s][:, k, n0:n0 + n] for s in range(2)], k == 0, k == K4 - 1)
                    mm.then_inc(pj_done, 1)

            pe.wait_ge(w_lo, WHALVES)
            pe.wait_ge(r_lo, NCH * K4 + 1)
            pe.wait_ge(pads_ok, 2)
            pe.wait_ge(ct_lo, 1)
            pe.wait_ge(tr_free, T_F)
            def rows_2(t):
                s = t % 2
                pe.wait_ge(pj_free, FREE0 + J_2 + t - 1)

                def layer(ks):
                    for k in ks:
                        mm = three(ps[:, PB + 1 + s, :], [rt[h][:, k, t * P:(t + 1) * P] for h in range(2)],
                                   [wt[:, WG2, h, k, :] for h in range(2)], k == 0, k == K4 - 1)
                    return mm

                layer(range(K4 - 1))
                for p in range(K4):
                    o = ps[:, PB + 1 + s, p * P:(p + 1) * P]
                    lhs = [qt[h][:, p, t * P:(t + 1) * P] for h in range(2)]
                    pe.matmul(o, lhs[0], ctxt[0][:, p, :], start=False, stop=False, skip_group_check=True)
                    pe.matmul(o, lhs[0], ctxt[1][:, p, :], start=False, stop=False, skip_group_check=True)
                    pe.matmul(o, lhs[1], ctxt[0][:, p, :], start=False, stop=False, skip_group_check=True)
                layer([K4 - 1]).then_inc(pj_done, 1)

            def turn_2(t):
                pe.wait_ge(xf_ok, t + 1)
                pe.wait_ge(tr_free, T_F + t - 1)
                for k in range(K4):
                    mm = pe.transpose(ps[:, TB + t % 2, k * P:(k + 1) * P], qf[:, t % 2, k * P:(k + 1) * P], ident)
                mm.then_inc(tr_done, 1)

            def gate(t):
                pe.wait_ge(tr_free, T_F + t + 1)
                for k in range(K4):
                    for s in range(2):
                        mm = pe.matmul(ps[:, AB + 1, t * 2 * NE:(t + 1) * 2 * NE], xft[t % 2][s][:, k, :],
                                       wgs[:, k, :, :].rearrange("p s e -> p (s e)"), start=(k == 0 and s == 0), stop=(k == K4 - 1 and s == 1))
                mm.then_inc(gate_done, 1)

            for t in range(T):
                if t == 0:
                    pe.wait_ge(wg_lo, 1)
                rows_2(t)
                if t >= 4:
                    turn_2(t - 4)
                if t >= 6:
                    gate(t - 6)
            for t in range(T - 4, T + 2):
                if t < T:
                    turn_2(t)
                gate(t - 2)
            pe.wait_ge(g_step, 10)
            rk_o = ps[:, AB, 0:T * NE]
            pe.matmul(rk_o, csh[:, H_TRI:H_TRI + P], ohh.rearrange("p t e -> p (t e)"), start=True, stop=False)
            for back in range(1, T):
                pe.matmul(rk_o, onesh, ohp[:, (T - 1 - back) * NE:(2 * T - 1 - back) * NE], start=False, stop=(back == T - 1))
            for t in range(T):
                mm = pe.matmul(ps[:, PB + 3, 0:NE], onesh, ohh[:, t, :], start=(t == 0), stop=(t == T - 1))
            mm.then_inc(rank_done, 1)

            def expert_of(j):
                return pe.value_load(texp[0:1, bass.ds(j, 1)], min_val=0, max_val=NE - 1)

            def turn_f(j, s):
                pe.wait_ge(f_x, j + 1)
                for k in range(K4):
                    mm = pe.transpose(ps[:, TB + s, k * P:(k + 1) * P], xff[:, s, k * P:(k + 1) * P], ident)
                mm.then_inc(f_tr, 1)

            def layer1(j, s):
                e = expert_of(j)
                pe.wait_ge(f_xt, j + 1)
                for m in range(2):
                    for k in range(K4):
                        lhs = [ffw[:, bass.ds(e, 1), h, k * HID + m * P:k * HID + (m + 1) * P].rearrange("p o n -> p (o n)") for h in range(2)]
                        mm = three(ps[:, AB + s, m * P:(m + 1) * P], lhs, [xft[s][h][:, k, :] for h in range(2)], k == 0, k == K4 - 1)
                mm.then_inc(f_h, 1)

            def layer2(j, s):
                e = expert_of(j)
                pe.wait_ge(f_hl, j + 1)
                for k in range(2):
                    rhs = [ffw[:, bass.ds(e, 1), 2 + h, k * D:(k + 1) * D].rearrange("p o n -> p (o n)") for h in range(2)]
                    mm = three(ps[:, PB + s, :], [hid[s][h][:, k, :] for h in range(2)], rhs, k == 0, k == 1)
                mm.then_inc(f_y, 1)

            pe.wait_ge(texp_ok, 1)
            turn_f(0, 0)
            turn_f(1, 1)
            pe.wait_ge(w_lo, WHALVES + 2 * NE)
            layer1(0, 0)
            with pe.Fori(0, (ET - 3) // 2) as i:
                for s in range(2):
                    turn_f(2 * i + s + 2, s)
                    layer1(2 * i + s + 1, 1 - s)
                    layer2(2 * i + s, s)
            turn_f(ET - 1, 0)
            layer1(ET - 2, 1)
            layer2(ET - 3, 0)
            layer1(ET - 1, 0)
            layer2(ET - 2, 1)
            layer2(ET - 1, 0)

        @block.scalar
        def _(act):
            act.dma_start(etab, edges.rearrange("(g p) n -> p g n", p=P)[:, :, P:2 * P]).then_inc(etab_in, 16)
            act.dma_start(cst[:, :], cf).then_inc(consts_in, 16)
            act.dma_start(csh[:, :], ch).then_inc(consts_in, 16)
            act.dma_start(bias[:, :], cols).then_inc(rows_in, 16)
            act.dma_start(bc[:, :], rows.partition_broadcast(P)).then_inc(rows_in, 16)
            act.dma_start(wgf, wg.rearrange("(k p) e -> p k e", p=P)).then_inc(wg_in, 16)

            def xn_tiles(ts):
                for t in ts:
                    act.wait_ge(xnf_ok, t + 1)
                    act.activation(xn[0][:, t, :], xnf[:, t, :], ACT.Copy).then_inc(xnh_ok, 1)
                    act.wait_ge(tr_done, t + 1)
                    act.activation(xt[0][:, :, t * P:(t + 1) * P], ps[:, TB + t % 2, :].rearrange("p (k n) -> p k n", k=K4),
                                   ACT.Copy).then_inc(tr_hi, 1)

            def w_part(i):
                act.wait_ge(w_in[i % 2], 16 * (i // 2 + 1))
                if i // 2 == 4:
                    act.wait_ge(pj_done, J_Q)
                act.activation(wt[:, w_slot[i // 2], 0, 2 * (i % 2):2 * (i % 2) + 2, :],
                               stage[:, i % 2, :].rearrange("p (k n) -> p k n", k=2), ACT.Copy, scale=WS).then_inc(w_hi, 1)

            for g in range(2):
                act.wait_ge(ln_var, g + 1)
                act.activation(sd[:, 5 * g:5 * g + 5], vpe[:, 5 * g:5 * g + 5], ACT.Sqrt).then_inc(ln_sd, 1)
                xn_tiles(range(5 * g, 5 * g + 5))
                w_part(2 * g)
                w_part(2 * g + 1)
            act.wait_ge(wg_in, 16)
            act.activation(wgs[:, :, 0, :], wgf, ACT.Copy, scale=WS).then_inc(wg_hi, 1)
            act.wait_ge(rows_in, 32)
            act.activation(b1s[:, :], bias[:, B_G1:B_G1 + K4], ACT.Copy, scale=HS).then_inc(b1s_ok, 1)
            act.preload_act_table(ACT.Exp)

            def counted(q, b):
                act.wait_ge(cnt_win, 2 + 2 * q + 2)
                act.activation(at[:, :, bass.ds(2 * WN * q, 2 * WN)],
                               ps[:, AB + b, 0:2 * KEYS].rearrange("p (d a) -> p a d", a=T), ACT.Copy).then_inc(cnt_free, 1)

            def turned_e(m, b):
                t0, nt = ETB[b]
                act.wait_ge(tr_done, T_E + NCH * m + b + 1)
                act.activation(e_nat[0][:, t0:t0 + nt, m * P:(m + 1) * P],
                               ps[:, TB + (NCH * m + b) % 2, 0:nt * P].rearrange("p (t n) -> p t n", t=nt),
                               ACT.Copy, scale=KS).then_inc(tr_hi, 1)

            for m in range(K4):
                for c in range(NCH):
                    u = NCH * m + c
                    if u >= 1:
                        counted(u - 1, (u - 1) % 2)
                    if m >= 1 and c == 1:
                        turned_e(m - 1, 0)
                act.wait_ge(k_max, m + 1)
                act.activation(kf[:, m % 2, 0:N], kf[:, m % 2, 0:N], ACT.Exp, bias=kmax[:, m:m + 1],
                               accum_out=ksum[:, m:m + 1]).then_inc(k_exp, 1)
                if m >= 1:
                    turned_e(m - 1, 1)
                act.wait_ge(k_rec, m + 1)
                act.activation(kf[:, m % 2, 0:N], kf[:, m % 2, 0:N], ACT.Copy, scale=krec[:, m:m + 1]).then_inc(k_norm, 1)
                if m >= 1:
                    turned_e(m - 1, 2)

            def q_exps(t, s):
                act.wait_ge(q_sub, t + 1)
                act.activation(qf[:, s, :], qf[:, s, :], ACT.Exp).then_inc(q_exp, 1)

            def q_turned(t, s):
                act.wait_ge(tr_done, T_Q + t + 1)
                act.activation(qt[0][:, :, bass.ds(t * P, P)], ps[:, TB + s, :].rearrange("p (k n) -> p k n", k=K4),
                               ACT.Copy).then_inc(tr_hi, 1)

            counted(CQ - 1, (CQ - 1) % 2)
            turned_e(K4 - 1, 0)
            q_exps(0, 0)
            counted(CQ, CQ % 2)
            turned_e(K4 - 1, 1)
            q_exps(1, 1)
            turned_e(K4 - 1, 2)
            with act.Fori(1, T // 2) as i:
                for s in range(2):
                    q_turned(2 * i + s - 2, s)
                    counted(CQ + 2 * i + s - 1, (CQ + s - 1) % 2)
                    q_exps(2 * i + s, s)
            q_turned(T - 2, 0)
            q_turned(T - 1, 1)
            w_part(4)
            w_part(5)
            for m in range(K4):
                if m >= 1:
                    counted(CG - 3 + 2 * m, (CG - 1) % 2)
                act.wait_ge(pj_done, J_G + m + 1)
                act.activation(gt[0][:, m, :], ps[:, PB + m, :], ACT.Copy, scale=1 / KS).then_inc(pj_hi, 1)
                if m >= 1:
                    counted(CG - 2 + 2 * m, CG % 2)

            act.wait_ge(flag_ok, 1)
            general = act.value_load(flag[0:1, 0:1], min_val=0, max_val=1)
            with act.If(general > 0):
                act.dma_start(ge_i, edge_cols).then_inc(gen_in, 16)
                with act.Fori(0, WINDOWS) as w:
                    act.wait_ge(gen_mm, w * EC + EC + 1)
                    act.activation(at[:, :, bass.ds(WN * w, WN)], ps[:, AB, 0:KEYS].rearrange("p (d a) -> p a d", a=T),
                                   ACT.Copy).then_inc(gen_ev, 1)

            act.wait_ge(ct_f, 2)
            act.wait_ge(ct_zero, 2)
            for h in range(2):
                r = slice(h * DH, (h + 1) * DH)
                act.activation(ctxt[0][r, :, r], ctxf[r, :, r], ACT.Copy).then_inc(ct_hi, 1)
            w_part(6)
            w_part(7)
            with act.Fori(0, K4) as m:
                for c, (n0, n) in enumerate(CH):
                    act.wait_ge(pj_done, J_A + NCH * m + c + 1)
                    act.activation(xt[0][:, bass.ds(m, 1), n0:n0 + n].rearrange("p o n -> p (o n)"), ps[:, PB + 1 + c, 0:n],
                                   ACT.Copy, scale=HS).then_inc(pj_hi, 1)
            w_part(8)
            w_part(9)

            def expert_part(h, s, landed):
                act.wait_ge(w_in[s], 16 * (WHALVES // 2) + 16 * landed)
                act.activation(ffh[:, bass.ds(h, 1), 0, :].rearrange("p o n -> p (o n)"), stage[:, s, :], ACT.Copy, scale=WS).then_inc(w_hi, 1)

            act.wait_ge(ct_lo, 1)
            with act.Fori(0, K4 // 2) as i:
                for r in range(2):
                    m = 2 * i + r
                    for c, (n0, n) in enumerate(CH):
                        act.wait_ge(pj_done, J_1 + NCH * m + c + 1)
                        act.activation(rt[0][:, bass.ds(m, 1), n0:n0 + n].rearrange("p o n -> p (o n)"), ps[:, PB + 1 + c, 0:n],
                                       ACT.Relu, scale=1 / WS, bias=b1s[:, bass.ds(m, 1)]).then_inc(pj_hi, 1)
                        u = NCH * r + c
                        expert_part(2 * NCH * i + u, u % 2, NCH * i + u // 2 + 1)
            act.wait_ge(pj_done, J_2)
            def turned(g):
                for t in range(2 * g, 2 * g + 2):
                    act.wait_ge(tr_done, T_F + t + 1)
                    if t >= 2:
                        act.wait_ge(gate_done, t - 1)
                    act.activation(xft[t % 2][0], ps[:, TB + t % 2, :].rearrange("p (k n) -> p k n", k=K4), ACT.Copy).then_inc(tr_hi, 1)

            for g in range(T // 2):
                if g < 2:
                    for s in range(2):
                        h = NCH * K4 + 2 * g + s
                        expert_part(h, s, h // 2 + 1)
                act.wait_ge(l2_var, g + 1)
                act.activation(sd[:, 2 * g:2 * g + 2], vpe[:, 2 * g:2 * g + 2], ACT.Sqrt).then_inc(l2_sd, 1)
                if g >= 2:
                    turned(g - 2)
            turned(T // 2 - 2)
            turned(T // 2 - 1)
            act.preload_act_table(ACT.Exp)
            act.wait_ge(g_step, 5)
            act.activation(le, le, ACT.Exp).then_inc(g_exp, 1)

            def turned_f(j, s):
                act.wait_ge(f_tr, j + 1)
                act.activation(xft[s][0], ps[:, TB + s, :].rearrange("p (k n) -> p k n", k=K4), ACT.Copy).then_inc(f_hi, 1)

            def relu_f(j, s):
                e = act.value_load(texp[0:1, bass.ds(j, 1)], min_val=0, max_val=NE - 1)
                act.wait_ge(f_h, j + 1)
                for m in range(2):
                    act.activation(hid[s][0][:, m, :], ps[:, AB + s, m * P:(m + 1) * P], ACT.Relu, scale=1 / WS,
                                   bias=bias[:, bass.ds(B_F1 + 2 * e + m, 1)]).then_inc(f_hr, 1)

            act.wait_ge(texp_ok, 1)
            turned_f(0, 0)
            turned_f(1, 1)
            relu_f(0, 0)
            with act.Fori(0, (ET - 3) // 2) as i:
                for s in range(2):
                    turned_f(2 * i + s + 2, s)
                    relu_f(2 * i + s + 1, 1 - s)
            turned_f(ET - 1, 0)
            relu_f(ET - 2, 1)
            relu_f(ET - 1, 0)

        @block.vector
        def _(dve):
            dve.wait_ge(etab_in, 16)
            dve.tensor_reduce(emax, etab, AX.X, ALU.max).then_inc(ed_range, 1)
            dve.tensor_reduce(emin, etab, AX.X, ALU.min).then_inc(ed_range, 1)
            dve.wait_ge(consts_in, 32)
            dve.wait_ge(ed_range, 2)
            for g in range(2):
                dve.tensor_scalar(before[:, g, :], cst[:, C_THR:C_THR + PAIRS], emax[:, g:g + 1], None, ALU.is_gt).then_inc(ed_before, 1)

            def statistics(ts, landed, step, var, base):
                n = len(ts)
                c = slice(ts[0], ts[0] + n)
                for t in ts:
                    landed(t)
                    dve.bn_stats(stats[:, t, :], X[:, t, 0:D]).then_inc(step, 1)
                for i, t in enumerate(ts):
                    dve.wait_ge(step, base + i + 1)
                    dve.bn_aggr(mv[:, t, :], stats[:, t, :]).then_inc(step, 1)
                dve.wait_ge(step, base + 2 * n)
                dve.tensor_scalar(vpe[:, c], mv[:, c, 1], EPS, None, ALU.add).then_inc(var, 1)

            def inverse(ts, group, step, var, sdone, base):
                c = slice(ts[0], ts[0] + len(ts))
                dve.wait_ge(sdone, group + 1)
                dve.wait_ge(var, group + 1)
                dve.reciprocal(sd[:, c], sd[:, c]).then_inc(step, 1)
                dve.wait_ge(step, base + 1)
                dve.tensor_tensor(nwt[:, c], sd[:, c], sd[:, c], ALU.mult).then_inc(step, 1)
                dve.wait_ge(step, base + 2)
                dve.tensor_tensor(nwt[:, c], nwt[:, c], vpe[:, c], ALU.mult).then_inc(step, 1)
                dve.wait_ge(step, base + 3)
                dve.tensor_scalar(nwt[:, c], nwt[:, c], -0.5, 1.5, ALU.mult, ALU.add).then_inc(step, 1)
                dve.wait_ge(step, base + 4)
                dve.tensor_tensor(rstd[:, c], sd[:, c], nwt[:, c], ALU.mult).then_inc(step, 1)
                dve.wait_ge(step, base + INV_STEPS)

            def xn_tiles(ts):
                for t in ts:
                    dve.tensor_scalar(xnf[:, t, :], X[:, t, 0:D], mv[:, t, 0:1], rstd[:, t:t + 1],
                                      ALU.subtract, ALU.mult).then_inc(xnf_ok, 1)
                for t in ts:
                    dve.wait_ge(xnh_ok, t + 1)
                    dve.wait_ge(xnf_ok, t + 1)
                    dve.tensor_tensor(xn[1][:, t, :], xnf[:, t, :], xn[0][:, t, :], ALU.subtract).then_inc(xnl_ok, 1)
                    dve.wait_ge(tr_hi, t + 1)
                    dve.tensor_tensor(xt[1][:, :, t * P:(t + 1) * P], ps[:, TB + t % 2, :].rearrange("p (k n) -> p k n", k=K4),
                                      xt[0][:, :, t * P:(t + 1) * P], ALU.subtract).then_inc(tr_free, 1)

            def w_part(i):
                dve.wait_ge(w_hi, i + 1)
                dve.scalar_tensor_tensor(wt[:, w_slot[i // 2], 1, 2 * (i % 2):2 * (i % 2) + 2, :].rearrange("p k n -> p (k n)"),
                                         stage[:, i % 2, :], WS,
                                         wt[:, w_slot[i // 2], 0, 2 * (i % 2):2 * (i % 2) + 2, :].rearrange("p k n -> p (k n)"),
                                         ALU.mult, ALU.subtract).then_inc(w_lo, 1)

            statistics(LN_GROUPS[0], lambda t: dve.wait_ge(x_in[0], 16), ln_step, ln_var, 0)
            dve.wait_ge(ed_count, 1)
            dve.tensor_tensor(pidx[0:PG, :], ps[0:PG, 5, 0:GATHERS], cst[0:PG, C_K:C_K + GATHERS], ALU.add).then_inc(ed_idx, 1)
            dve.tensor_copy(vio[0], ps[:, 5, 64:64 + WINDOWS]).then_inc(pj_free, 1)
            inverse(LN_GROUPS[0], 0, ln_step, ln_var, ln_sd, 10)
            xn_tiles(range(0, 5))
            for g in range(GATHERS):
                dve.wait_ge(ed_got[g], 16)
                dve.tensor_scalar(g_a[g], got[g][:, 0:P], 7, None, ALU.logical_shift_right).then_inc(ed_int, 1)
                dve.tensor_scalar(g_b[g], got[g][:, 0:P], P - 1, None, ALU.bitwise_and).then_inc(ed_int, 1)
                dve.wait_ge(ed_int, 4 * g + 2)
                dve.scalar_tensor_tensor(g_key[g], got[g][:, P:2 * P], float(T), g_a[g], ALU.mult, ALU.add).then_inc(ed_int, 1)
                dve.tensor_copy(g_bf[g], g_b[g]).then_inc(ed_int, 1)
                dve.wait_ge(ed_int, 4 * g + 4)
                dve.tensor_scalar(g_key[g], g_key[g], cst[0:PG, C_WK + g:C_WK + g + 1], None, ALU.subtract).then_inc(ed_key, 1)
            VS = 0
            dve.wait_ge(pj_free, 1)
            for g in range(2):
                thr = cst[:, C_THR:C_THR + PAIRS:WCH]
                last, first, dist, sq = vio[1], vio[2], vio[3], vio[4]
                dve.tensor_scalar(last, thr, emax[:, g:g + 1], None, ALU.is_le).then_inc(ed_vio, 1)
                dve.tensor_scalar(first, thr, float(WN - 1), emin[:, g:g + 1], ALU.add, ALU.is_ge).then_inc(ed_vio, 1)
                dve.tensor_scalar(dist, vio[0], -1.0, cst[:, C_C + g:C_C + g + 1], ALU.mult, ALU.add).then_inc(ed_vio, 1)
                dve.wait_ge(ed_vio, VS + 3)
                dve.tensor_scalar(dist, dist, -(WCH - 1) / 2, None, ALU.add).then_inc(ed_vio, 1)
                dve.tensor_tensor(last, last, first, ALU.mult).then_inc(ed_vio, 1)
                dve.wait_ge(ed_vio, VS + 5)
                dve.tensor_tensor(sq, dist, dist, ALU.mult).then_inc(ed_vio, 1)
                dve.wait_ge(ed_vio, VS + 6)
                dve.tensor_scalar(sq, sq, (WCH / 2) ** 2, None, ALU.is_gt).then_inc(ed_vio, 1)
                dve.wait_ge(ed_vio, VS + 7)
                dve.tensor_tensor(sq, sq, last, ALU.mult).then_inc(ed_vio, 1)
                dve.wait_ge(ed_vio, VS + 8)
                dve.tensor_reduce(viosum[:, g:g + 1], sq, AX.X, ALU.max).then_inc(ed_vio, 1)
                VS += 9
                dve.wait_ge(ed_vio, VS)
            statistics(LN_GROUPS[1], lambda t: dve.wait_ge(x_in[1], 32), ln_step, ln_var, 15)
            for i in range(2):
                w_part(i)
            inverse(LN_GROUPS[1], 1, ln_step, ln_var, ln_sd, 25)
            xn_tiles(range(5, T))
            dve.wait_ge(ed_turned, 1)
            for s in range(2):
                dve.tensor_copy(keys[:, s, :, :], ps[:, 7 - s, 0:PAIRS].unsqueeze(2).to_broadcast([P, PAIRS, 2])).then_inc(pj_free, 1)
            dve.wait_ge(pj_free, FREE0)
            for s in range(2):
                dve.memset(kf[:, s, N:NPAD], 0.0).then_inc(kf_zero, 1)
                dve.memset(ps[:, AB + s, :], 0.0).then_inc(cnt_free, 1)
                dve.memset(ohb[:, s * WCH, :], 0.0).then_inc(cnt_win, 1)
            dve.memset(vioh, 0.0).then_inc(keys_ok, 1)
            dve.memset(ohp, 0.0).then_inc(oh_zero, 1)
            for i in range(2, 4):
                w_part(i)
            dve.wait_ge(keys_ok, 1)
            dve.tensor_tensor(vioh[:, 0:1], viosum[:, 0:1], viosum[:, 1:2], ALU.max).then_inc(keys_ok, 1)
            dve.wait_ge(wg_hi, 1)
            dve.scalar_tensor_tensor(wgs[:, :, 1, :], wgf, WS, wgs[:, :, 0, :], ALU.mult, ALU.subtract).then_inc(wg_lo, 1)

            def one_hots(q):
                for h in range(2):
                    dve.wait_ge(cnt_win, 2 * q + h + 1)
                    for s, o, n in ((1, ohb, P), (0, ohk, KEYS)):
                        of = [P, WCH, n // 2, 2]
                        d = dve.tensor_tensor(o[:, h * WCH:(h + 1) * WCH, :].rearrange("p k (n j) -> p k n j", j=2),
                                              csh[:, H_IOTA:H_IOTA + n].rearrange("p (n j) -> p n j", j=2).unsqueeze(1).to_broadcast(of),
                                              keys[:, s, bass.ds((2 * q + h) * WCH, WCH), :].unsqueeze(2).to_broadcast(of), ALU.is_equal)
                    d.then_inc(oh_ok, 1)

            def turned_e(m, b):
                t0, nt = ETB[b]
                dve.wait_ge(tr_hi, T_E + NCH * m + b + 1)
                dve.scalar_tensor_tensor(e_nat[1][:, t0:t0 + nt, m * P:(m + 1) * P],
                                         ps[:, TB + (NCH * m + b) % 2, 0:nt * P].rearrange("p (t n) -> p t n", t=nt), KS,
                                         e_nat[0][:, t0:t0 + nt, m * P:(m + 1) * P], ALU.mult, ALU.subtract).then_inc(tr_free, 1)

            dve.wait_ge(ed_viotot, 1)
            dve.tensor_scalar(flag[0:1, :], ps[0:1, PB, 0:1], 1.0, None, ALU.min).then_inc(flag_ok, 1)
            for m in range(K4):
                for c, (n0, n) in enumerate(CH):
                    u = NCH * m + c
                    dve.wait_ge(pj_done, u + 1)
                    dve.tensor_scalar(kf[:, m % 2, n0:n0 + n], ps[:, PB + 1 + c, 0:n], 1 / WS, bias[:, B_K + m:B_K + m + 1],
                                      ALU.mult, ALU.add).then_inc(pj_free, 1)
                    if c == NCH - 1:
                        dve.wait_ge(pj_free, FREE0 + NCH * m + NCH)
                        dve.tensor_reduce(kmax[:, m:m + 1], kf[:, m % 2, 0:N], AX.X, ALU.max, negate=True).then_inc(k_max, 1)
                    one_hots(u)
                    if c == NCH - 1:
                        dve.wait_ge(k_exp, m + 1)
                        dve.reciprocal(krec[:, m:m + 1], ksum[:, m:m + 1]).then_inc(k_rec, 1)
                    if m >= 1 and c >= 1:
                        turned_e(m - 1, c - 1)
                    if m >= 2 and c == 0:
                        turned_e(m - 2, 2)

            def q_first(t, s):
                dve.wait_ge(pj_done, J_Q + t + 1)
                dve.scalar_tensor_tensor(qf[:, s, :], ps[:, PB + 1 + s, :], 1 / WS, bc[:, R_BQ:R_BQ + D],
                                         ALU.mult, ALU.add).then_inc(pj_free, 1)
                dve.wait_ge(pj_free, FREE0 + J_Q + t + 1)
                dve.tensor_reduce(qmax[:, s, :], qf[:, s, :].rearrange("p (h n) -> p h n", h=HEADS), AX.X, ALU.max,
                                  negate=True).then_inc(q_max, 1)

            def q_second(t, s):
                dve.wait_ge(q_exp, t + 1)
                dve.tensor_reduce(qsum[:, s, :], qf[:, s, :].rearrange("p (h n) -> p h n", h=HEADS), AX.X, ALU.add).then_inc(q_sum, 1)
                dve.wait_ge(q_sum, t + 1)
                dve.reciprocal(qrec[:, s, :], qsum[:, s, :]).then_inc(q_rec, 1)

            def q_turned(t, s):
                dve.wait_ge(tr_hi, T_Q + t + 1)
                dve.tensor_tensor(qt[1][:, :, bass.ds(t * P, P)], ps[:, TB + s, :].rearrange("p (k n) -> p k n", k=K4),
                                  qt[0][:, :, bass.ds(t * P, P)], ALU.subtract).then_inc(tr_free, 1)

            dve.wait_ge(fill_out, 16)
            q_first(0, 0)
            one_hots(CQ)
            turned_e(K4 - 2, 2)
            turned_e(K4 - 1, 0)
            q_second(0, 0)
            q_first(1, 1)
            one_hots(CQ + 1)
            turned_e(K4 - 1, 1)
            q_second(1, 1)
            turned_e(K4 - 1, 2)
            with dve.Fori(1, T // 2) as i:
                for s in range(2):
                    q_turned(2 * i + s - 2, s)
                    q_first(2 * i + s, s)
                    one_hots(CQ + 2 * i + s)
                    q_second(2 * i + s, s)
            q_turned(T - 2, 0)
            q_turned(T - 1, 1)
            w_part(4)
            for m in range(K4):
                dve.wait_ge(pj_hi, m + 1)
                dve.scalar_tensor_tensor(gt[1][:, m, :], ps[:, PB + m, :], 1 / KS, gt[0][:, m, :], ALU.mult, ALU.subtract).then_inc(pj_free, 1)
                if m == 0:
                    w_part(5)
                for q in (CG - 2 + 2 * m, CG - 1 + 2 * m):
                    if m >= 1 and q < WPAIRS:
                        one_hots(q)

            dve.wait_ge(flag_ok, 1)
            general = dve.value_load(flag[0:1, 0:1], min_val=0, max_val=1)
            with dve.If(general > 0):
                dve.wait_ge(cnt_win, 2 + WINDOWS)
                dve.wait_ge(cnt_free, 2 + WPAIRS)
                dve.memset(ohb[:, 0, :], 0.0).then_inc(gen_mm, 1)
                dve.memset(ps[:, AB, :], 0.0).then_inc(gen_ev, 1)
                dve.wait_ge(gen_mm, 1)
                dve.wait_ge(gen_in, 16)
                dve.tensor_scalar(ge_t[:, 0, :], ge_i[:, 0, :], 7, None, ALU.logical_shift_right).then_inc(gen_step, 1)
                dve.tensor_scalar(ge_t[:, 1, :], ge_i[:, 0, :], P - 1, None, ALU.bitwise_and).then_inc(gen_step, 1)
                dve.wait_ge(gen_step, 2)
                dve.scalar_tensor_tensor(ge_w, ge_i[:, 1, :], float(T), ge_t[:, 0, :], ALU.mult, ALU.add).then_inc(gen_step, 1)
                dve.tensor_copy(ge_b, ge_t[:, 1, :]).then_inc(gen_step, 1)
                with dve.Fori(0, WINDOWS) as w:
                    with dve.Fori(0, EC) as c:
                        dve.wait_ge(gen_step, w + 4)
                        dve.wait_ge(gen_mm, w * EC + c + 1)
                        dve.tensor_scalar(ohb[:, 0, :], csh[:, H_IOTA:H_IOTA + P], ge_b[:, bass.ds(c, 1)], None, ALU.is_equal)
                        dve.tensor_scalar(ohk[:, 0, :], csh[:, H_IOTA:H_IOTA + KEYS], ge_w[:, bass.ds(c, 1)], None,
                                          ALU.is_equal).then_inc(gen_oh, 1)
                    dve.wait_ge(gen_oh, w * EC + EC)
                    dve.tensor_scalar(ge_w, ge_w, float(KEYS), None, ALU.subtract).then_inc(gen_step, 1)
                dve.wait_ge(gen_ev, WINDOWS + 1)

            dve.wait_ge(cnt_free, 2 + WPAIRS)
            for a in range(T):
                dve.tensor_tensor(at[:, a, a * P:(a + 1) * P], at[:, a, a * P:(a + 1) * P], ident, ALU.add).then_inc(at_ok, 1)
            dve.wait_ge(pj_done, J_C + 1)
            for h in range(2):
                r = slice(h * DH, (h + 1) * DH)
                dve.scalar_tensor_tensor(ctxf[r, :, r], ps[r, PB, :].rearrange("p (k n) -> p k n", k=K4)[:, :, r], 1 / WS,
                                         bc[r, R_BV:R_BV + D].rearrange("p (k n) -> p k n", k=K4)[:, :, r], ALU.mult, ALU.add).then_inc(ct_f, 1)
            dve.wait_ge(ct_f, 2)
            dve.memset(nwt[:, 0:1], 0.0).then_inc(pj_free, 1)
            dve.wait_ge(ct_hi, 2)
            for h in range(2):
                r = slice(h * DH, (h + 1) * DH)
                d = dve.tensor_tensor(ctxt[1][r, :, r], ctxf[r, :, r], ctxt[0][r, :, r], ALU.subtract)
            d.then_inc(ct_lo, 1)
            w_part(6)
            w_part(7)
            with dve.Fori(0, K4) as m:
                for c, (n0, n) in enumerate(CH):
                    dve.wait_ge(pj_hi, K4 + NCH * m + c + 1)
                    dve.scalar_tensor_tensor(xt[1][:, bass.ds(m, 1), n0:n0 + n].rearrange("p o n -> p (o n)"), ps[:, PB + 1 + c, 0:n], HS,
                                             xt[0][:, bass.ds(m, 1), n0:n0 + n].rearrange("p o n -> p (o n)"),
                                             ALU.mult, ALU.subtract).then_inc(pj_free, 1)
            dve.wait_ge(pj_done, J_1)
            for i in range(2):
                dve.memset(rt[i][:, :, N:NPAD], 0.0).then_inc(pads_ok, 1)
            for i in range(8, WHALVES):
                w_part(i)
            J1H = NCH * K4 + K4
            lin = qf.rearrange("p s n -> p (s n)")
            dve.wait_ge(tr_free, T_F)
            dve.memset(lin[:, 0:1], 0.0).then_inc(r_lo, 1)

            def expert_part(h, s):
                dve.wait_ge(w_hi, WHALVES + h + 1)
                dve.scalar_tensor_tensor(ffh[:, bass.ds(h, 1), 1, :].rearrange("p o n -> p (o n)"), stage[:, s, :], WS,
                                         ffh[:, bass.ds(h, 1), 0, :].rearrange("p o n -> p (o n)"), ALU.mult, ALU.subtract).then_inc(w_lo, 1)

            with dve.Fori(0, K4 // 2) as i:
                for r in range(2):
                    m = 2 * i + r
                    for c, (n0, n) in enumerate(CH):
                        hi = rt[0][:, bass.ds(m, 1), n0:n0 + n].rearrange("p o n -> p (o n)")
                        lo = rt[1][:, bass.ds(m, 1), n0:n0 + n].rearrange("p o n -> p (o n)")
                        dve.wait_ge(pj_hi, J1H + NCH * m + c + 1)
                        dve.wait_ge(r_lo, NCH * m + c + 1)
                        dve.tensor_scalar(lin[:, 0:n], ps[:, PB + 1 + c, 0:n], 1 / WS, b1s[:, bass.ds(m, 1)],
                                          ALU.mult, ALU.add).then_inc(pj_free, 1)
                        dve.wait_ge(pj_free, FREE0 + J_1 + NCH * m + c + 1)
                        dve.scalar_tensor_tensor(lo, lin[:, 0:n], 0.0, hi, ALU.max, ALU.subtract).then_inc(r_lo, 1)
                        expert_part(2 * NCH * i + NCH * r + c, (NCH * r + c) % 2)
            dve.tensor_copy(X[:, :, D + 3].bitcast(I32), cst[:, C_TOK:C_TOK + T]).then_inc(tok_ok, 1)
            dve.tensor_scalar(valid, cst[:, C_TOK:C_TOK + T], float(N), None, ALU.is_lt).then_inc(tok_ok, 1)
            def normalised(g):
                inverse(range(2 * g, 2 * g + 2), g, l2_step, l2_var, l2_sd, 4 * min(g + 2, T // 2) + INV_STEPS * g)
                for t in range(2 * g, 2 * g + 2):
                    if t >= 2:
                        dve.wait_ge(tr_done, T_F + t - 1)
                    dve.tensor_scalar(qf[:, t % 2, :], X[:, t, 0:D], mv[:, t, 0:1], rstd[:, t:t + 1], ALU.subtract, ALU.mult).then_inc(xf_ok, 1)

            def turned(g):
                for t in range(2 * g, 2 * g + 2):
                    dve.wait_ge(tr_hi, T_F + t + 1)
                    dve.tensor_tensor(xft[t % 2][1], ps[:, TB + t % 2, :].rearrange("p (k n) -> p k n", k=K4), xft[t % 2][0],
                                      ALU.subtract).then_inc(tr_free, 1)

            dve.wait_ge(xb_ok, T)
            for g in range(T // 2):
                for t in range(2 * g, 2 * g + 2):
                    dve.wait_ge(pj_done, J_2 + t + 1)
                    dve.scalar_tensor_tensor(X[:, t, 0:D], ps[:, PB + 1 + t % 2, :], HS, X[:, t, 0:D], ALU.mult, ALU.add).then_inc(pj_free, 1)
                statistics(range(2 * g, 2 * g + 2), lambda t: dve.wait_ge(pj_free, FREE0 + J_2 + t + 1), l2_step, l2_var,
                           4 * g + INV_STEPS * max(g - 1, 0))
                if g >= 1:
                    normalised(g - 1)
                if g >= 2:
                    turned(g - 2)
                if g < 2:
                    for h in range(2):
                        expert_part(NCH * K4 + 2 * g + h, h)
            normalised(T // 2 - 1)
            turned(T // 2 - 2)
            turned(T // 2 - 1)
            dve.tensor_copy(X[:, :, D + 1], rstd).then_inc(tok_ok, 1)
            dve.tensor_copy(X[:, :, D], mv[:, :, 0]).then_inc(tok_ok, 1)

            def step(n):
                dve.wait_ge(g_step, n)

            dve.wait_ge(gate_done, T)
            gp = ps[:, AB + 1, 0:2 * T * NE].rearrange("p (t s e) -> p t s e", t=T, s=2)
            bge = [P, T, NE]
            dve.tensor_scalar(rk, gp[:, :, 0, :], 1 / WS, None, ALU.mult).then_inc(g_step, 1)
            step(1)
            dve.scalar_tensor_tensor(lg, gp[:, :, 1, :], 1 / WS, rk, ALU.mult, ALU.add).then_inc(g_step, 1)
            step(2)
            dve.tensor_tensor(lg, lg, bc[:, R_BG:R_BG + NE].unsqueeze(1).to_broadcast(bge), ALU.add).then_inc(g_step, 1)
            step(3)
            dve.tensor_reduce(lmax, lg, AX.X, ALU.max).then_inc(g_step, 1)
            step(4)
            dve.tensor_tensor(le, lg, lmax.unsqueeze(2).to_broadcast(bge), ALU.subtract).then_inc(g_step, 1)
            dve.tensor_tensor(oh, lg, lmax.unsqueeze(2).to_broadcast(bge), ALU.is_equal).then_inc(g_step, 1)
            step(6)
            dve.tensor_tensor(oh, oh, cst[:, C_J:C_J + NE].unsqueeze(1).to_broadcast(bge), ALU.mult).then_inc(g_step, 1)
            step(7)
            dve.tensor_reduce(lpick, oh, AX.X, ALU.max).then_inc(g_step, 1)
            step(8)
            dve.tensor_tensor(oh, oh, lpick.unsqueeze(2).to_broadcast(bge), ALU.is_equal).then_inc(g_step, 1)
            step(9)
            dve.wait_ge(oh_zero, 1)
            dve.tensor_tensor(ohh, oh, valid.unsqueeze(2).to_broadcast(bge), ALU.mult).then_inc(g_step, 1)
            dve.wait_ge(g_exp, 1)
            dve.tensor_reduce(lsum, le, AX.X, ALU.add).then_inc(g_step, 1)
            step(11)
            dve.reciprocal(X[:, :, D + 2], lsum).then_inc(g_step, 1)
            dve.wait_ge(rank_done, 1)
            dve.tensor_scalar(ne_i, ps[:, PB + 3, 0:NE], float(P - 1), None, ALU.add).then_inc(g_step, 1)
            step(13)
            dve.tensor_scalar(ne_i, ne_i, 7, None, ALU.logical_shift_right).then_inc(g_step, 1)
            step(14)
            dve.tensor_copy(tiles, ne_i).then_inc(g_step, 1)
            step(15)
            dve.tensor_tensor(tri_p, cst[:, C_TRI:C_TRI + NE * NE].rearrange("p (a b) -> p a b", a=NE),
                              tiles.unsqueeze(1).to_broadcast([P, NE, NE]), ALU.mult).then_inc(g_step, 1)
            step(16)
            dve.tensor_reduce(base, tri_p, AX.X, ALU.add).then_inc(g_step, 1)
            step(17)
            dve.scalar_tensor_tensor(rk, base.unsqueeze(1).to_broadcast(bge), float(P),
                                     ps[:, AB, 0:T * NE].rearrange("p (t e) -> p t e", t=T), ALU.mult, ALU.add).then_inc(g_step, 1)
            step(18)
            dve.tensor_tensor(rk, rk, oh, ALU.mult).then_inc(g_step, 1)
            step(19)
            dve.tensor_reduce(lpick, rk, AX.X, ALU.add).then_inc(g_step, 1)
            step(20)
            dve.tensor_copy(slot_i, lpick).then_inc(slot_ok, 1)
            dve.tensor_tensor(ends, base, tiles, ALU.add).then_inc(g_step, 1)
            step(21)
            dve.tensor_tensor(tile_p, cst[:, C_TILE:C_TILE + ET * NE].rearrange("p (j e) -> p j e", j=ET),
                              ends.unsqueeze(1).to_broadcast([P, ET, NE]), ALU.is_ge).then_inc(g_step, 1)
            step(22)
            dve.tensor_reduce(texp_f, tile_p, AX.X, ALU.add).then_inc(g_step, 1)
            step(23)
            dve.tensor_scalar(texp, texp_f, float(NE - 1), None, ALU.min).then_inc(texp_ok, 1)

            def rows_f(j, i, s):
                dve.wait_ge(row_in[s], 16 * i + 16)
                dve.tensor_scalar(xff[:, s, :], rb[:, bass.ds(j, 1), 0:D].rearrange("p o n -> p (o n)"),
                                  rb[:, bass.ds(j, 1), D], rb[:, bass.ds(j, 1), D + 1], ALU.subtract, ALU.mult).then_inc(f_x, 1)

            def turned_f(j, s):
                dve.wait_ge(f_hi, j + 1)
                dve.tensor_tensor(xft[s][1], ps[:, TB + s, :].rearrange("p (k n) -> p k n", k=K4), xft[s][0], ALU.subtract).then_inc(f_xt, 1)

            def relu_f(j, s):
                e = dve.value_load(texp[0:1, bass.ds(j, 1)], min_val=0, max_val=NE - 1)
                dve.wait_ge(f_hr, 2 * j + 2)
                for m in range(2):
                    dve.tensor_scalar(hidf[:, s, m * P:(m + 1) * P], ps[:, AB + s, m * P:(m + 1) * P], 1 / WS,
                                      bias[:, bass.ds(B_F1 + 2 * e + m, 1)], ALU.mult, ALU.add).then_inc(f_hf, 1)
                dve.wait_ge(f_hf, 2 * j + 2)
                dve.scalar_tensor_tensor(hid[s][1].rearrange("p m n -> p (m n)"), hidf[:, s, :], 0.0,
                                         hid[s][0].rearrange("p m n -> p (m n)"), ALU.max, ALU.subtract).then_inc(f_hl, 1)

            def rows_out(j, i, s, first=False):
                e = dve.value_load(texp[0:1, bass.ds(j, 1)], min_val=0, max_val=NE - 1)
                if not first:
                    dve.wait_ge(out_done[s], 16 * i)
                dve.tensor_copy(tokc[:, s:s + 1], rb[:, bass.ds(j, 1), D + 3].bitcast(I32)).then_inc(f_tok, 1)
                dve.wait_ge(f_y, j + 1)
                dve.scalar_tensor_tensor(yf[:, s, :], ps[:, PB + s, :], 1 / WS, b2b[:, bass.ds(e * D, D)], ALU.mult, ALU.add).then_inc(f_yb, 1)
                dve.wait_ge(f_yb, j + 1)
                dve.wait_ge(f_tok, j + 1)
                dve.scalar_tensor_tensor(yf[:, s, :], yf[:, s, :], rb[:, bass.ds(j, 1), D + 2],
                                         rb[:, bass.ds(j, 1), 0:D].rearrange("p o n -> p (o n)"), ALU.mult, ALU.add).then_inc(f_out, 1)

            dve.wait_ge(texp_ok, 1)
            dve.wait_ge(b2f_in, 16)
            rows_f(0, 0, 0)
            rows_f(1, 0, 1)
            turned_f(0, 0)
            rows_f(2, 1, 0)
            turned_f(1, 1)
            relu_f(0, 0)

            def step_f(j, i, s, last=ET, first=False):
                out_i, row_i = (i - 1 + s), (i + 1 + s)
                if last > j - 1 >= 0 if isinstance(j, int) else True:
                    rows_out(j - 1, out_i, 1 - s, first)
                if not isinstance(j, int) or j + 3 < last:
                    rows_f(j + 3, row_i, 1 - s)
                if not isinstance(j, int) or j + 2 < last:
                    turned_f(j + 2, s)
                if not isinstance(j, int) or j + 1 < last:
                    relu_f(j + 1, 1 - s)

            for j in range(3):
                step_f(j, j // 2, j % 2, first=True)
            with dve.Fori(1, (ET - 5) // 2) as i:
                step_f(2 * i + 1, i, 1)
                step_f(2 * i + 2, i + 1, 0)
            for j in range(2 * ((ET - 5) // 2) + 1, ET + 1):
                step_f(j, j // 2, j % 2)


def kernel(x, src, dst, L0_gnn_W1, L0_gnn_b1, L0_gnn_W2, L0_gnn_b2, L0_mix_Wq, L0_mix_bq, L0_mix_Wk, L0_mix_bk,
           L0_mix_Wv, L0_mix_bv, L0_ffn_Wg, L0_ffn_bg, L0_ffn_W1, L0_ffn_b1, L0_ffn_W2, L0_ffn_b2):
    from concourse import bacc
    from concourse.bass_utils import run_bass_kernel_spmd

    src, dst = np.asarray(src), np.asarray(dst)
    table = np.zeros((ECP, 2, P), np.int32)
    table[:, 1, :] = PAD_DST
    flat = np.zeros((2, ECP * P), np.int32)
    flat[1] = PAD_DST
    flat[0, :EDGES], flat[1, :EDGES] = src, dst
    table = np.ascontiguousarray(flat.reshape(2, ECP, P).transpose(1, 0, 2)).reshape(ECP, 2 * P)
    columns = np.ascontiguousarray(flat[:, :ECF * P].reshape(2, ECF, P).transpose(2, 0, 1))
    cf, ch = constants()
    arrays = {
        "x": x, "edges": table, "edge_cols": columns,
        "wk": np.ascontiguousarray(np.asarray(L0_mix_Wk).T), "wq": np.ascontiguousarray(np.asarray(L0_mix_Wq).T),
        "wv": np.ascontiguousarray(np.asarray(L0_mix_Wv).T), "g1": L0_gnn_W1, "g2": L0_gnn_W2,
        "w1": np.asarray(L0_ffn_W1).reshape(NE * D, HID), "w2": np.asarray(L0_ffn_W2).reshape(NE * HID, D), "wg": L0_ffn_Wg,
        "rows": np.concatenate([np.asarray(v) for v in (L0_mix_bq, L0_mix_bv, L0_gnn_b2, L0_ffn_bg)]),
        "b2f": np.asarray(L0_ffn_b2).reshape(-1),
        "cols": np.ascontiguousarray(np.concatenate([np.asarray(L0_mix_bk), np.asarray(L0_gnn_b1),
                                                     np.asarray(L0_ffn_b1).reshape(-1)]).reshape(-1, P).T),
        "cf": cf, "ch": ch,
    }
    nc = bacc.Bacc("TRN2", target_bir_lowering=False, num_devices=1)
    aps = {}
    for name, a in arrays.items():
        arrays[name] = a = np.ascontiguousarray(a)
        aps[name] = nc.dram_tensor(name, a.shape, mybir.dt.from_np(a.dtype), kind="ExternalInput").ap()
    out = nc.dram_tensor("out", (N, D), F32, kind="ExternalOutput").ap()
    build(nc, out=out, **aps)
    r = run_bass_kernel_spmd(nc, [arrays], core_ids=[0])
    return r.results[0]["out"]
```

```python
from contextlib import ExitStack

import numpy as np

import concourse.bass as bass
from concourse import mybir

ALU = mybir.AluOpType
ACT = mybir.ActivationFunctionType
AX = mybir.AxisListType
F32 = mybir.dt.float32
F16 = mybir.dt.float16
I32 = mybir.dt.int32

P = 128
N, D = 1250, 512
T = -(-N // P)
NPAD = T * P
LAST = N - (T - 1) * P
K4 = D // P
HEADS, DH = 8, 64
CH = ((0, 420), (420, 420), (840, 410))
NCH = len(CH)

EDGES = 20000
EC = -(-EDGES // P)
ECP = 256
ECF = 160
WN = 24
KEYS = WN * T
WINDOWS = 54
WCH = 5
PAIRS = WINDOWS * WCH
GATHERS = 3
PG = PAIRS // GATHERS
ATW = WINDOWS * WN
PAD_DST = ATW
WPAIRS = WINDOWS // 2

NE, HID = 8, 256
ET = (N + NE * (P - 1)) // P
ROW = D + 3
AHEAD = 6
EMPTY = NPAD - 1

WS = 64.0
HS = 0.125
KS = 4096.0
EPS = 1e-5

C_ID, C_THR = 0, P
C_K = C_THR + PAIRS
C_WK = C_K + GATHERS
C_C = C_WK + GATHERS
C_J = C_C + 2
C_TRI = C_J + NE
C_TILE = C_TRI + NE * NE
C_TOK = C_TILE + ET * NE
C_ALL = C_TOK + T
H_IOTA, H_TRI, H_ONE = 0, KEYS, KEYS + P
H_ALL = KEYS + 2 * P
R_BQ, R_BV, R_B2, R_BG = 0, D, 2 * D, 3 * D
R_ALL = 3 * D + NE
B_K, B_G1, B_F1 = 0, K4, 2 * K4
B_ALL = 2 * K4 + 2 * NE


def constants():
    f = np.zeros((P, C_ALL), np.float32)
    p = np.arange(P)
    f[:, C_ID:C_ID + P] = np.eye(P)
    pair = np.arange(PAIRS)
    f[:, C_THR:C_THR + PAIRS] = (pair // WCH) * WN
    for g in range(GATHERS):
        q = g * PG + np.minimum(p, PG - 1)
        f[:, C_K + g] = q % WCH
        f[:, C_WK + g] = (q // WCH) * KEYS
    for g in range(2):
        f[:, C_C + g] = g * P + p
    f[:, C_J:C_J + NE] = NE - np.arange(NE)
    f[:, C_TRI:C_TRI + NE * NE] = (np.arange(NE)[None, :] < np.arange(NE)[:, None]).reshape(-1)
    f[:, C_TILE:C_TILE + ET * NE] = np.repeat(np.arange(ET), NE)
    f[:, C_TOK:C_TOK + T] = np.arange(T)[None, :] * P + p[:, None]
    h = np.zeros((P, H_ALL), np.float16)
    h[:, H_IOTA:H_IOTA + KEYS] = np.arange(KEYS)
    h[:, H_TRI:H_TRI + P] = p[:, None] < p[None, :]
    h[:, H_ONE:H_ONE + P] = 1
    return f, h


def build(nc, x, edges, edge_cols, wk, wq, wv, g1, g2, w1, w2, wg, rows, b2f, cols, cf, ch, out):
    ctx = ExitStack()
    with ctx:
        def sb(name, shape, dt=F32):
            return ctx.enter_context(nc.sbuf_tensor(name, shape, dt))

        def sem(name):
            return ctx.enter_context(nc.semaphore(name))

        token_rows = nc.dram_tensor("token_rows", (NPAD, ROW), F32, kind="Internal").ap()

        AT_W, E_W, KF_W, XT_W = ATW * T // 2, T * D, 2 * NPAD, K4 * NPAD
        one = sb("one", [P, AT_W + E_W + KF_W + XT_W])
        two = sb("two", [P, 2 * XT_W])

        def halves(region, start, words, pattern, **dims):
            w = words // 2
            return [region[:, start + i * w:start + (i + 1) * w].bitcast(F16).rearrange(pattern, **dims)
                    for i in range(2)]

        at = one[:, 0:AT_W].bitcast(F16).rearrange("p (a d) -> p a d", a=T)
        e_nat = halves(one, AT_W, E_W, "p (t n) -> p t n", t=T)
        kf = one[:, AT_W + E_W:AT_W + E_W + KF_W].rearrange("p (r n) -> p r n", r=2)
        gt = halves(one, AT_W + E_W, K4 * D, "p (k n) -> p k n", k=K4)
        xt = halves(one, AT_W + E_W + KF_W, XT_W, "p (k n) -> p k n", k=K4)
        ctxf = one[:, AT_W + E_W + K4 * D:AT_W + E_W + K4 * D + D].rearrange("p (k n) -> p k n", k=K4)
        ffw = one[:, 0:NE * 2048].bitcast(F16).rearrange("p (e s n) -> p e s n", e=NE, s=4)
        ffh = one[:, 0:NE * 2048].bitcast(F16).rearrange("p (e s n) -> p e s n", e=2 * NE, s=2)
        tail = one[:, NE * 2048:NE * 2048 + 2560]
        xft = [halves(tail, s * 512, 512, "p (k n) -> p k n", k=K4) for s in range(2)]
        hidf = tail[:, 1024:1536].rearrange("p (s n) -> p s n", s=2)
        hid = [halves(tail, 1536 + s * 256, 256, "p (m n) -> p m n", m=2) for s in range(2)]
        xn = halves(two, 0, XT_W, "p (t n) -> p t n", t=T)
        rt = halves(two, 0, XT_W, "p (k n) -> p k n", k=K4)
        xnf = two[:, XT_W:2 * XT_W].rearrange("p (t n) -> p t n", t=T)
        qt = halves(two, XT_W, XT_W, "p (k n) -> p k n", k=K4)
        rb = two[:, 0:ET * ROW].rearrange("p (t n) -> p t n", t=ET)
        xff = two[:, ET * ROW:ET * ROW + 2 * D].rearrange("p (s n) -> p s n", s=2)

        X = sb("X", [P, T, ROW])
        wt = sb("wt", [P, 4, 2, K4, D], F16)
        b2b = wt[:, 1:3].rearrange("p w s k n -> p (w s k n)").bitcast(F32)
        stage = sb("stage", [P, 2, 1024])
        ohb = sb("ohb", [P, 2 * WCH, P], F16)
        ohk = sb("ohk", [P, 2 * WCH, KEYS], F16)
        keys = sb("keys", [P, 2, PAIRS, 2], F16)
        bc = sb("bc", [P, R_ALL])
        bias = sb("bias", [P, B_ALL])
        b1s = sb("b1s", [P, K4])
        qf = sb("qf", [P, 2, D])
        QR = 4
        qs = [qf[:, s, :] for s in range(2)] + [kf[:, 0, s * D:(s + 1) * D] for s in range(2)]
        YR = 4
        yf = stage.rearrange("p a b -> p (a b)").rearrange("p (s n) -> p s n", s=YR)
        ctxt = [sb(f"ctxt{i}", [P, K4, P], F16) for i in range(2)]
        cst = sb("cst", [P, C_ALL])
        csh = sb("csh", [P, H_ALL], F16)
        ident = cst[:, C_ID:C_ID + P]
        onesh = csh[:, H_ONE:H_ONE + P]
        small = sb("small", [P, 1016])
        used = [0]

        def sm(n, dt=F32):
            a = small[:, used[0]:used[0] + n]
            used[0] += n
            assert used[0] <= 1016, used
            return a if dt == F32 else a.bitcast(dt)

        def sm2(a, b, dt=F32):
            return sm(a * b, dt).rearrange("p (a b) -> p a b", a=a)

        ps = ctx.enter_context(nc.psum_tensor("ps", [P, 8, 512], F32))
        TB, AB, PB = 0, 2, 4

        stats, mv = sm2(T, 6), sm2(T, 2)
        vpe, sd, rstd, nwt = (sm(T) for _ in range(4))
        scr = one
        etab = scr[:, 0:256].bitcast(I32).rearrange("p (g n) -> p g n", g=2)
        GW = GATHERS * P
        got = scr[0:PG, 256:256 + 2 * GW].bitcast(I32).rearrange("p (g n) -> p g n", g=GATHERS)
        g_a, g_b = (scr[0:PG, 1024 + GW * i:1024 + GW * (i + 1)].bitcast(I32).rearrange("p (g n) -> p g n", g=GATHERS) for i in range(2))
        g_key, g_bf = (scr[0:PG, 1792 + GW * i:1792 + GW * (i + 1)].rearrange("p (g n) -> p g n", g=GATHERS) for i in range(2))
        before = scr[:, 2560:2560 + PAIRS].bitcast(F16).rearrange("p (g n) -> p g n", g=2)
        emax, emin = sm(2), sm(2)
        pidx = sm(GATHERS, I32)
        viosum, vioh = sm(2), sm(1).bitcast(F16)
        flag = sm(1, I32)
        gen = qf.rearrange("p s n -> p (s n)")
        ge_i = gen[:, 0:2 * ECF].bitcast(I32).rearrange("p (s n) -> p s n", s=2)
        ge_t = gen[:, 2 * ECF:4 * ECF].bitcast(I32).rearrange("p (s n) -> p s n", s=2)
        ge_b = gen[:, 4 * ECF:5 * ECF]
        ge_w = gen[:, 5 * ECF:6 * ECF]
        kmax, ksum, krec = sm(K4), sm(K4), sm(K4)
        qmax, qsum, qrec = sm2(2, HEADS), sm2(2, HEADS), sm2(2, HEADS)
        wgf = sm2(K4, NE)
        wgs = sm(K4 * NE).bitcast(F16).rearrange("p (k s e) -> p k s e", k=K4, s=2)
        lgle = sm(2 * T * NE)
        lg, le = (lgle[:, i * T * NE:(i + 1) * T * NE].rearrange("p (t e) -> p t e", t=T) for i in range(2))
        oh, rk = sm2(T, NE), sm2(T, NE)
        vio = [rk.rearrange("p a b -> p (a b)")[:, 0:WINDOWS]]
        vio += [one[:, AT_W + E_W + K4 * D + WINDOWS * i:AT_W + E_W + K4 * D + WINDOWS * (i + 1)] for i in range(4)]
        ohp = sm((2 * T - 1) * NE // 2).bitcast(F16)
        ohh = ohp[:, (T - 1) * NE:].rearrange("p (t e) -> p t e", t=T)
        valid, lmax, lsum, lpick = sm(T), sm(T), sm(T), sm(T)
        slot_i, low_i, tile_i = sm(T, I32), sm(T, I32), sm(T, I32)
        low_h, tile_h = (sm(T).bitcast(F16).rearrange("p (t j) -> p t j", j=2) for _ in range(2))
        token_h = sm(T // 2).bitcast(F16)
        slot_low = ohk.rearrange("p a b -> p (a b)")[:, 0:T * P].rearrange("p (t n) -> p t n", t=T)
        slot_tile = ohb.rearrange("p a b -> p (a b)")[:, 0:T * ET].rearrange("p (t n) -> p t n", t=T)
        token_i = sm(ET, I32)
        ne_i, tiles, base, ends = sm(NE, I32), sm(NE), sm(NE), sm(NE)
        tri_p = rk.rearrange("p a b -> p (a b)")[:, 0:NE * NE].rearrange("p (a b) -> p a b", a=NE)
        tile_p = lgle[:, 0:ET * NE].rearrange("p (j e) -> p j e", j=ET)
        texp_f, texp = sm(ET), sm(ET, I32)
        def sems(names):
            return [sem(n) for n in names.split()]

        consts_in, etab_in, rows_in, cols_in, wg_in, b2f_in, pad_zero = sems("consts_in etab_in rows_in cols_in wg_in b2f_in pad_zero")
        x_in, w_in, row_in, out_done = sems("x_in0 x_in1 x_in2"), sems("w_in0 w_in1"), sems("row_in0 row_in1"), sems("out_done0 out_done1 out_done2 out_done3")
        w_hi, w_lo, wg_hi, wg_lo = sems("w_hi w_lo wg_hi wg_lo")
        ln_step, ln_var, ln_sd, xnf_ok, xnh_ok, xnl_ok = sems("ln_step ln_var ln_sd xnf_ok xnh_ok xnl_ok")
        tr_done, tr_hi, tr_free = sems("tr_done tr_hi tr_free")
        ed_range, ed_before, ed_count, ed_idx, ed_int, ed_key, ed_turned, ed_vio, ed_viotot = sems(
            "ed_range ed_before ed_count ed_idx ed_int ed_key ed_turned ed_vio ed_viotot")
        ed_got = sems("ed_got0 ed_got1 ed_got2")
        vio_ok, flag_ok, oh_zero = sems("vio_ok flag_ok oh_zero")
        oh_ok, cnt_win, cnt_free, at_ok = sems("oh_ok cnt_win cnt_free at_ok")
        gen_in, gen_step, gen_oh, gen_mm, gen_ev = sems("gen_in gen_step gen_oh gen_mm gen_ev")
        pj_done, pj_hi, pj_free = sems("pj_done pj_hi pj_free")
        kf_zero, k_max, k_exp, k_rec, k_norm = sems("kf_zero k_max k_exp k_rec k_norm")
        q_max, q_exp, q_rec, q_norm = sems("q_max q_exp q_rec q_norm")
        xb_ok, ct_zero, ct_f, ct_hi, ct_lo, b1s_ok, r_lo, pads_ok = sems(
            "xb_ok ct_zero ct_f ct_hi ct_lo b1s_ok r_lo pads_ok")
        l2_step, l2_var, l2_sd, xf_ok, gate_done, g_step, g_exp, rank_done = sems(
            "l2_step l2_var l2_sd xf_ok gate_done g_step g_exp rank_done")
        valid_ok, x2_out, cols_ok, cols_out, inv_ok, inv_done, token_ok, texp_ok = sems(
            "valid_ok x2_out cols_ok cols_out inv_ok inv_done token_ok texp_ok")
        f_x, f_tr, f_hi, f_xt, f_h, f_hr, f_hf, f_hl, f_y, f_yb, f_out = sems(
            "f_x f_tr f_hi f_xt f_h f_hr f_hf f_hl f_y f_yb f_out")

        J_K, J_Q = 0, NCH * K4
        J_G = J_Q + T
        J_C = J_G + K4
        J_A = J_C + 1
        J_1 = J_A + NCH * K4
        J_2 = J_1 + NCH * K4
        J_END = J_2 + T
        FREE0 = 3
        T_X, T_E = 0, T
        T_Q = T_E + NCH * K4
        T_F = T_Q + T
        ETB = ((0, 4), (4, 4), (8, 2))
        CK, CQ, CG = 0, NCH * K4, NCH * K4 + T
        assert CG + 5 == WPAIRS
        BLOCKS = [(m, c, n0, w) for m in range(K4) for c, (n0, w) in enumerate(CH)]
        WHALVES = 10
        w_dram = [w.rearrange("(k p) n -> p k n", p=P) for w in (wk, wq, wv, g1, g2)]
        w_slot = (0, 1, 2, 3, 0)
        WK, WQ, WV, WG1, WG2 = w_slot
        LN_GROUPS = (range(0, 5), range(5, T))
        INV_STEPS = 5
        XG = ((0, 2), (2, 5), (5, T - 1))

        block = ctx.enter_context(nc.Block())

        @block.sync
        def _(sp):
            for s, (a, b) in enumerate(XG):
                sp.dma_start(X[:, a:b, 0:D], x[a * P:b * P, :].rearrange("(t p) n -> p t n", p=P)).then_inc(x_in[s], 16)
            sp.wait_ge(pad_zero, 1)
            sp.dma_start(X[0:LAST, T - 1, 0:D], x[(T - 1) * P:N, :]).then_inc(x_in[2], 16)
            for i in range(WHALVES):
                if i >= 2:
                    sp.wait_ge(w_lo, i - 1)
                sp.dma_start(stage[:, i % 2, :].rearrange("p (k n) -> p k n", k=2),
                             w_dram[i // 2][:, 2 * (i % 2):2 * (i % 2) + 2, :]).then_inc(w_in[i % 2], 16)
            for first, last, at_ in ((4, 6, 0), (0, 4, 2), (6, 8, 6)):
                with sp.Fori(first, last) as e:
                    sp.wait_ge(w_lo, WHALVES - 1 + 2 * (e - first + at_))
                    sp.dma_start(stage[:, 0, :].rearrange("p (k n) -> p k n", k=K4),
                                 w1[bass.ds(e * D, D), :].rearrange("(k p) n -> p k n", p=P)).then_inc(w_in[0], 16)
                    sp.wait_ge(w_lo, WHALVES + 2 * (e - first + at_))
                    sp.dma_start(stage[:, 1, :].rearrange("p (k n) -> p k n", k=2),
                                 w2[bass.ds(e * HID, HID), :].rearrange("(k p) n -> p k n", p=P)).then_inc(w_in[1], 16)
            sp.wait_ge(pj_done, J_1)
            sp.dma_start(b2b, b2f.partition_broadcast(P)).then_inc(b2f_in, 16)
            dram_rows = token_rows.rearrange("(t p) n -> p t n", p=P)
            for t in range(0, T, 2):
                sp.wait_ge(pj_free, FREE0 + J_2 + t + 2)
                sp.dma_start(dram_rows[:, t:t + 2, 0:D], X[:, t:t + 2, 0:D]).then_inc(x2_out, 16)
            sp.wait_ge(cols_ok, 2)
            sp.wait_ge(g_step, 12)
            sp.dma_start(dram_rows[:, :, D:ROW], X[:, :, D:ROW]).then_inc(cols_out, 16)

        @block.gpsimd
        def _(pool):
            pool.memset(X[:, T - 1, :], 0.0).then_inc(pad_zero, 1)
            pool.wait_ge(ed_idx, 1)
            for g in range(GATHERS):
                pool.indirect_dma_start(out=got[:, g, :], out_offset=None, in_=edges,
                                        in_offset=bass.IndirectOffsetOnAxis(ap=pidx[0:PG, g:g + 1], axis=0),
                                        bounds_check=ECP - 1, oob_is_err=False).then_inc(ed_got[g], 16)
            for t in range(T):
                pool.wait_ge(xnh_ok, t + 1)
                pool.tensor_tensor(xn[1][:, t, :], xnf[:, t, :], xn[0][:, t, :], ALU.subtract).then_inc(xnl_ok, 1)
            for i in range(2):
                pool.memset(ctxt[i][:, :, :], 0.0).then_inc(ct_zero, 1)
            pool.wait_ge(rows_in, 16)
            pool.wait_ge(xnf_ok, T)
            for t in range(T):
                pool.tensor_tensor(X[:, t, 0:D], X[:, t, 0:D], bc[:, R_B2:R_B2 + D], ALU.add).then_inc(xb_ok, 1)

            for t in range(T):
                q = qs[t % QR].rearrange("p (h n) -> p h n", h=HEADS)
                pool.wait_ge(q_rec, t + 1)
                pool.tensor_tensor(q, q, qrec[:, t % 2, :].unsqueeze(2).to_broadcast([P, HEADS, DH]), ALU.mult).then_inc(q_norm, 1)

            def gather(j):
                if j >= 2:
                    pool.wait_ge(row_in[j % 2], 16 * (j // 2))
                pool.indirect_dma_start(out=rb[:, j, :], out_offset=None, in_=token_rows,
                                        in_offset=bass.IndirectOffsetOnAxis(ap=token_i[:, j:j + 1], axis=0),
                                        bounds_check=NPAD - 1, oob_is_err=False).then_inc(row_in[j % 2], 16)

            pool.wait_ge(x2_out, 16 * (T // 2))
            pool.wait_ge(cols_out, 16)
            pool.wait_ge(token_ok, 1)
            for j in range(AHEAD):
                gather(j)
            for j in range(ET):
                if j + AHEAD < ET:
                    gather(j + AHEAD)
                pool.wait_ge(f_out, j + 1)
                pool.indirect_dma_start(out=out, out_offset=bass.IndirectOffsetOnAxis(ap=token_i[:, j:j + 1], axis=0),
                                        in_=yf[:, j % YR, :], in_offset=None, bounds_check=N - 1, oob_is_err=False).then_inc(out_done[j % YR], 16)
            for k in range(YR):
                pool.wait_ge(out_done[k], 16 * len(range(k, ET, YR)))

        @block.tensor
        def _(pe):
            def three(o, lhs, rhs, start, stop):
                pe.matmul(o, lhs[0], rhs[0], start=start, stop=False)
                pe.matmul(o, lhs[0], rhs[1], start=False, stop=False)
                return pe.matmul(o, lhs[1], rhs[0], start=False, stop=stop)

            pe.wait_ge(consts_in, 32)
            def turn_x(t):
                pe.wait_ge(xnf_ok, t + 1)
                if t >= 4:
                    pe.wait_ge(tr_free, t - 3)
                for k in range(K4):
                    mm = pe.transpose(ps[:, TB + t % 4, k * P:(k + 1) * P], xnf[:, t, k * P:(k + 1) * P], ident)
                mm.then_inc(tr_done, 1)

            for t in range(4):
                turn_x(t)
            pe.wait_ge(ed_before, 2)
            for g in range(GATHERS):
                for h in range(2):
                    pe.matmul(ps[0:PG, 5, g:g + 1], before[:, h, g * PG:(g + 1) * PG], onesh[:, 0:1], start=(h == 0), stop=(h == 1))
            for h in range(2):
                mm = pe.matmul(ps[:, 5, 64:64 + WINDOWS], onesh, before[:, h, 0:PAIRS:WCH], start=(h == 0), stop=(h == 1))
            mm.then_inc(ed_count, 1)
            for t in range(4, 8):
                turn_x(t)
            pe.wait_ge(ed_key, GATHERS)
            for g in range(GATHERS):
                pe.transpose(ps[:, 7, g * PG:(g + 1) * PG], g_key[:, g, :], ident[0:PG, 0:PG])
            for g in range(GATHERS):
                mm = pe.transpose(ps[:, 6, g * PG:(g + 1) * PG], g_bf[:, g, :], ident[0:PG, 0:PG])
            mm.then_inc(ed_turned, 1)
            for t in range(8, T):
                turn_x(t)

            def count_pair(q, b):
                pe.wait_ge(cnt_free, q + 1)
                for h in range(2):
                    pe.wait_ge(oh_ok, 2 * q + h + 1)
                    for k in range(WCH):
                        mm = pe.matmul(ps[:, AB + b, h * KEYS:(h + 1) * KEYS], ohb[:, h * WCH + k, :], ohk[:, h * WCH + k, :],
                                       start=(k == 0), stop=(k == WCH - 1))
                    mm.then_inc(cnt_win, 1)

            pe.wait_ge(pj_free, FREE0)
            pe.wait_ge(w_lo, 2)
            pe.wait_ge(tr_free, T)
            def turn_e(m, b):
                t0, nt = ETB[b]
                pe.wait_ge(k_norm, m + 1)
                pe.wait_ge(tr_free, T_E + NCH * m + b - 1)
                for t in range(nt):
                    mm = pe.transpose(ps[:, TB + (NCH * m + b) % 2, t * P:(t + 1) * P], kf[:, m % 2, (t0 + t) * P:(t0 + t + 1) * P], ident)
                mm.then_inc(tr_done, 1)

            for m in range(K4):
                for c, (n0, n) in enumerate(CH):
                    pe.wait_ge(pj_free, FREE0 + NCH * m + c - 2)
                    for k in range(K4):
                        mm = three(ps[:, PB + 1 + c, 0:n], [wt[:, WK, s, k, m * P:(m + 1) * P] for s in range(2)],
                                   [xt[s][:, k, n0:n0 + n] for s in range(2)], k == 0, k == K4 - 1)
                    mm.then_inc(pj_done, 1)
                    u = NCH * m + c
                    if u >= 1:
                        count_pair(u - 1, (u - 1) % 2)
                    if m >= 1 and c >= 1:
                        turn_e(m - 1, c - 1)
                        if c == 2:
                            turn_e(m - 1, 2)

            def q_rows(t, s):
                pe.wait_ge(pj_free, FREE0 + J_Q + t - 1)
                for k in range(K4):
                    lhs = [xt[h][:, k, bass.ds(t * P, P)] for h in range(2)]
                    mm = three(ps[:, PB + 1 + s, :], lhs, [wt[:, WQ, h, k, :] for h in range(2)], k == 0, k == K4 - 1)
                mm.then_inc(pj_done, 1)

            def turn_q(t, s):
                pe.wait_ge(q_norm, t + 1)
                pe.wait_ge(tr_free, T_Q + t - 1)
                for k in range(K4):
                    mm = pe.transpose(ps[:, TB + s % 2, k * P:(k + 1) * P], qs[s][:, k * P:(k + 1) * P], ident)
                mm.then_inc(tr_done, 1)

            pe.wait_ge(w_lo, 4)
            q_rows(0, 0)
            count_pair(CQ - 1, (CQ - 1) % 2)
            turn_e(K4 - 1, 0)
            q_rows(1, 1)
            count_pair(CQ, CQ % 2)
            turn_e(K4 - 1, 1)
            turn_e(K4 - 1, 2)
            with pe.Fori(0, (T - 2) // QR) as i:
                for s in range(QR):
                    q_rows(QR * i + s + 2, s % 2)
                    turn_q(QR * i + s, s)
                    count_pair(CQ + QR * i + s + 1, (CQ + s + 1) % 2)

            def keys_xn(m, ts):
                for t in ts:
                    mm = three(ps[:, bass.ds(PB + m, 1), :].rearrange("p o n -> p (o n)"), [xn[s][:, t, bass.ds(m * P, P)] for s in range(2)],
                               [e_nat[s][:, t, :] for s in range(2)], t == 0, t == T - 1)
                return mm

            pe.wait_ge(xnl_ok, T)
            pe.wait_ge(tr_free, T_Q)
            pe.wait_ge(pj_free, FREE0 + J_Q + T - 1)
            keys_xn(0, range(T)).then_inc(pj_done, 1)
            turn_q(T - 2, 0)
            turn_q(T - 1, 1)
            pe.wait_ge(pj_free, FREE0 + J_G)
            with pe.Fori(1, K4) as m:
                keys_xn(m, range(T // 2))
                count_pair(CG - 3 + 2 * m, (CG - 1) % 2)
                keys_xn(m, range(T // 2, T)).then_inc(pj_done, 1)
                count_pair(CG - 2 + 2 * m, CG % 2)

            pe.wait_ge(vio_ok, 1)
            pe.wait_ge(cnt_free, 2 + WPAIRS)
            pe.matmul(ps[0:1, AB, 0:1], vioh[:, 0:1], onesh[:, 0:1], start=True, stop=True).then_inc(ed_viotot, 1)

            pe.wait_ge(w_lo, 6)
            pe.wait_ge(pj_free, FREE0 + J_C)
            for p in range(K4):
                for k in range(K4):
                    mm = three(ps[:, PB, p * P:(p + 1) * P], [gt[s][:, k, p * P:(p + 1) * P] for s in range(2)],
                               [wt[:, WV, s, k, p * P:(p + 1) * P] for s in range(2)], k == 0, k == K4 - 1)
            mm.then_inc(pj_done, 1)

            pe.wait_ge(flag_ok, 1)
            general = pe.value_load(flag[0:1, 0:1], min_val=0, max_val=1)
            with pe.If(general > 0):
                with pe.Fori(0, WINDOWS) as w:
                    pe.wait_ge(gen_ev, w + 1)

                    def count(c, start, stop):
                        pe.wait_ge(gen_oh, w * EC + c + 1)
                        pe.matmul(ps[:, AB, 0:KEYS], ohb[:, 0, :], ohk[:, 0, :], start=start, stop=stop).then_inc(gen_mm, 1)

                    count(0, True, False)
                    with pe.Fori(1, EC - 1) as c:
                        count(c, False, False)
                    count(EC - 1, False, True)

            pe.wait_ge(at_ok, T)
            with pe.Fori(0, K4) as m:
                for c, (n0, n) in enumerate(CH):
                    pe.wait_ge(pj_free, FREE0 + J_A + NCH * m + c - 1)
                    o = ps[:, PB + 1 + c, 0:n]
                    for a in range(T):
                        for s in range(2):
                            mm = pe.matmul(o, xn[s][:, a, bass.ds(m * P, P)], at[:, a, n0:n0 + n],
                                           start=(a == 0 and s == 0), stop=(a == T - 1 and s == 1))
                    mm.then_inc(pj_done, 1)

            pe.wait_ge(w_lo, 8)
            with pe.Fori(0, K4) as m:
                for c, (n0, n) in enumerate(CH):
                    pe.wait_ge(pj_free, FREE0 + J_1 + NCH * m + c - 1)
                    for k in range(K4):
                        mm = three(ps[:, PB + 1 + c, 0:n], [wt[:, WG1, s, k, bass.ds(m * P, P)] for s in range(2)],
                                   [xt[s][:, k, n0:n0 + n] for s in range(2)], k == 0, k == K4 - 1)
                    mm.then_inc(pj_done, 1)

            pe.wait_ge(w_lo, WHALVES)
            pe.wait_ge(r_lo, 2 + NCH * K4)
            pe.wait_ge(pads_ok, 2)
            pe.wait_ge(ct_lo, 1)
            pe.wait_ge(tr_free, T_F)
            def rows_2(t):
                s = t % 2
                pe.wait_ge(pj_free, FREE0 + J_2 + t - 1)

                def layer(ks):
                    for k in ks:
                        mm = three(ps[:, PB + 1 + s, :], [rt[h][:, k, t * P:(t + 1) * P] for h in range(2)],
                                   [wt[:, WG2, h, k, :] for h in range(2)], k == 0, k == K4 - 1)
                    return mm

                layer(range(K4 - 1))
                for p in range(K4):
                    o = ps[:, PB + 1 + s, p * P:(p + 1) * P]
                    lhs = [qt[h][:, p, t * P:(t + 1) * P] for h in range(2)]
                    pe.matmul(o, lhs[0], ctxt[0][:, p, :], start=False, stop=False, skip_group_check=True)
                    pe.matmul(o, lhs[0], ctxt[1][:, p, :], start=False, stop=False, skip_group_check=True)
                    pe.matmul(o, lhs[1], ctxt[0][:, p, :], start=False, stop=False, skip_group_check=True)
                layer([K4 - 1]).then_inc(pj_done, 1)

            def turn_2(t):
                pe.wait_ge(xf_ok, t + 1)
                pe.wait_ge(tr_free, T_F + t - 1)
                for k in range(K4):
                    mm = pe.transpose(ps[:, TB + t % 2, k * P:(k + 1) * P], qf[:, t % 2, k * P:(k + 1) * P], ident)
                mm.then_inc(tr_done, 1)

            def gate(t):
                pe.wait_ge(tr_free, T_F + t + 1)
                for k in range(K4):
                    for s in range(2):
                        mm = pe.matmul(ps[:, AB + 1, t * 2 * NE:(t + 1) * 2 * NE], xft[t % 2][s][:, k, :],
                                       wgs[:, k, :, :].rearrange("p s e -> p (s e)"), start=(k == 0 and s == 0), stop=(k == K4 - 1 and s == 1))
                mm.then_inc(gate_done, 1)

            pe.wait_ge(wg_lo, 1)
            for g in range(T // 2):
                for t in range(2 * g, 2 * g + 2):
                    rows_2(t)
                if g >= 1:
                    turn_2(2 * g - 2)
                    turn_2(2 * g - 1)
                if g >= 2:
                    gate(2 * g - 4)
                    gate(2 * g - 3)
            gate(T - 4)
            gate(T - 3)
            turn_2(T - 2)
            turn_2(T - 1)
            gate(T - 2)
            gate(T - 1)
            pe.wait_ge(g_step, 10)
            rk_o = ps[:, AB, 0:T * NE]
            pe.matmul(rk_o, csh[:, H_TRI:H_TRI + P], ohh.rearrange("p t e -> p (t e)"), start=True, stop=False)
            for back in range(1, T):
                pe.matmul(rk_o, onesh, ohp[:, (T - 1 - back) * NE:(2 * T - 1 - back) * NE], start=False, stop=(back == T - 1))
            for t in range(T):
                mm = pe.matmul(ps[:, PB + 3, 0:NE], onesh, ohh[:, t, :], start=(t == 0), stop=(t == T - 1))
            mm.then_inc(rank_done, 1)
            pe.wait_ge(inv_ok, 3)
            for t in range(T):
                mm = pe.matmul(ps[:, PB + 2, 0:ET], slot_low[:, t, :], slot_tile[:, t, :], start=(t == 0), stop=(t == T - 1))
            mm.then_inc(inv_done, 1)

            def turn_f(j, s):
                pe.wait_ge(f_x, j + 1)
                for k in range(K4):
                    mm = pe.transpose(ps[:, TB + s, k * P:(k + 1) * P], xff[:, s, k * P:(k + 1) * P], ident)
                mm.then_inc(f_tr, 1)

            def layer1(j, s, e):
                pe.wait_ge(f_xt, j + 1)
                for m in range(2):
                    for k in range(K4):
                        lhs = [ffw[:, bass.ds(e, 1), h, k * HID + m * P:k * HID + (m + 1) * P].rearrange("p o n -> p (o n)") for h in range(2)]
                        mm = three(ps[:, AB + s, m * P:(m + 1) * P], lhs, [xft[s][h][:, k, :] for h in range(2)], k == 0, k == K4 - 1)
                mm.then_inc(f_h, 1)

            def layer2(j, s, e):
                pe.wait_ge(f_hl, j + 1)
                for k in range(2):
                    rhs = [ffw[:, bass.ds(e, 1), 2 + h, k * D:(k + 1) * D].rearrange("p o n -> p (o n)") for h in range(2)]
                    mm = three(ps[:, PB + s, :], [hid[s][h][:, k, :] for h in range(2)], rhs, k == 0, k == 1)
                mm.then_inc(f_y, 1)

            pe.wait_ge(texp_ok, 1)
            turn_f(0, 0)
            turn_f(1, 1)
            pe.wait_ge(w_lo, WHALVES + 2 * NE)
            held = [pe.alloc_register(f"expert_{n}") for n in ("even", "odd")]

            def load_expert(j, s):
                pe.reg_load(held[s], texp[0:1, bass.ds(j, 1)])

            def expert(s):
                return pe.snap(held[s], min_val=0, max_val=NE - 1)

            load_expert(0, 0)
            layer1(0, 0, expert(0))
            with pe.Fori(0, (ET - 3) // 2) as i:
                for s in range(2):
                    turn_f(2 * i + s + 2, s)
                    load_expert(2 * i + s + 1, 1 - s)
                    layer1(2 * i + s + 1, 1 - s, expert(1 - s))
                    layer2(2 * i + s, s, expert(s))
            turn_f(ET - 1, 0)
            load_expert(ET - 2, 1)
            layer1(ET - 2, 1, expert(1))
            layer2(ET - 3, 0, expert(0))
            load_expert(ET - 1, 0)
            layer1(ET - 1, 0, expert(0))
            layer2(ET - 2, 1, expert(1))
            layer2(ET - 1, 0, expert(0))

        @block.scalar
        def _(act):
            act.dma_start(etab, edges.rearrange("(g p) n -> p g n", p=P)[:, :, P:2 * P]).then_inc(etab_in, 16)
            act.dma_start(cst[:, :], cf).then_inc(consts_in, 16)
            act.dma_start(csh[:, :], ch).then_inc(consts_in, 16)

            def xn_tiles(ts):
                for t in ts:
                    act.wait_ge(xnf_ok, t + 1)
                    act.activation(xn[0][:, t, :], xnf[:, t, :], ACT.Copy).then_inc(xnh_ok, 1)
                    act.wait_ge(tr_done, t + 1)
                    act.activation(xt[0][:, :, t * P:(t + 1) * P], ps[:, TB + t % 4, :].rearrange("p (k n) -> p k n", k=K4),
                                   ACT.Copy).then_inc(tr_hi, 1)

            def w_part(i):
                act.wait_ge(w_in[i % 2], 16 * (i // 2 + 1))
                if i // 2 == 4:
                    act.wait_ge(pj_done, J_Q)
                act.activation(wt[:, w_slot[i // 2], 0, 2 * (i % 2):2 * (i % 2) + 2, :],
                               stage[:, i % 2, :].rearrange("p (k n) -> p k n", k=2), ACT.Copy, scale=WS).then_inc(w_hi, 1)

            def root(g):
                c = slice(LN_GROUPS[g][0], LN_GROUPS[g][-1] + 1)
                act.wait_ge(ln_var, g + 1)
                act.activation(sd[:, c], vpe[:, c], ACT.Sqrt).then_inc(ln_sd, 1)

            root(0)
            xn_tiles(range(4))
            root(1)
            w_part(0)
            w_part(1)
            act.dma_start(bias[:, :], cols).then_inc(cols_in, 16)
            act.dma_start(bc[:, :], rows.partition_broadcast(P)).then_inc(rows_in, 16)
            act.dma_start(wgf, wg.rearrange("(k p) e -> p k e", p=P)).then_inc(wg_in, 16)
            xn_tiles(range(4, T))
            act.wait_ge(ed_turned, 1)
            for s in range(2):
                act.activation(keys[:, s, :, :], ps[:, 7 - s, 0:PAIRS].unsqueeze(2).to_broadcast([P, PAIRS, 2]),
                               ACT.Copy).then_inc(pj_free, 1)
            w_part(2)
            w_part(3)
            act.wait_ge(wg_in, 16)
            act.activation(wgs[:, :, 0, :], wgf, ACT.Copy, scale=WS).then_inc(wg_hi, 1)
            act.wait_ge(cols_in, 16)
            act.activation(b1s[:, :], bias[:, B_G1:B_G1 + K4], ACT.Copy, scale=HS).then_inc(b1s_ok, 1)
            act.preload_act_table(ACT.Exp)

            def counted(q, b):
                act.wait_ge(cnt_win, 2 + 2 * q + 2)
                act.activation(at[:, :, bass.ds(2 * WN * q, 2 * WN)],
                               ps[:, AB + b, 0:2 * KEYS].rearrange("p (d a) -> p a d", a=T), ACT.Copy).then_inc(cnt_free, 1)

            def turned_e(m, b):
                t0, nt = ETB[b]
                act.wait_ge(tr_done, T_E + NCH * m + b + 1)
                act.activation(e_nat[0][:, t0:t0 + nt, m * P:(m + 1) * P],
                               ps[:, TB + (NCH * m + b) % 2, 0:nt * P].rearrange("p (t n) -> p t n", t=nt),
                               ACT.Copy, scale=KS).then_inc(tr_hi, 1)

            for m in range(K4):
                for c, (n0, n) in enumerate(CH):
                    u = NCH * m + c
                    act.wait_ge(pj_done, u + 1)
                    if c == 0 and m >= 2:
                        act.wait_ge(tr_done, T_E + NCH * (m - 1))
                    act.activation(kf[:, m % 2, n0:n0 + n], ps[:, PB + 1 + c, 0:n], ACT.Identity, scale=1 / WS,
                                   bias=bias[:, B_K + m:B_K + m + 1]).then_inc(pj_free, 1)
                    if u >= 1:
                        counted(u - 1, (u - 1) % 2)
                    if m >= 1 and c == 1:
                        turned_e(m - 1, 0)
                act.wait_ge(k_max, m + 1)
                act.activation(kf[:, m % 2, 0:N], kf[:, m % 2, 0:N], ACT.Exp, bias=kmax[:, m:m + 1],
                               accum_out=ksum[:, m:m + 1]).then_inc(k_exp, 1)
                if m >= 1:
                    turned_e(m - 1, 1)
                act.wait_ge(k_rec, m + 1)
                act.activation(kf[:, m % 2, 0:N], kf[:, m % 2, 0:N], ACT.Copy, scale=krec[:, m:m + 1]).then_inc(k_norm, 1)
                if m >= 1:
                    turned_e(m - 1, 2)

            def q_exps(t, s):
                act.wait_ge(q_max, t + 1)
                for h in range(HEADS):
                    act.activation(qs[s][:, h * DH:(h + 1) * DH], qs[s][:, h * DH:(h + 1) * DH], ACT.Exp, bias=qmax[:, s % 2, h:h + 1],
                                   accum_out=qsum[:, s % 2, h:h + 1]).then_inc(q_exp, 1)

            def q_turned(t, s):
                act.wait_ge(tr_done, T_Q + t + 1)
                act.activation(qt[0][:, :, bass.ds(t * P, P)], ps[:, TB + s, :].rearrange("p (k n) -> p k n", k=K4),
                               ACT.Copy).then_inc(tr_hi, 1)

            counted(CQ - 1, (CQ - 1) % 2)
            turned_e(K4 - 1, 0)
            q_exps(0, 0)
            counted(CQ, CQ % 2)
            turned_e(K4 - 1, 1)
            q_exps(1, 1)
            turned_e(K4 - 1, 2)
            with act.Fori(0, (T - 2) // QR) as i:
                for s in range(QR):
                    q_turned(QR * i + s, s % 2)
                    counted(CQ + QR * i + s + 1, (CQ + s + 1) % 2)
                    q_exps(QR * i + s + 2, (s + 2) % QR)
            q_turned(T - 2, 0)
            q_turned(T - 1, 1)
            w_part(4)
            w_part(5)
            for m in range(K4):
                if m >= 1:
                    counted(CG - 3 + 2 * m, (CG - 1) % 2)
                act.wait_ge(pj_done, J_G + m + 1)
                act.activation(gt[0][:, m, :], ps[:, PB + m, :], ACT.Copy, scale=1 / KS).then_inc(pj_hi, 1)
                if m >= 1:
                    counted(CG - 2 + 2 * m, CG % 2)

            act.wait_ge(flag_ok, 1)
            general = act.value_load(flag[0:1, 0:1], min_val=0, max_val=1)
            with act.If(general > 0):
                act.dma_start(ge_i, edge_cols).then_inc(gen_in, 16)
                with act.Fori(0, WINDOWS) as w:
                    act.wait_ge(gen_mm, w * EC + EC + 1)
                    act.activation(at[:, :, bass.ds(WN * w, WN)], ps[:, AB, 0:KEYS].rearrange("p (d a) -> p a d", a=T),
                                   ACT.Copy).then_inc(gen_ev, 1)

            act.wait_ge(ct_f, 2)
            act.wait_ge(ct_zero, 2)
            for h in range(2):
                r = slice(h * DH, (h + 1) * DH)
                act.activation(ctxt[0][r, :, r], ctxf[r, :, r], ACT.Copy).then_inc(ct_hi, 1)
            def expert_part(h, row, s):
                act.wait_ge(w_in[s], 16 * (WHALVES // 2) + 8 * (h - s) + 16)
                act.activation(ffh[:, bass.ds(row, 1), 0, :].rearrange("p o n -> p (o n)"), stage[:, s, :], ACT.Copy, scale=WS).then_inc(w_hi, 1)

            for n, (m, c, n0, w) in enumerate(BLOCKS):
                act.wait_ge(pj_done, J_A + n + 1)
                act.activation(xt[0][:, m, n0:n0 + w], ps[:, PB + 1 + c, 0:w], ACT.Copy, scale=HS).then_inc(pj_hi, 1)
                if n < WHALVES - 6:
                    w_part(6 + n)
                elif n < WHALVES - 2:
                    h = n - (WHALVES - 6)
                    expert_part(h, h + 8, h % 2)
            act.wait_ge(pj_done, J_1)
            with act.Fori(0, K4 // 2) as i:
                for r in range(2):
                    m = 2 * i + r
                    for c, (n0, n) in enumerate(CH):
                        act.wait_ge(pj_done, J_1 + NCH * m + c + 1)
                        act.wait_ge(r_lo, NCH * m + c + 1)
                        relu = dict(scale=1 / WS, bias=b1s[:, bass.ds(m, 1)])
                        act.activation(rt[0][:, bass.ds(m, 1), n0:n0 + n].rearrange("p o n -> p (o n)"), ps[:, PB + 1 + c, 0:n],
                                       ACT.Relu, **relu).then_inc(pj_hi, 1)
                        act.activation(qf[:, (NCH * r + c) % 2, 0:n], ps[:, PB + 1 + c, 0:n], ACT.Relu, **relu).then_inc(pj_free, 1)
                        if c < 2:
                            u = 4 * i + 2 * r + c
                            expert_part(u + 4, u, c)
            act.preload_act_table(ACT.Sqrt)
            act.wait_ge(pj_done, J_2)
            def turned(g):
                for t in range(2 * g, 2 * g + 2):
                    act.wait_ge(tr_done, T_F + t + 1)
                    if t >= 2:
                        act.wait_ge(gate_done, t - 1)
                    act.activation(xft[t % 2][0], ps[:, TB + t % 2, :].rearrange("p (k n) -> p k n", k=K4), ACT.Copy).then_inc(tr_hi, 1)

            for g in range(T // 2):
                if g < 2:
                    for s in range(2):
                        expert_part(12 + 2 * g + s, 12 + 2 * g + s, s)
                if g >= 2:
                    turned(g - 2)
                act.wait_ge(l2_var, g + 1)
                act.activation(sd[:, 2 * g:2 * g + 2], vpe[:, 2 * g:2 * g + 2], ACT.Sqrt).then_inc(l2_sd, 1)
            turned(T // 2 - 2)
            turned(T // 2 - 1)
            act.preload_act_table(ACT.Exp)
            act.wait_ge(g_step, 5)
            act.activation(le, le, ACT.Exp).then_inc(g_exp, 1)

            def turned_f(j, s):
                act.wait_ge(f_tr, j + 1)
                act.activation(xft[s][0], ps[:, TB + s, :].rearrange("p (k n) -> p k n", k=K4), ACT.Copy).then_inc(f_hi, 1)

            def expert_of(j):
                return act.value_load(texp[0:1, bass.ds(j, 1)], min_val=0, max_val=NE - 1)

            def relu_f(j, s, e):
                act.wait_ge(f_h, j + 1)
                for m in range(2):
                    act.activation(hid[s][0][:, m, :], ps[:, AB + s, m * P:(m + 1) * P], ACT.Relu, scale=1 / WS,
                                   bias=bias[:, bass.ds(B_F1 + 2 * e + m, 1)]).then_inc(f_hr, 1)

            def rows_f(j, i, s):
                act.wait_ge(row_in[s], 16 * i + 16)
                act.activation(xff[:, s, :], rb[:, bass.ds(j, 1), 0:D].rearrange("p o n -> p (o n)"), ACT.Identity,
                               bias=rb[:, bass.ds(j, 1), D], scale=rb[:, bass.ds(j, 1), D + 1]).then_inc(f_x, 1)

            rows_f(0, 0, 0)
            rows_f(1, 0, 1)
            act.wait_ge(texp_ok, 1)
            turned_f(0, 0)
            rows_f(2, 1, 0)
            turned_f(1, 1)
            relu_f(0, 0, expert_of(0))
            with act.Fori(0, (ET - 3) // 2) as i:
                for s in range(2):
                    e = expert_of(2 * i + s + 1)
                    rows_f(2 * i + s + 3, i + 1 + s, 1 - s)
                    turned_f(2 * i + s + 2, s)
                    relu_f(2 * i + s + 1, 1 - s, e)
            turned_f(ET - 1, 0)
            relu_f(ET - 2, 1, expert_of(ET - 2))
            relu_f(ET - 1, 0, expert_of(ET - 1))

        @block.vector
        def _(dve):
            def statistics(ts, landed, step, var, base):
                n = len(ts)
                c = slice(ts[0], ts[0] + n)
                for t in ts:
                    landed(t)
                    dve.bn_stats(stats[:, t, :], X[:, t, 0:D]).then_inc(step, 1)
                for i, t in enumerate(ts):
                    dve.wait_ge(step, base + i + 1)
                    dve.bn_aggr(mv[:, t, :], stats[:, t, :]).then_inc(step, 1)
                dve.wait_ge(step, base + 2 * n)
                dve.tensor_scalar(vpe[:, c], mv[:, c, 1], EPS, None, ALU.add).then_inc(var, 1)

            def inverse(ts, group, step, var, sdone, base):
                c = slice(ts[0], ts[0] + len(ts))
                dve.wait_ge(sdone, group + 1)
                dve.wait_ge(var, group + 1)
                dve.reciprocal(sd[:, c], sd[:, c]).then_inc(step, 1)
                dve.wait_ge(step, base + 1)
                dve.tensor_tensor(nwt[:, c], sd[:, c], sd[:, c], ALU.mult).then_inc(step, 1)
                dve.wait_ge(step, base + 2)
                dve.tensor_tensor(nwt[:, c], nwt[:, c], vpe[:, c], ALU.mult).then_inc(step, 1)
                dve.wait_ge(step, base + 3)
                dve.tensor_scalar(nwt[:, c], nwt[:, c], -0.5, 1.5, ALU.mult, ALU.add).then_inc(step, 1)
                dve.wait_ge(step, base + 4)
                dve.tensor_tensor(rstd[:, c], sd[:, c], nwt[:, c], ALU.mult).then_inc(step, 1)
                dve.wait_ge(step, base + INV_STEPS)

            def xn_tiles(ts):
                for t in ts:
                    dve.tensor_scalar(xnf[:, t, :], X[:, t, 0:D], mv[:, t, 0:1], rstd[:, t:t + 1],
                                      ALU.subtract, ALU.mult).then_inc(xnf_ok, 1)

            def turned_x(ts):
                for t in ts:
                    dve.wait_ge(tr_hi, t + 1)
                    dve.tensor_tensor(xt[1][:, :, t * P:(t + 1) * P], ps[:, TB + t % 4, :].rearrange("p (k n) -> p k n", k=K4),
                                      xt[0][:, :, t * P:(t + 1) * P], ALU.subtract).then_inc(tr_free, 1)

            def w_part(i):
                dve.wait_ge(w_hi, i + 1)
                dve.scalar_tensor_tensor(wt[:, w_slot[i // 2], 1, 2 * (i % 2):2 * (i % 2) + 2, :].rearrange("p k n -> p (k n)"),
                                         stage[:, i % 2, :], WS,
                                         wt[:, w_slot[i // 2], 0, 2 * (i % 2):2 * (i % 2) + 2, :].rearrange("p k n -> p (k n)"),
                                         ALU.mult, ALU.subtract).then_inc(w_lo, 1)

            def landed(t):
                dve.wait_ge(x_in[0 if t < 2 else 1 if t < 5 else 2], 16 if t < 5 else 32)

            statistics(LN_GROUPS[0], landed, ln_step, ln_var, 0)
            inverse(LN_GROUPS[0], 0, ln_step, ln_var, ln_sd, 10)
            xn_tiles(LN_GROUPS[0])
            dve.wait_ge(etab_in, 16)
            dve.tensor_reduce(emax, etab, AX.X, ALU.max).then_inc(ed_range, 1)
            dve.tensor_reduce(emin, etab, AX.X, ALU.min).then_inc(ed_range, 1)
            dve.wait_ge(consts_in, 32)
            dve.wait_ge(ed_range, 2)
            for g in range(2):
                dve.tensor_scalar(before[:, g, :], cst[:, C_THR:C_THR + PAIRS], emax[:, g:g + 1], None, ALU.is_gt).then_inc(ed_before, 1)
            statistics(LN_GROUPS[1], landed, ln_step, ln_var, 15)
            dve.wait_ge(ed_count, 1)
            dve.tensor_tensor(pidx[0:PG, :], ps[0:PG, 5, 0:GATHERS], cst[0:PG, C_K:C_K + GATHERS], ALU.add).then_inc(ed_idx, 1)
            dve.tensor_copy(vio[0], ps[:, 5, 64:64 + WINDOWS]).then_inc(pj_free, 1)
            turned_x(range(2))
            inverse(LN_GROUPS[1], 1, ln_step, ln_var, ln_sd, 25)
            xn_tiles(LN_GROUPS[1])
            turned_x(range(2, 5))
            for g in range(GATHERS):
                dve.wait_ge(ed_got[g], 16)
            dve.tensor_scalar(g_a, got[:, :, 0:P], 7, None, ALU.logical_shift_right).then_inc(ed_int, 1)
            dve.tensor_scalar(g_b, got[:, :, 0:P], P - 1, None, ALU.bitwise_and).then_inc(ed_int, 1)
            dve.wait_ge(ed_int, 2)
            dve.scalar_tensor_tensor(g_key, got[:, :, P:2 * P], float(T), g_a, ALU.mult, ALU.add).then_inc(ed_int, 1)
            dve.tensor_copy(g_bf, g_b).then_inc(ed_int, 1)
            dve.wait_ge(ed_int, 4)
            for g in range(GATHERS):
                dve.tensor_scalar(g_key[:, g, :], g_key[:, g, :], cst[0:PG, C_WK + g:C_WK + g + 1], None, ALU.subtract).then_inc(ed_key, 1)
            turned_x(range(5, 8))
            w_part(0)
            w_part(1)
            turned_x(range(8, T))
            dve.wait_ge(tr_free, T)
            for s in range(2):
                dve.memset(kf[:, s, N:NPAD], 0.0).then_inc(kf_zero, 1)
                dve.memset(ps[:, AB + s, 0:1], 0.0).then_inc(cnt_free, 1)
                dve.memset(ohb[:, s * WCH, 0:2], 0.0).then_inc(cnt_win, 1)
            dve.memset(vioh, 0.0).then_inc(ed_vio, 1)
            dve.memset(ohp, 0.0).then_inc(oh_zero, 1)
            def one_hots(q):
                for h in range(2):
                    dve.wait_ge(cnt_win, 2 * q + h + 1)
                    for s, o, n in ((1, ohb, P), (0, ohk, KEYS)):
                        of = [P, WCH, n // 2, 2]
                        d = dve.tensor_tensor(o[:, h * WCH:(h + 1) * WCH, :].rearrange("p k (n j) -> p k n j", j=2),
                                              csh[:, H_IOTA:H_IOTA + n].rearrange("p (n j) -> p n j", j=2).unsqueeze(1).to_broadcast(of),
                                              keys[:, s, bass.ds((2 * q + h) * WCH, WCH), :].unsqueeze(2).to_broadcast(of), ALU.is_equal)
                    d.then_inc(oh_ok, 1)

            def turned_e(m, b):
                t0, nt = ETB[b]
                dve.wait_ge(tr_hi, T_E + NCH * m + b + 1)
                dve.scalar_tensor_tensor(e_nat[1][:, t0:t0 + nt, m * P:(m + 1) * P],
                                         ps[:, TB + (NCH * m + b) % 2, 0:nt * P].rearrange("p (t n) -> p t n", t=nt), KS,
                                         e_nat[0][:, t0:t0 + nt, m * P:(m + 1) * P], ALU.mult, ALU.subtract).then_inc(tr_free, 1)

            dve.wait_ge(pj_free, FREE0)
            for m in range(K4):
                for c in range(NCH):
                    u = NCH * m + c
                    if c == NCH - 1:
                        dve.wait_ge(pj_free, FREE0 + NCH * m + NCH)
                        dve.tensor_reduce(kmax[:, m:m + 1], kf[:, m % 2, 0:N], AX.X, ALU.max, negate=True).then_inc(k_max, 1)
                    one_hots(u)
                    if c == NCH - 1:
                        dve.wait_ge(k_exp, m + 1)
                        dve.reciprocal(krec[:, m:m + 1], ksum[:, m:m + 1]).then_inc(k_rec, 1)
                    if m >= 1 and c >= 1:
                        turned_e(m - 1, c - 1)
                    if m >= 2 and c == 0:
                        turned_e(m - 2, 2)
                    if u in (3, 4):
                        w_part(u - 1)
                    if u == 6:
                        dve.wait_ge(wg_hi, 1)
                        dve.scalar_tensor_tensor(wgs[:, :, 1, :], wgf, WS, wgs[:, :, 0, :], ALU.mult, ALU.subtract).then_inc(wg_lo, 1)

            def q_first(t, s):
                dve.wait_ge(pj_done, J_Q + t + 1)
                dve.scalar_tensor_tensor(qs[s], ps[:, PB + 1 + s % 2, :], 1 / WS, bc[:, R_BQ:R_BQ + D],
                                         ALU.mult, ALU.add).then_inc(pj_free, 1)
                dve.wait_ge(pj_free, FREE0 + J_Q + t + 1)
                dve.tensor_reduce(qmax[:, s % 2, :], qs[s].rearrange("p (h n) -> p h n", h=HEADS), AX.X, ALU.max,
                                  negate=True).then_inc(q_max, 1)

            def q_second(t, s):
                dve.wait_ge(q_exp, HEADS * t + HEADS)
                dve.reciprocal(qrec[:, s, :], qsum[:, s, :]).then_inc(q_rec, 1)

            def q_turned(t, s):
                dve.wait_ge(tr_hi, T_Q + t + 1)
                dve.tensor_tensor(qt[1][:, :, bass.ds(t * P, P)], ps[:, TB + s, :].rearrange("p (k n) -> p k n", k=K4),
                                  qt[0][:, :, bass.ds(t * P, P)], ALU.subtract).then_inc(tr_free, 1)

            dve.wait_ge(rows_in, 16)
            q_first(0, 0)
            one_hots(CQ)
            turned_e(K4 - 2, 2)
            turned_e(K4 - 1, 0)
            q_first(1, 1)
            q_second(0, 0)
            one_hots(CQ + 1)
            turned_e(K4 - 1, 1)
            turned_e(K4 - 1, 2)
            with dve.Fori(0, (T - 2) // QR) as i:
                for s in range(QR):
                    q_second(QR * i + s + 1, (s + 1) % 2)
                    q_first(QR * i + s + 2, (s + 2) % QR)
                    q_turned(QR * i + s, s % 2)
                    one_hots(CQ + QR * i + s + 2)
            q_turned(T - 2, 0)
            q_second(T - 1, 1)
            q_turned(T - 1, 1)
            VS = 1
            dve.wait_ge(tr_hi, T_Q)
            for g in range(2):
                thr = cst[:, C_THR:C_THR + PAIRS:WCH]
                last, first, dist, sq = vio[1], vio[2], vio[3], vio[4]
                dve.tensor_scalar(last, thr, emax[:, g:g + 1], None, ALU.is_le).then_inc(ed_vio, 1)
                dve.tensor_scalar(first, thr, float(WN - 1), emin[:, g:g + 1], ALU.add, ALU.is_ge).then_inc(ed_vio, 1)
                dve.tensor_scalar(dist, vio[0], -1.0, cst[:, C_C + g:C_C + g + 1], ALU.mult, ALU.add).then_inc(ed_vio, 1)
                dve.wait_ge(ed_vio, VS + 3)
                dve.tensor_scalar(dist, dist, -(WCH - 1) / 2, None, ALU.add).then_inc(ed_vio, 1)
                dve.tensor_tensor(last, last, first, ALU.mult).then_inc(ed_vio, 1)
                dve.wait_ge(ed_vio, VS + 5)
                dve.tensor_tensor(sq, dist, dist, ALU.mult).then_inc(ed_vio, 1)
                dve.wait_ge(ed_vio, VS + 6)
                dve.tensor_scalar(sq, sq, (WCH / 2) ** 2, None, ALU.is_gt).then_inc(ed_vio, 1)
                dve.wait_ge(ed_vio, VS + 7)
                dve.tensor_tensor(sq, sq, last, ALU.mult).then_inc(ed_vio, 1)
                dve.wait_ge(ed_vio, VS + 8)
                dve.tensor_reduce(viosum[:, g:g + 1], sq, AX.X, ALU.max).then_inc(ed_vio, 1)
                VS += 9
                dve.wait_ge(ed_vio, VS)
            dve.tensor_tensor(vioh[:, 0:1], viosum[:, 0:1], viosum[:, 1:2], ALU.max).then_inc(vio_ok, 1)
            w_part(4)
            for m in range(K4):
                if m >= 1:
                    one_hots(CG - 2 + 2 * m)
                dve.wait_ge(pj_hi, m + 1)
                dve.scalar_tensor_tensor(gt[1][:, m, :], ps[:, PB + m, :], 1 / KS, gt[0][:, m, :], ALU.mult, ALU.subtract).then_inc(pj_free, 1)
                if m == 0:
                    w_part(5)
                elif CG - 1 + 2 * m < WPAIRS:
                    one_hots(CG - 1 + 2 * m)
            dve.wait_ge(ed_viotot, 1)
            dve.tensor_scalar(flag[0:1, :], ps[0:1, AB, 0:1], 1.0, None, ALU.min).then_inc(flag_ok, 1)

            dve.wait_ge(flag_ok, 1)
            general = dve.value_load(flag[0:1, 0:1], min_val=0, max_val=1)
            with dve.If(general > 0):
                dve.wait_ge(cnt_win, 2 + WINDOWS)
                dve.wait_ge(cnt_free, 2 + WPAIRS)
                dve.memset(ohb[:, 0, :], 0.0).then_inc(gen_mm, 1)
                dve.memset(ps[:, AB, :], 0.0).then_inc(gen_ev, 1)
                dve.wait_ge(gen_mm, 1)
                dve.wait_ge(gen_in, 16)
                dve.tensor_scalar(ge_t[:, 0, :], ge_i[:, 0, :], 7, None, ALU.logical_shift_right).then_inc(gen_step, 1)
                dve.tensor_scalar(ge_t[:, 1, :], ge_i[:, 0, :], P - 1, None, ALU.bitwise_and).then_inc(gen_step, 1)
                dve.wait_ge(gen_step, 2)
                dve.scalar_tensor_tensor(ge_w, ge_i[:, 1, :], float(T), ge_t[:, 0, :], ALU.mult, ALU.add).then_inc(gen_step, 1)
                dve.tensor_copy(ge_b, ge_t[:, 1, :]).then_inc(gen_step, 1)
                with dve.Fori(0, WINDOWS) as w:
                    with dve.Fori(0, EC) as c:
                        dve.wait_ge(gen_step, w + 4)
                        dve.wait_ge(gen_mm, w * EC + c + 1)
                        dve.tensor_scalar(ohb[:, 0, :], csh[:, H_IOTA:H_IOTA + P], ge_b[:, bass.ds(c, 1)], None, ALU.is_equal)
                        dve.tensor_scalar(ohk[:, 0, :], csh[:, H_IOTA:H_IOTA + KEYS], ge_w[:, bass.ds(c, 1)], None,
                                          ALU.is_equal).then_inc(gen_oh, 1)
                    dve.wait_ge(gen_oh, w * EC + EC)
                    dve.tensor_scalar(ge_w, ge_w, float(KEYS), None, ALU.subtract).then_inc(gen_step, 1)
                dve.wait_ge(gen_ev, WINDOWS + 1)

            dve.wait_ge(cnt_free, 2 + WPAIRS)
            for a in range(T):
                dve.tensor_tensor(at[:, a, a * P:(a + 1) * P], at[:, a, a * P:(a + 1) * P], ident, ALU.add).then_inc(at_ok, 1)
            dve.wait_ge(pj_done, J_C + 1)
            for h in range(2):
                r = slice(h * DH, (h + 1) * DH)
                dve.scalar_tensor_tensor(ctxf[r, :, r], ps[r, PB, :].rearrange("p (k n) -> p k n", k=K4)[:, :, r], 1 / WS,
                                         bc[r, R_BV:R_BV + D].rearrange("p (k n) -> p k n", k=K4)[:, :, r], ALU.mult, ALU.add).then_inc(ct_f, 1)
            dve.wait_ge(ct_f, 2)
            dve.memset(nwt[:, 0:1], 0.0).then_inc(pj_free, 1)
            dve.wait_ge(ct_hi, 2)
            for h in range(2):
                r = slice(h * DH, (h + 1) * DH)
                d = dve.tensor_tensor(ctxt[1][r, :, r], ctxf[r, :, r], ctxt[0][r, :, r], ALU.subtract)
            d.then_inc(ct_lo, 1)
            def expert_part(h, row, s):
                dve.wait_ge(w_hi, WHALVES + h + 1)
                dve.scalar_tensor_tensor(ffh[:, bass.ds(row, 1), 1, :].rearrange("p o n -> p (o n)"), stage[:, s, :], WS,
                                         ffh[:, bass.ds(row, 1), 0, :].rearrange("p o n -> p (o n)"), ALU.mult, ALU.subtract).then_inc(w_lo, 1)

            for n, (m, c, n0, w) in enumerate(BLOCKS):
                dve.wait_ge(pj_hi, K4 + n + 1)
                dve.scalar_tensor_tensor(xt[1][:, m, n0:n0 + w], ps[:, PB + 1 + c, 0:w], HS, xt[0][:, m, n0:n0 + w],
                                         ALU.mult, ALU.subtract).then_inc(pj_free, 1)
                if n < WHALVES - 6:
                    w_part(6 + n)
                elif n < WHALVES - 2:
                    h = n - (WHALVES - 6)
                    expert_part(h, h + 8, h % 2)
            dve.wait_ge(pj_done, J_1)
            for i in range(2):
                dve.memset(rt[i][:, :, N:NPAD], 0.0).then_inc(pads_ok, 1)
            dve.wait_ge(tr_free, T_F)
            for b in range(2):
                dve.memset(qf[:, b, 0:1], 0.0).then_inc(r_lo, 1)
            with dve.Fori(0, K4 // 2) as i:
                for r in range(2):
                    m = 2 * i + r
                    for c, (n0, n) in enumerate(CH):
                        hi = rt[0][:, bass.ds(m, 1), n0:n0 + n].rearrange("p o n -> p (o n)")
                        lo = rt[1][:, bass.ds(m, 1), n0:n0 + n].rearrange("p o n -> p (o n)")
                        dve.wait_ge(pj_free, FREE0 + J_1 + NCH * m + c + 1)
                        dve.tensor_tensor(lo, qf[:, (NCH * r + c) % 2, 0:n], hi, ALU.subtract).then_inc(r_lo, 1)
                        if c < 2:
                            u = 4 * i + 2 * r + c
                            expert_part(u + 4, u, c)
            dve.tensor_scalar(valid, cst[:, C_TOK:C_TOK + T], float(N), None, ALU.is_lt).then_inc(valid_ok, 1)
            dve.wait_ge(valid_ok, 1)
            dve.scalar_tensor_tensor(token_h, cst[:, C_TOK:C_TOK + T], float(EMPTY), valid, ALU.subtract, ALU.mult).then_inc(valid_ok, 1)

            def normalised(g):
                inverse(range(2 * g, 2 * g + 2), g, l2_step, l2_var, l2_sd, 4 * (g + 1) + INV_STEPS * g)
                for t in range(2 * g, 2 * g + 2):
                    if t >= 2:
                        dve.wait_ge(tr_done, T_F + t - 1)
                    dve.tensor_scalar(qf[:, t % 2, :], X[:, t, 0:D], mv[:, t, 0:1], rstd[:, t:t + 1], ALU.subtract, ALU.mult).then_inc(xf_ok, 1)

            def turned(g):
                for t in range(2 * g, 2 * g + 2):
                    dve.wait_ge(tr_hi, T_F + t + 1)
                    dve.tensor_tensor(xft[t % 2][1], ps[:, TB + t % 2, :].rearrange("p (k n) -> p k n", k=K4), xft[t % 2][0],
                                      ALU.subtract).then_inc(tr_free, 1)

            dve.wait_ge(xb_ok, T)
            def rows_2(t):
                dve.wait_ge(pj_done, J_2 + t + 1)
                dve.scalar_tensor_tensor(X[:, t, 0:D], ps[:, PB + 1 + t % 2, :], HS, X[:, t, 0:D], ALU.mult, ALU.add).then_inc(pj_free, 1)

            for g in range(T // 2):
                if g < 2:
                    for s in range(2):
                        expert_part(12 + 2 * g + s, 12 + 2 * g + s, s)
                rows_2(2 * g)
                if g >= 2:
                    turned(g - 2)
                if g >= 1:
                    normalised(g - 1)
                rows_2(2 * g + 1)
                statistics(range(2 * g, 2 * g + 2), lambda t: dve.wait_ge(pj_free, FREE0 + J_2 + t + 1), l2_step, l2_var,
                           (4 + INV_STEPS) * g)
            turned(T // 2 - 2)
            normalised(T // 2 - 1)
            turned(T // 2 - 1)
            dve.tensor_copy(X[:, :, D + 1], rstd).then_inc(cols_ok, 1)
            dve.scalar_tensor_tensor(X[:, :, D], mv[:, :, 0], -1.0, rstd, ALU.mult, ALU.mult).then_inc(cols_ok, 1)

            def step(n):
                dve.wait_ge(g_step, n)

            dve.wait_ge(gate_done, T)
            gp = ps[:, AB + 1, 0:2 * T * NE].rearrange("p (t s e) -> p t s e", t=T, s=2)
            bge = [P, T, NE]
            dve.tensor_scalar(rk, gp[:, :, 0, :], 1 / WS, None, ALU.mult).then_inc(g_step, 1)
            step(1)
            dve.scalar_tensor_tensor(lg, gp[:, :, 1, :], 1 / WS, rk, ALU.mult, ALU.add).then_inc(g_step, 1)
            step(2)
            dve.tensor_tensor(lg, lg, bc[:, R_BG:R_BG + NE].unsqueeze(1).to_broadcast(bge), ALU.add).then_inc(g_step, 1)
            step(3)
            dve.tensor_reduce(lmax, lg, AX.X, ALU.max).then_inc(g_step, 1)
            step(4)
            dve.tensor_tensor(le, lg, lmax.unsqueeze(2).to_broadcast(bge), ALU.subtract).then_inc(g_step, 1)
            dve.tensor_tensor(oh, lg, lmax.unsqueeze(2).to_broadcast(bge), ALU.is_equal).then_inc(g_step, 1)
            step(6)
            dve.tensor_tensor(oh, oh, cst[:, C_J:C_J + NE].unsqueeze(1).to_broadcast(bge), ALU.mult).then_inc(g_step, 1)
            step(7)
            dve.tensor_reduce(lpick, oh, AX.X, ALU.max).then_inc(g_step, 1)
            step(8)
            dve.tensor_tensor(oh, oh, lpick.unsqueeze(2).to_broadcast(bge), ALU.is_equal).then_inc(g_step, 1)
            step(9)
            dve.wait_ge(oh_zero, 1)
            dve.tensor_tensor(ohh, oh, valid.unsqueeze(2).to_broadcast(bge), ALU.mult).then_inc(g_step, 1)
            dve.wait_ge(g_exp, 1)
            dve.tensor_reduce(lsum, le, AX.X, ALU.add).then_inc(g_step, 1)
            step(11)
            dve.reciprocal(X[:, :, D + 2], lsum).then_inc(g_step, 1)
            dve.wait_ge(rank_done, 1)
            dve.tensor_scalar(ne_i, ps[:, PB + 3, 0:NE], float(P - 1), None, ALU.add).then_inc(g_step, 1)
            step(13)
            dve.tensor_scalar(ne_i, ne_i, 7, None, ALU.logical_shift_right).then_inc(g_step, 1)
            step(14)
            dve.tensor_copy(tiles, ne_i).then_inc(g_step, 1)
            step(15)
            dve.tensor_tensor(tri_p, cst[:, C_TRI:C_TRI + NE * NE].rearrange("p (a b) -> p a b", a=NE),
                              tiles.unsqueeze(1).to_broadcast([P, NE, NE]), ALU.mult).then_inc(g_step, 1)
            step(16)
            dve.tensor_reduce(base, tri_p, AX.X, ALU.add).then_inc(g_step, 1)
            step(17)
            dve.scalar_tensor_tensor(rk, base.unsqueeze(1).to_broadcast(bge), float(P),
                                     ps[:, AB, 0:T * NE].rearrange("p (t e) -> p t e", t=T), ALU.mult, ALU.add).then_inc(g_step, 1)
            step(18)
            dve.tensor_tensor(rk, rk, oh, ALU.mult).then_inc(g_step, 1)
            step(19)
            dve.tensor_reduce(lpick, rk, AX.X, ALU.add).then_inc(g_step, 1)
            step(20)
            dve.tensor_copy(slot_i, lpick).then_inc(g_step, 1)
            step(21)
            dve.tensor_scalar(tile_i, slot_i, 7, None, ALU.logical_shift_right).then_inc(g_step, 1)
            dve.tensor_scalar(low_i, slot_i, P - 1, None, ALU.bitwise_and).then_inc(g_step, 1)
            step(23)
            dve.tensor_copy(low_h, low_i.unsqueeze(2).to_broadcast([P, T, 2])).then_inc(g_step, 1)
            dve.tensor_copy(tile_h, tile_i.unsqueeze(2).to_broadcast([P, T, 2])).then_inc(g_step, 1)
            step(25)
            iota = csh[:, H_IOTA:H_IOTA + P]
            dve.tensor_tensor(slot_low.rearrange("p t (n j) -> p t n j", j=2),
                              iota.rearrange("p (n j) -> p n j", j=2).unsqueeze(1).to_broadcast([P, T, P // 2, 2]),
                              low_h.unsqueeze(2).to_broadcast([P, T, P // 2, 2]), ALU.is_equal).then_inc(inv_ok, 1)
            dve.tensor_tensor(slot_tile, iota[:, 0:ET].unsqueeze(1).to_broadcast([P, T, ET]),
                              tile_h[:, :, 0:1].to_broadcast([P, T, ET]), ALU.is_equal).then_inc(inv_ok, 1)
            dve.wait_ge(inv_ok, 2)
            dve.tensor_tensor(slot_tile, slot_tile, token_h.unsqueeze(2).to_broadcast([P, T, ET]), ALU.mult).then_inc(inv_ok, 1)
            dve.wait_ge(inv_done, 1)
            dve.tensor_scalar(token_i, ps[:, PB + 2, 0:ET], float(EMPTY), None, ALU.add).then_inc(token_ok, 1)
            dve.tensor_tensor(ends, base, tiles, ALU.add).then_inc(g_step, 1)
            step(26)
            dve.tensor_tensor(tile_p, cst[:, C_TILE:C_TILE + ET * NE].rearrange("p (j e) -> p j e", j=ET),
                              ends.unsqueeze(1).to_broadcast([P, ET, NE]), ALU.is_ge).then_inc(g_step, 1)
            step(27)
            dve.tensor_reduce(texp_f, tile_p, AX.X, ALU.add).then_inc(g_step, 1)
            step(28)
            dve.tensor_scalar(texp, texp_f, float(NE - 1), None, ALU.min).then_inc(texp_ok, 1)

            def turned_f(j, s):
                dve.wait_ge(f_hi, j + 1)
                dve.tensor_tensor(xft[s][1], ps[:, TB + s, :].rearrange("p (k n) -> p k n", k=K4), xft[s][0], ALU.subtract).then_inc(f_xt, 1)

            held = [dve.alloc_register(f"expert_of_tile_{k}") for k in range(YR)]

            def expert(k):
                return dve.snap(held[k], min_val=0, max_val=NE - 1)

            def relu_f(j, s, k):
                e = expert(k)
                dve.wait_ge(f_hr, 2 * j + 2)
                for m in range(2):
                    dve.tensor_scalar(hidf[:, s, m * P:(m + 1) * P], ps[:, AB + s, m * P:(m + 1) * P], 1 / WS,
                                      bias[:, bass.ds(B_F1 + 2 * e + m, 1)], ALU.mult, ALU.add).then_inc(f_hf, 1)
                dve.wait_ge(f_hf, 2 * j + 2)
                dve.scalar_tensor_tensor(hid[s][1].rearrange("p m n -> p (m n)"), hidf[:, s, :], 0.0,
                                         hid[s][0].rearrange("p m n -> p (m n)"), ALU.max, ALU.subtract).then_inc(f_hl, 1)

            def step_f(j, k, i=None):
                static = isinstance(j, int)
                out_, turn_, relu_ = (not static or 1 <= j, not static or j + 2 < ET, not static or 0 <= j + 1 < ET)
                y = yf[:, k, :]
                if relu_:
                    dve.reg_load(held[(k + 2) % YR], texp[0:1, bass.ds(j + 1, 1)])
                if out_:
                    e = expert(k)
                    if i is not None:
                        dve.wait_ge(out_done[k], 16 * i)
                    dve.wait_ge(f_y, j)
                    dve.scalar_tensor_tensor(y, ps[:, PB + k % 2, :], 1 / WS, b2b[:, bass.ds(e * D, D)], ALU.mult, ALU.add).then_inc(f_yb, 1)
                if turn_:
                    turned_f(j + 2, (k + 1) % 2)
                if out_:
                    dve.wait_ge(f_yb, j)
                    dve.scalar_tensor_tensor(y, y, rb[:, bass.ds(j - 1, 1), D + 2],
                                             rb[:, bass.ds(j - 1, 1), 0:D].rearrange("p o n -> p (o n)"), ALU.mult, ALU.add).then_inc(f_out, 1)
                if relu_:
                    relu_f(j + 1, k % 2, (k + 2) % YR)

            dve.wait_ge(texp_ok, 1)
            dve.wait_ge(b2f_in, 16)
            dve.wait_ge(w_lo, WHALVES + 2 * NE)
            loops = (ET - 2) // YR
            for j in range(-2, YR + 1):
                step_f(j, (j - 1) % YR)
            with dve.Fori(1, loops) as i:
                for k in range(YR):
                    step_f(YR * i + k + 1, k, i)
            for j in range(YR * loops + 1, ET + 1):
                step_f(j, (j - 1) % YR, (j - 1) // YR)


def kernel(x, src, dst, L0_gnn_W1, L0_gnn_b1, L0_gnn_W2, L0_gnn_b2, L0_mix_Wq, L0_mix_bq, L0_mix_Wk, L0_mix_bk,
           L0_mix_Wv, L0_mix_bv, L0_ffn_Wg, L0_ffn_bg, L0_ffn_W1, L0_ffn_b1, L0_ffn_W2, L0_ffn_b2):
    from concourse import bacc
    from concourse.bass_utils import run_bass_kernel_spmd

    src, dst = np.asarray(src), np.asarray(dst)
    flat = np.zeros((2, ECP * P), np.int32)
    flat[1] = PAD_DST
    flat[0, :EDGES], flat[1, :EDGES] = src, dst
    table = np.ascontiguousarray(flat.reshape(2, ECP, P).transpose(1, 0, 2)).reshape(ECP, 2 * P)
    columns = np.ascontiguousarray(flat[:, :ECF * P].reshape(2, ECF, P).transpose(2, 0, 1))
    cf, ch = constants()
    arrays = {
        "x": x, "edges": table, "edge_cols": columns,
        "wk": np.ascontiguousarray(np.asarray(L0_mix_Wk).T), "wq": np.ascontiguousarray(np.asarray(L0_mix_Wq).T),
        "wv": np.ascontiguousarray(np.asarray(L0_mix_Wv).T), "g1": L0_gnn_W1, "g2": L0_gnn_W2,
        "w1": np.asarray(L0_ffn_W1).reshape(NE * D, HID), "w2": np.asarray(L0_ffn_W2).reshape(NE * HID, D), "wg": L0_ffn_Wg,
        "rows": np.concatenate([np.asarray(v) for v in (L0_mix_bq, L0_mix_bv, L0_gnn_b2, L0_ffn_bg)]),
        "b2f": np.asarray(L0_ffn_b2).reshape(-1),
        "cols": np.ascontiguousarray(np.concatenate([np.asarray(L0_mix_bk), np.asarray(L0_gnn_b1),
                                                     np.asarray(L0_ffn_b1).reshape(-1)]).reshape(-1, P).T),
        "cf": cf, "ch": ch,
    }
    nc = bacc.Bacc("TRN2", target_bir_lowering=False, num_devices=1)
    aps = {}
    for name, a in arrays.items():
        arrays[name] = a = np.ascontiguousarray(a)
        aps[name] = nc.dram_tensor(name, a.shape, mybir.dt.from_np(a.dtype), kind="ExternalInput").ap()
    out = nc.dram_tensor("out", (N, D), F32, kind="ExternalOutput").ap()
    build(nc, out=out, **aps)
    r = run_bass_kernel_spmd(nc, [arrays], core_ids=[0])
    return r.results[0]["out"]
```
